# Optimizing a Trainium2 kernel written in Bass

```python
import numpy as np
import jax
import jax.numpy as jnp

def _softmax(x, axis=-1):
    return jax.nn.softmax(x, axis=axis)

def _gelu(x):
    return jax.nn.gelu(x, approximate=True)

def _silu(x):
    return jax.nn.silu(x)

def _sigmoid(x):
    return jax.nn.sigmoid(x)

def _layernorm(x, axis=-1, eps=1e-05):
    m = jnp.mean(x, axis=axis, keepdims=True)
    v = jnp.var(x, axis=axis, keepdims=True)
    return (x - m) / jnp.sqrt(v + eps)

def _scatter_add(tgt, idx, src, axis=0):
    return tgt.at[idx].add(src)

def _segment_sum(src, seg, n):
    return jax.ops.segment_sum(src, seg, n)
kernel_name = 'mk_prb_d4_jaxref_r8_e42a52'

def setup_inputs(seed: int=0):
    np.random.seed(seed)
    _w = jnp.asarray

    def _L0_attn_setup():
        import jax, jax.numpy as jnp
        import numpy as np
        B_SZ, T, D, N = (4, 256, 256, 64)

        def _reference_tuple_inner(x, A, B, C_w, C_b, D_w, D_b, log_delta):
            A_diag = jnp.exp(-jax.nn.softplus(log_delta))
            x_proj = (x @ C_w.T + C_b) * jax.nn.sigmoid(x @ D_w.T + D_b)
            xp_t = jnp.transpose(x_proj, (1, 0, 2))

            def step(g, xt):
                g = g * A_diag + xt
                return (g, g)
            g_last, gs = jax.lax.scan(step, jnp.zeros((x.shape[0], x.shape[2]), x.dtype), xp_t)
            gs = jnp.transpose(gs, (1, 0, 2))
            AB = jnp.sum(A * B, axis=-1)
            output = gs * AB
            h = g_last[:, :, None] * B[None, :, :]
            return (output, h)
        key = jax.random.key(seed)
        ks = jax.random.split(key, 8)
        s = 1.0 / np.sqrt(D)
        return {'x': jax.random.normal(ks[0], (B_SZ, T, D), dtype=jnp.float32), 'A': jax.random.normal(ks[1], (D, N), dtype=jnp.float32), 'B': jax.random.normal(ks[2], (D, N), dtype=jnp.float32), 'C_w': jax.random.uniform(ks[3], (D, D), jnp.float32, -s, s), 'C_b': jax.random.uniform(ks[4], (D,), jnp.float32, -s, s), 'D_w': jax.random.uniform(ks[5], (D, D), jnp.float32, -s, s), 'D_b': jax.random.uniform(ks[6], (D,), jnp.float32, -s, s), 'log_delta': jnp.zeros((D,), dtype=jnp.float32)}
    _L0_attn_in = _L0_attn_setup()

    def _L0_ffn_setup():
        import jax, jax.numpy as jnp
        import numpy as np
        EPS = 1e-06
        K_STEPS = 4
        USE_GATING = True

        def layer_norm(x, gamma, beta):
            mu = jnp.mean(x, axis=-1, keepdims=True)
            var = jnp.mean(jnp.square(x - mu), axis=-1, keepdims=True)
            return (x - mu) * jax.lax.rsqrt(var + EPS) * gamma + beta
        key = jax.random.key(seed)
        B, L, D, H = (4, 512, 256, 1024)
        ks = jax.random.split(key, 16)
        s = 0.02
        return {'x': jax.random.normal(ks[0], (B, L, D), dtype=jnp.float32), 'in_gamma': jnp.ones((D,), jnp.float32), 'in_beta': jnp.zeros((D,), jnp.float32), 'agg_w': jax.random.normal(ks[1], (D, D), jnp.float32) * s, 'agg_b': jnp.zeros((D,), jnp.float32), 'pn_gamma': jnp.ones((D,), jnp.float32), 'pn_beta': jnp.zeros((D,), jnp.float32), 'd1_w': jax.random.normal(ks[2], (D, H), jnp.float32) * s, 'd1_b': jnp.zeros((H,), jnp.float32), 'd2_w': jax.random.normal(ks[3], (H, D), jnp.float32) * s, 'd2_b': jnp.zeros((D,), jnp.float32), 'bc_w': jax.random.normal(ks[4], (D, D), jnp.float32) * s, 'bc_b': jnp.zeros((D,), jnp.float32), 'gate_w': jax.random.normal(ks[5], (D, D), jnp.float32) * s, 'gate_b': jnp.zeros((D,), jnp.float32), 'out_gamma': jnp.ones((D,), jnp.float32), 'out_beta': jnp.zeros((D,), jnp.float32)}
    _L0_ffn_in = _L0_ffn_setup()

    def _L1_attn_setup():
        import jax, jax.numpy as jnp
        import numpy as np
        D_MODEL = 256
        NUM_HEADS = 16
        DILATION = 2
        SEG = 64
        HEAD_DIM = D_MODEL // NUM_HEADS

        def _dilated_attention(x):
            B, N, D = x.shape
            w, r, H, hd = (SEG, DILATION, NUM_HEADS, HEAD_DIM)
            pad = -N % w
            x = jnp.pad(x, ((0, 0), (0, pad), (0, 0)))
            Np = N + pad
            nseg = Np // w
            s = w // r
            xs = x.reshape(B, nseg, w, H, hd).transpose(0, 1, 3, 2, 4)
            offsets = jnp.arange(H) % r
            idx = offsets[:, None] + jnp.arange(s)[None, :] * r
            g = jnp.take_along_axis(xs, idx[None, None, :, :, None], axis=3)
            scale = jnp.asarray(hd, x.dtype) ** (-0.5)
            scores = jnp.einsum('bnhqd,bnhkd->bnhqk', g, g) * scale
            attn = jax.nn.softmax(scores, axis=-1)
            out = jnp.einsum('bnhqk,bnhkd->bnhqd', attn, g)
            out_full = jnp.zeros((B, nseg, H, w, hd), dtype=x.dtype)
            out_full = out_full.at[:, :, jnp.arange(H)[:, None], idx, :].set(out)
            out_full = out_full.transpose(0, 1, 3, 2, 4).reshape(B, Np, D)
            return out_full[:, :N, :]
        key = jax.random.key(seed)
        x = jax.random.normal(key, (4, 1024, D_MODEL), dtype=jnp.float32)
        return {'x': x}
    _L1_attn_in = _L1_attn_setup()

    def _L1_ffn_setup():
        import jax, jax.numpy as jnp
        import numpy as np
        SWIGLU_ALPHA = 1.702
        SWIGLU_LIMIT = 7.0
        B, S, H, E, K, I = (2, 256, 256, 32, 4, 128)
        key = jax.random.key(seed)
        ks = jax.random.split(key, 8)
        return {'hidden_states': jax.random.normal(ks[0], (B, S, H), jnp.float32), 'gate_w': jax.random.normal(ks[1], (E, H), jnp.float32) * 0.02, 'gate_b': jnp.zeros((E,), jnp.float32), 'w_gate': jax.random.normal(ks[2], (E, H, I), jnp.float32) * 0.02, 'b_gate': jnp.zeros((E, I), jnp.float32), 'w_up': jax.random.normal(ks[3], (E, H, I), jnp.float32) * 0.02, 'b_up': jnp.zeros((E, I), jnp.float32), 'w_down': jax.random.normal(ks[4], (E, I, H), jnp.float32) * 0.02, 'b_down': jnp.zeros((E, H), jnp.float32)}
    _L1_ffn_in = _L1_ffn_setup()

    def _L2_attn_setup():
        import jax, jax.numpy as jnp
        import numpy as np
        B, T, D = (1, 256, 256)
        H, DK, DV, M = (16, 64, 128, 64)
        KEY_DIM, VALUE_DIM = (H * DK, H * DV)
        EPS = 1e-05
        CLAMP_MIN, CLAMP_MAX = (-32.0, 32.0)
        XAVIER_GAIN = 2.0 ** (-2.5)

        def _chunk_abc(q, k, v, s):
            scale = q.shape[-1] ** (-0.5)
            z = jax.lax.cumlogsumexp(s, axis=2)
            g = jnp.exp(jnp.concatenate([z[:, :, :1], z[:, :, :-1]], axis=2) - z)
            p = jnp.exp(s - z)
            tfirst = lambda x: jnp.moveaxis(x, 2, 0)
            qT, kT, vT, pT, gT = map(tfirst, (q * scale, k, v, p, g))
            b, h = (q.shape[0], q.shape[1])
            hk0 = jnp.zeros((b, h, q.shape[-1], s.shape[-1]), q.dtype)

            def step_k(hk, x):
                q_t, k_t, p_t, g_t = x
                hk = hk * g_t[:, :, None, :] + k_t[..., None] * p_t[:, :, None, :]
                return (hk, jnp.einsum('bhk,bhkm->bhm', q_t, hk))
            _, okT = jax.lax.scan(step_k, hk0, (qT, kT, pT, gT))
            pvT = jax.nn.softmax(okT, axis=-1)
            hv0 = jnp.zeros((b, h, s.shape[-1], v.shape[-1]), q.dtype)

            def step_v(hv, x):
                pv_t, v_t, p_t, g_t = x
                hv = hv * g_t[..., None] + p_t[..., None] * v_t[:, :, None, :]
                return (hv, jnp.einsum('bhm,bhmv->bhv', pv_t, hv))
            _, ovT = jax.lax.scan(step_v, hv0, (pvT, vT, pT, gT))
            return jnp.moveaxis(ovT, 0, 2)
        key = jax.random.key(seed)
        ks = jax.random.split(key, 8)

        def w(k, fan_in, fan_out):
            std = XAVIER_GAIN * np.sqrt(2.0 / (fan_in + fan_out))
            return jax.random.normal(k, (fan_in, fan_out), jnp.float32) * std
        return {'hidden_states': jax.random.normal(ks[0], (B, T, D), jnp.float32), 'Wq': w(ks[1], D, KEY_DIM), 'Wk': w(ks[2], D, KEY_DIM), 'Wv': w(ks[3], D, VALUE_DIM), 'Wg': w(ks[4], D, VALUE_DIM), 'Ws': w(ks[5], D, H * M), 'Wo': w(ks[6], VALUE_DIM, D), 'g_norm_weight': jnp.ones((DV,), jnp.float32)}
    _L2_attn_in = _L2_attn_setup()

    def _L2_ffn_setup():
        import jax, jax.numpy as jnp
        import numpy as np
        B, S, H = (4, 128, 256)
        NH = 16
        HD = H // NH
        RD = HD // 2
        LAT = H // 4
        I = 128
        NE = 8
        NSH = 1
        NR = NE - NSH
        TOPK = 2
        EPS = 1e-05
        SCALING = 8.0

        def _w(key, shape, fan_in):
            return jax.random.normal(key, shape, dtype=jnp.float32) / np.sqrt(fan_in)

        def rmsnorm(x, w):
            rms = jax.lax.rsqrt(jnp.mean(x * x, axis=-1, keepdims=True) + EPS)
            return w * rms * x

        def rope_cos_sin(seq_len):
            inv_freq = 1.0 / 10000.0 ** (jnp.arange(0, RD, 2, dtype=jnp.float32) / RD)
            t = jnp.arange(seq_len, dtype=jnp.float32)
            ang = jnp.outer(t, inv_freq)
            emb = jnp.concatenate([ang, ang], axis=-1)
            return (jnp.cos(emb), jnp.sin(emb))

        def apply_rope(x, cos, sin):
            c = cos[None, :, None, :]
            s = sin[None, :, None, :]
            x1, x2 = jnp.split(x, 2, axis=-1)
            rot = jnp.concatenate([-x2, x1], axis=-1)
            return x * c + rot * s

        def expert_ffn(x, wg, wu, wd):
            h = jax.nn.silu(x @ wg) * (x @ wu) / SCALING
            return h @ wd

        def attention(x, kv_d_w, q_d_w, k_u_w, v_u_w, q_u_w, rope_k_w, rope_q_w, o_w):
            b, s, _ = x.shape
            kv_d = x @ kv_d_w
            q_d = x @ q_d_w
            k_p = (kv_d @ k_u_w).reshape(b, s, NH, RD)
            q_p = (q_d @ q_u_w).reshape(b, s, NH, RD)
            v = (kv_d @ v_u_w).reshape(b, s, NH, HD)
            k_r = (x @ rope_k_w).reshape(b, s, NH, RD)
            q_r = (q_d @ rope_q_w).reshape(b, s, NH, RD)
            cos, sin = rope_cos_sin(s)
            k_r = apply_rope(k_r, cos, sin)
            q_r = apply_rope(q_r, cos, sin)
            k = jnp.concatenate([k_p, k_r], axis=-1)
            q = jnp.concatenate([q_p, q_r], axis=-1)
            scale = 1.0 / np.sqrt(HD)
            scores = jnp.einsum('bqhd,bkhd->bhqk', q, k) * scale
            causal = jnp.tril(jnp.ones((s, s), dtype=bool))
            scores = jnp.where(causal[None, None], scores, jnp.finfo(scores.dtype).min)
            probs = jax.nn.softmax(scores, axis=-1)
            out = jnp.einsum('bhqk,bkhd->bqhd', probs, v).reshape(b, s, H)
            return out @ o_w

        def moe(x, sh_gate, sh_up, sh_down, r_gate, r_up, r_down, router_w, router_b):
            shared = expert_ffn(x, sh_gate, sh_up, sh_down)
            logits = x @ router_w + router_b
            probs = jax.nn.sigmoid(logits)
            scores, idx = jax.lax.top_k(probs, TOPK)
            scores = scores / jnp.sum(scores, axis=-1, keepdims=True)
            w = jnp.sum(jax.nn.one_hot(idx, NR, dtype=x.dtype) * scores[..., None], axis=-2)
            combined = jnp.zeros_like(x)
            for e in range(NR):
                combined = combined + w[..., e:e + 1] * expert_ffn(x, r_gate[e], r_up[e], r_down[e])
            return shared + combined
        key = jax.random.key(seed)
        ks = jax.random.split(key, 24)
        return {'x': jax.random.normal(ks[0], (B, S, H), dtype=jnp.float32), 'ln1_w': jnp.ones((H,), jnp.float32), 'ln2_w': jnp.ones((H,), jnp.float32), 'kv_d_w': _w(ks[1], (H, LAT), H), 'q_d_w': _w(ks[2], (H, LAT), H), 'k_u_w': _w(ks[3], (LAT, H // 2), LAT), 'v_u_w': _w(ks[4], (LAT, H), LAT), 'q_u_w': _w(ks[5], (LAT, H // 2), LAT), 'rope_k_w': _w(ks[6], (H, H // 2), H), 'rope_q_w': _w(ks[7], (LAT, H // 2), LAT), 'o_w': _w(ks[8], (H, H), H), 'sh_gate': _w(ks[9], (H, I), H), 'sh_up': _w(ks[10], (H, I), H), 'sh_down': _w(ks[11], (I, H), I), 'r_gate': _w(ks[12], (NR, H, I), H), 'r_up': _w(ks[13], (NR, H, I), H), 'r_down': _w(ks[14], (NR, I, H), I), 'router_w': _w(ks[15], (H, NR), H), 'router_b': jnp.zeros((NR,), jnp.float32)}
    _L2_ffn_in = _L2_ffn_setup()

    def _L3_attn_setup():
        import jax, jax.numpy as jnp
        import numpy as np
        HIDDEN = 256
        KEY = 256
        EPS = 1e-05
        key = jax.random.key(seed)
        k1, k2, k3 = jax.random.split(key, 3)
        B, S = (4, 256)
        x = jax.random.normal(k1, (B, S, HIDDEN), dtype=jnp.float32)
        bq = 1.0 / np.sqrt(HIDDEN)
        qkv = jax.random.uniform(k2, (HIDDEN, KEY * 3), minval=-bq, maxval=bq, dtype=jnp.float32)
        bo = 1.0 / np.sqrt(KEY)
        o_proj = jax.random.uniform(k3, (KEY, HIDDEN), minval=-bo, maxval=bo, dtype=jnp.float32)
        gamma = jnp.ones((HIDDEN,), dtype=jnp.float32)
        beta = jnp.zeros((HIDDEN,), dtype=jnp.float32)
        return {'x': x, 'qkv': qkv, 'o_proj': o_proj, 'gamma': gamma, 'beta': beta}
    _L3_attn_in = _L3_attn_setup()

    def _L3_ffn_setup():
        import jax, jax.numpy as jnp
        import numpy as np
        B, S, D, M, E, K = (4, 256, 256, 512, 8, 2)

        def _routed_moe(x, gate_w, w0, w1, wo):
            T = x.shape[0]
            logits = jnp.einsum('td,de->te', x, gate_w)
            top_logits, top_idx = jax.lax.top_k(logits, K)
            top_w = jax.nn.softmax(top_logits, axis=-1)
            cw = jnp.zeros((T, E), dtype=x.dtype).at[jnp.arange(T)[:, None], top_idx].add(top_w)
            out = jnp.zeros_like(x)
            for e in range(E):
                h = jax.nn.silu(x @ w0[e]) * (x @ w1[e])
                out = out + cw[:, e:e + 1] * (h @ wo[e])
            return out
        key = jax.random.key(seed)
        ks = jax.random.split(key, 5)
        inputs = jax.random.normal(ks[0], (B, S, D), dtype=jnp.float32)
        gate_w = jax.random.normal(ks[1], (D, E), dtype=jnp.float32) * D ** (-0.5)
        w0 = jax.random.normal(ks[2], (E, D, M), dtype=jnp.float32) * D ** (-0.5)
        w1 = jax.random.normal(ks[3], (E, D, M), dtype=jnp.float32) * D ** (-0.5)
        wo = jax.random.normal(ks[4], (E, M, D), dtype=jnp.float32) * M ** (-0.5)
        decoder_segment_ids = jax.random.randint(jax.random.fold_in(key, 1), (B, S), 0, 2).astype(jnp.int32)
        decoder_positions = jnp.tile(jnp.arange(S, dtype=jnp.int32)[None, :], (B, 1))
        return {'inputs': inputs, 'gate_w': gate_w, 'w0': w0, 'w1': w1, 'wo': wo, 'decoder_segment_ids': decoder_segment_ids, 'decoder_positions': decoder_positions}
    _L3_ffn_in = _L3_ffn_setup()
    _d = {'L0_attn_x': _L0_attn_in['x'], 'L0_attn_A': _L0_attn_in['A'], 'L0_attn_B': _L0_attn_in['B'], 'L0_attn_C_w': _L0_attn_in['C_w'], 'L0_attn_C_b': _L0_attn_in['C_b'], 'L0_attn_D_w': _L0_attn_in['D_w'], 'L0_attn_D_b': _L0_attn_in['D_b'], 'L0_attn_log_delta': _L0_attn_in['log_delta'], 'L0_ffn_in_gamma': _L0_ffn_in['in_gamma'], 'L0_ffn_in_beta': _L0_ffn_in['in_beta'], 'L0_ffn_agg_w': _L0_ffn_in['agg_w'], 'L0_ffn_agg_b': _L0_ffn_in['agg_b'], 'L0_ffn_pn_gamma': _L0_ffn_in['pn_gamma'], 'L0_ffn_pn_beta': _L0_ffn_in['pn_beta'], 'L0_ffn_d1_w': _L0_ffn_in['d1_w'], 'L0_ffn_d1_b': _L0_ffn_in['d1_b'], 'L0_ffn_d2_w': _L0_ffn_in['d2_w'], 'L0_ffn_d2_b': _L0_ffn_in['d2_b'], 'L0_ffn_bc_w': _L0_ffn_in['bc_w'], 'L0_ffn_bc_b': _L0_ffn_in['bc_b'], 'L0_ffn_gate_w': _L0_ffn_in['gate_w'], 'L0_ffn_gate_b': _L0_ffn_in['gate_b'], 'L0_ffn_out_gamma': _L0_ffn_in['out_gamma'], 'L0_ffn_out_beta': _L0_ffn_in['out_beta'], 'L1_ffn_gate_w': _L1_ffn_in['gate_w'], 'L1_ffn_gate_b': _L1_ffn_in['gate_b'], 'L1_ffn_w_gate': _L1_ffn_in['w_gate'], 'L1_ffn_b_gate': _L1_ffn_in['b_gate'], 'L1_ffn_w_up': _L1_ffn_in['w_up'], 'L1_ffn_b_up': _L1_ffn_in['b_up'], 'L1_ffn_w_down': _L1_ffn_in['w_down'], 'L1_ffn_b_down': _L1_ffn_in['b_down'], 'L2_attn_Wq': _L2_attn_in['Wq'], 'L2_attn_Wk': _L2_attn_in['Wk'], 'L2_attn_Wv': _L2_attn_in['Wv'], 'L2_attn_Wg': _L2_attn_in['Wg'], 'L2_attn_Ws': _L2_attn_in['Ws'], 'L2_attn_Wo': _L2_attn_in['Wo'], 'L2_attn_g_norm_weight': _L2_attn_in['g_norm_weight'], 'L2_ffn_ln1_w': _L2_ffn_in['ln1_w'], 'L2_ffn_ln2_w': _L2_ffn_in['ln2_w'], 'L2_ffn_kv_d_w': _L2_ffn_in['kv_d_w'], 'L2_ffn_q_d_w': _L2_ffn_in['q_d_w'], 'L2_ffn_k_u_w': _L2_ffn_in['k_u_w'], 'L2_ffn_v_u_w': _L2_ffn_in['v_u_w'], 'L2_ffn_q_u_w': _L2_ffn_in['q_u_w'], 'L2_ffn_rope_k_w': _L2_ffn_in['rope_k_w'], 'L2_ffn_rope_q_w': _L2_ffn_in['rope_q_w'], 'L2_ffn_o_w': _L2_ffn_in['o_w'], 'L2_ffn_sh_gate': _L2_ffn_in['sh_gate'], 'L2_ffn_sh_up': _L2_ffn_in['sh_up'], 'L2_ffn_sh_down': _L2_ffn_in['sh_down'], 'L2_ffn_r_gate': _L2_ffn_in['r_gate'], 'L2_ffn_r_up': _L2_ffn_in['r_up'], 'L2_ffn_r_down': _L2_ffn_in['r_down'], 'L2_ffn_router_w': _L2_ffn_in['router_w'], 'L2_ffn_router_b': _L2_ffn_in['router_b'], 'L3_attn_qkv': _L3_attn_in['qkv'], 'L3_attn_o_proj': _L3_attn_in['o_proj'], 'L3_attn_gamma': _L3_attn_in['gamma'], 'L3_attn_beta': _L3_attn_in['beta'], 'L3_ffn_gate_w': _L3_ffn_in['gate_w'], 'L3_ffn_w0': _L3_ffn_in['w0'], 'L3_ffn_w1': _L3_ffn_in['w1'], 'L3_ffn_wo': _L3_ffn_in['wo'], 'L3_ffn_decoder_segment_ids': _L3_ffn_in['decoder_segment_ids'], 'L3_ffn_decoder_positions': _L3_ffn_in['decoder_positions']}
    _x0 = _d['L0_attn_x']
    _d['L0_attn_x'] = jax.random.normal(jax.random.fold_in(jax.random.key(seed), 1), (4, 512, 256), dtype=_x0.dtype)
    del _x0
    return _d

def reference(L0_attn_x, L0_attn_A, L0_attn_B, L0_attn_C_w, L0_attn_C_b, L0_attn_D_w, L0_attn_D_b, L0_attn_log_delta, L0_ffn_in_gamma, L0_ffn_in_beta, L0_ffn_agg_w, L0_ffn_agg_b, L0_ffn_pn_gamma, L0_ffn_pn_beta, L0_ffn_d1_w, L0_ffn_d1_b, L0_ffn_d2_w, L0_ffn_d2_b, L0_ffn_bc_w, L0_ffn_bc_b, L0_ffn_gate_w, L0_ffn_gate_b, L0_ffn_out_gamma, L0_ffn_out_beta, L1_ffn_gate_w, L1_ffn_gate_b, L1_ffn_w_gate, L1_ffn_b_gate, L1_ffn_w_up, L1_ffn_b_up, L1_ffn_w_down, L1_ffn_b_down, L2_attn_Wq, L2_attn_Wk, L2_attn_Wv, L2_attn_Wg, L2_attn_Ws, L2_attn_Wo, L2_attn_g_norm_weight, L2_ffn_ln1_w, L2_ffn_ln2_w, L2_ffn_kv_d_w, L2_ffn_q_d_w, L2_ffn_k_u_w, L2_ffn_v_u_w, L2_ffn_q_u_w, L2_ffn_rope_k_w, L2_ffn_rope_q_w, L2_ffn_o_w, L2_ffn_sh_gate, L2_ffn_sh_up, L2_ffn_sh_down, L2_ffn_r_gate, L2_ffn_r_up, L2_ffn_r_down, L2_ffn_router_w, L2_ffn_router_b, L3_attn_qkv, L3_attn_o_proj, L3_attn_gamma, L3_attn_beta, L3_ffn_gate_w, L3_ffn_w0, L3_ffn_w1, L3_ffn_wo, L3_ffn_decoder_segment_ids, L3_ffn_decoder_positions):

    def _L0_attn_ref(x, A, B, C_w, C_b, D_w, D_b, log_delta):
        import jax, jax.numpy as jnp
        import numpy as np
        B_SZ, T, D, N = (4, 256, 256, 64)

        def _reference_tuple_inner(x, A, B, C_w, C_b, D_w, D_b, log_delta):
            A_diag = jnp.exp(-jax.nn.softplus(log_delta))
            x_proj = (x @ C_w.T + C_b) * jax.nn.sigmoid(x @ D_w.T + D_b)
            xp_t = jnp.transpose(x_proj, (1, 0, 2))

            def step(g, xt):
                g = g * A_diag + xt
                return (g, g)
            g_last, gs = jax.lax.scan(step, jnp.zeros((x.shape[0], x.shape[2]), x.dtype), xp_t)
            gs = jnp.transpose(gs, (1, 0, 2))
            AB = jnp.sum(A * B, axis=-1)
            output = gs * AB
            h = g_last[:, :, None] * B[None, :, :]
            return (output, h)
        return _reference_tuple_inner(x, A, B, C_w, C_b, D_w, D_b, log_delta)[0]

    def _L0_ffn_ref(x, in_gamma, in_beta, agg_w, agg_b, pn_gamma, pn_beta, d1_w, d1_b, d2_w, d2_b, bc_w, bc_b, gate_w, gate_b, out_gamma, out_beta):
        import jax, jax.numpy as jnp
        import numpy as np
        EPS = 1e-06
        K_STEPS = 4
        USE_GATING = True

        def layer_norm(x, gamma, beta):
            mu = jnp.mean(x, axis=-1, keepdims=True)
            var = jnp.mean(jnp.square(x - mu), axis=-1, keepdims=True)
            return (x - mu) * jax.lax.rsqrt(var + EPS) * gamma + beta
        x_norm = layer_norm(x, in_gamma, in_beta)
        thought = x_norm[:, -1, :] @ agg_w + agg_b
        for _ in range(K_STEPS):
            t = layer_norm(thought, pn_gamma, pn_beta)
            t = jax.nn.gelu(t @ d1_w + d1_b, approximate=False)
            thought = thought + (t @ d2_w + d2_b)
        broadcast = (thought @ bc_w + bc_b)[:, None, :]
        if USE_GATING:
            gate = jax.nn.sigmoid(x @ gate_w + gate_b)
            out = x + gate * broadcast
        else:
            out = x + broadcast
        return layer_norm(out, out_gamma, out_beta)

    def _L1_attn_ref(x):
        import jax, jax.numpy as jnp
        import numpy as np
        D_MODEL = 256
        NUM_HEADS = 16
        DILATION = 2
        SEG = 64
        HEAD_DIM = D_MODEL // NUM_HEADS

        def _dilated_attention(x):
            B, N, D = x.shape
            w, r, H, hd = (SEG, DILATION, NUM_HEADS, HEAD_DIM)
            pad = -N % w
            x = jnp.pad(x, ((0, 0), (0, pad), (0, 0)))
            Np = N + pad
            nseg = Np // w
            s = w // r
            xs = x.reshape(B, nseg, w, H, hd).transpose(0, 1, 3, 2, 4)
            offsets = jnp.arange(H) % r
            idx = offsets[:, None] + jnp.arange(s)[None, :] * r
            g = jnp.take_along_axis(xs, idx[None, None, :, :, None], axis=3)
            scale = jnp.asarray(hd, x.dtype) ** (-0.5)
            scores = jnp.einsum('bnhqd,bnhkd->bnhqk', g, g) * scale
            attn = jax.nn.softmax(scores, axis=-1)
            out = jnp.einsum('bnhqk,bnhkd->bnhqd', attn, g)
            out_full = jnp.zeros((B, nseg, H, w, hd), dtype=x.dtype)
            out_full = out_full.at[:, :, jnp.arange(H)[:, None], idx, :].set(out)
            out_full = out_full.transpose(0, 1, 3, 2, 4).reshape(B, Np, D)
            return out_full[:, :N, :]
        return _dilated_attention(x)

    def _L1_ffn_ref(hidden_states, gate_w, gate_b, w_gate, b_gate, w_up, b_up, w_down, b_down):
        import jax, jax.numpy as jnp
        import numpy as np
        SWIGLU_ALPHA = 1.702
        SWIGLU_LIMIT = 7.0
        B, S, H, E, K, I = (2, 256, 256, 32, 4, 128)
        Bb, Ss, Hh = hidden_states.shape
        x = hidden_states.reshape(-1, Hh)
        logits = x @ gate_w.T + gate_b
        topk_logits, topk_idx = jax.lax.top_k(logits, K)
        topk_weight = jax.nn.softmax(topk_logits.astype(jnp.float32), axis=-1)
        flat_idx = topk_idx.reshape(-1)
        xs = jnp.repeat(x, K, axis=0)
        order = jnp.argsort(flat_idx)
        xt = xs[order]
        gid = flat_idx[order]
        group_sizes = jnp.bincount(flat_idx, length=E).astype(jnp.int32)
        gate = jax.lax.ragged_dot(xt, w_gate, group_sizes) + b_gate[gid]
        up = jax.lax.ragged_dot(xt, w_up, group_sizes) + b_up[gid]
        gate = jnp.minimum(gate, SWIGLU_LIMIT)
        up = jnp.clip(up, -SWIGLU_LIMIT, SWIGLU_LIMIT)
        glu = gate * jax.nn.sigmoid(SWIGLU_ALPHA * gate)
        activated = (up + 1.0) * glu
        outs = jax.lax.ragged_dot(activated, w_down, group_sizes) + b_down[gid]
        inv = jnp.argsort(order)
        outs = outs[inv].reshape(-1, K, Hh)
        y = jnp.sum(outs * topk_weight[..., None], axis=1).astype(x.dtype)
        return y.reshape(Bb, Ss, Hh)

    def _L2_attn_ref(hidden_states, Wq, Wk, Wv, Wg, Ws, Wo, g_norm_weight):
        import jax, jax.numpy as jnp
        import numpy as np
        B, T, D = (1, 256, 256)
        H, DK, DV, M = (16, 64, 128, 64)
        KEY_DIM, VALUE_DIM = (H * DK, H * DV)
        EPS = 1e-05
        CLAMP_MIN, CLAMP_MAX = (-32.0, 32.0)
        XAVIER_GAIN = 2.0 ** (-2.5)

        def _chunk_abc(q, k, v, s):
            scale = q.shape[-1] ** (-0.5)
            z = jax.lax.cumlogsumexp(s, axis=2)
            g = jnp.exp(jnp.concatenate([z[:, :, :1], z[:, :, :-1]], axis=2) - z)
            p = jnp.exp(s - z)
            tfirst = lambda x: jnp.moveaxis(x, 2, 0)
            qT, kT, vT, pT, gT = map(tfirst, (q * scale, k, v, p, g))
            b, h = (q.shape[0], q.shape[1])
            hk0 = jnp.zeros((b, h, q.shape[-1], s.shape[-1]), q.dtype)

            def step_k(hk, x):
                q_t, k_t, p_t, g_t = x
                hk = hk * g_t[:, :, None, :] + k_t[..., None] * p_t[:, :, None, :]
                return (hk, jnp.einsum('bhk,bhkm->bhm', q_t, hk))
            _, okT = jax.lax.scan(step_k, hk0, (qT, kT, pT, gT))
            pvT = jax.nn.softmax(okT, axis=-1)
            hv0 = jnp.zeros((b, h, s.shape[-1], v.shape[-1]), q.dtype)

            def step_v(hv, x):
                pv_t, v_t, p_t, g_t = x
                hv = hv * g_t[..., None] + p_t[..., None] * v_t[:, :, None, :]
                return (hv, jnp.einsum('bhm,bhmv->bhv', pv_t, hv))
            _, ovT = jax.lax.scan(step_v, hv0, (pvT, vT, pT, gT))
            return jnp.moveaxis(ovT, 0, 2)
        b, t, _ = hidden_states.shape
        to_heads = lambda x, d: jnp.transpose(x.reshape(b, t, H, d), (0, 2, 1, 3))
        q = to_heads(hidden_states @ Wq, DK)
        k = to_heads(hidden_states @ Wk, DK)
        v = to_heads(hidden_states @ Wv, DV)
        s = jnp.clip(to_heads(hidden_states @ Ws, M), CLAMP_MIN, CLAMP_MAX)
        o = jnp.transpose(_chunk_abc(q, k, v, s), (0, 2, 1, 3))
        g = (hidden_states @ Wg).reshape(b, t, H, DV)
        o = o * jax.lax.rsqrt(jnp.mean(jnp.square(o), axis=-1, keepdims=True) + EPS) * g_norm_weight
        o = o * (g * jax.nn.sigmoid(g))
        return o.reshape(b, t, VALUE_DIM) @ Wo

    def _L2_ffn_ref(x, ln1_w, ln2_w, kv_d_w, q_d_w, k_u_w, v_u_w, q_u_w, rope_k_w, rope_q_w, o_w, sh_gate, sh_up, sh_down, r_gate, r_up, r_down, router_w, router_b):
        import jax, jax.numpy as jnp
        import numpy as np
        B, S, H = (4, 128, 256)
        NH = 16
        HD = H // NH
        RD = HD // 2
        LAT = H // 4
        I = 128
        NE = 8
        NSH = 1
        NR = NE - NSH
        TOPK = 2
        EPS = 1e-05
        SCALING = 8.0

        def _w(key, shape, fan_in):
            return jax.random.normal(key, shape, dtype=jnp.float32) / np.sqrt(fan_in)

        def rmsnorm(x, w):
            rms = jax.lax.rsqrt(jnp.mean(x * x, axis=-1, keepdims=True) + EPS)
            return w * rms * x

        def rope_cos_sin(seq_len):
            inv_freq = 1.0 / 10000.0 ** (jnp.arange(0, RD, 2, dtype=jnp.float32) / RD)
            t = jnp.arange(seq_len, dtype=jnp.float32)
            ang = jnp.outer(t, inv_freq)
            emb = jnp.concatenate([ang, ang], axis=-1)
            return (jnp.cos(emb), jnp.sin(emb))

        def apply_rope(x, cos, sin):
            c = cos[None, :, None, :]
            s = sin[None, :, None, :]
            x1, x2 = jnp.split(x, 2, axis=-1)
            rot = jnp.concatenate([-x2, x1], axis=-1)
            return x * c + rot * s

        def expert_ffn(x, wg, wu, wd):
            h = jax.nn.silu(x @ wg) * (x @ wu) / SCALING
            return h @ wd

        def attention(x, kv_d_w, q_d_w, k_u_w, v_u_w, q_u_w, rope_k_w, rope_q_w, o_w):
            b, s, _ = x.shape
            kv_d = x @ kv_d_w
            q_d = x @ q_d_w
            k_p = (kv_d @ k_u_w).reshape(b, s, NH, RD)
            q_p = (q_d @ q_u_w).reshape(b, s, NH, RD)
            v = (kv_d @ v_u_w).reshape(b, s, NH, HD)
            k_r = (x @ rope_k_w).reshape(b, s, NH, RD)
            q_r = (q_d @ rope_q_w).reshape(b, s, NH, RD)
            cos, sin = rope_cos_sin(s)
            k_r = apply_rope(k_r, cos, sin)
            q_r = apply_rope(q_r, cos, sin)
            k = jnp.concatenate([k_p, k_r], axis=-1)
            q = jnp.concatenate([q_p, q_r], axis=-1)
            scale = 1.0 / np.sqrt(HD)
            scores = jnp.einsum('bqhd,bkhd->bhqk', q, k) * scale
            causal = jnp.tril(jnp.ones((s, s), dtype=bool))
            scores = jnp.where(causal[None, None], scores, jnp.finfo(scores.dtype).min)
            probs = jax.nn.softmax(scores, axis=-1)
            out = jnp.einsum('bhqk,bkhd->bqhd', probs, v).reshape(b, s, H)
            return out @ o_w

        def moe(x, sh_gate, sh_up, sh_down, r_gate, r_up, r_down, router_w, router_b):
            shared = expert_ffn(x, sh_gate, sh_up, sh_down)
            logits = x @ router_w + router_b
            probs = jax.nn.sigmoid(logits)
            scores, idx = jax.lax.top_k(probs, TOPK)
            scores = scores / jnp.sum(scores, axis=-1, keepdims=True)
            w = jnp.sum(jax.nn.one_hot(idx, NR, dtype=x.dtype) * scores[..., None], axis=-2)
            combined = jnp.zeros_like(x)
            for e in range(NR):
                combined = combined + w[..., e:e + 1] * expert_ffn(x, r_gate[e], r_up[e], r_down[e])
            return shared + combined
        h = x + attention(rmsnorm(x, ln1_w), kv_d_w, q_d_w, k_u_w, v_u_w, q_u_w, rope_k_w, rope_q_w, o_w)
        out = h + moe(rmsnorm(h, ln2_w), sh_gate, sh_up, sh_down, r_gate, r_up, r_down, router_w, router_b)
        return out

    def _L3_attn_ref(x, qkv, o_proj, gamma, beta):
        import jax, jax.numpy as jnp
        import numpy as np
        HIDDEN = 256
        KEY = 256
        EPS = 1e-05
        residual = x
        mu = jnp.mean(x, axis=-1, keepdims=True)
        var = jnp.mean((x - mu) ** 2, axis=-1, keepdims=True)
        x_norm = (x - mu) / jnp.sqrt(var + EPS) * gamma + beta
        q = x_norm @ qkv[:, :KEY]
        k = x_norm @ qkv[:, KEY:2 * KEY]
        v = x_norm @ qkv[:, 2 * KEY:]
        scale = 1.0 / jnp.sqrt(jnp.float32(KEY))
        scores = jnp.einsum('bsk,btk->bst', q, k) * scale
        S_len = x.shape[1]
        causal = jnp.tril(jnp.ones((S_len, S_len), dtype=bool))
        scores = jnp.where(causal[None], scores, -jnp.inf)
        attn = jax.nn.softmax(scores, axis=-1)
        out = attn @ v
        out = out @ o_proj
        return out + residual

    def _L3_ffn_ref(inputs, gate_w, w0, w1, wo, decoder_segment_ids, decoder_positions):
        import jax, jax.numpy as jnp
        import numpy as np
        B, S, D, M, E, K = (4, 256, 256, 512, 8, 2)

        def _routed_moe(x, gate_w, w0, w1, wo):
            T = x.shape[0]
            logits = jnp.einsum('td,de->te', x, gate_w)
            top_logits, top_idx = jax.lax.top_k(logits, K)
            top_w = jax.nn.softmax(top_logits, axis=-1)
            cw = jnp.zeros((T, E), dtype=x.dtype).at[jnp.arange(T)[:, None], top_idx].add(top_w)
            out = jnp.zeros_like(x)
            for e in range(E):
                h = jax.nn.silu(x @ w0[e]) * (x @ w1[e])
                out = out + cw[:, e:e + 1] * (h @ wo[e])
            return out
        b, s, d = inputs.shape
        x = inputs.reshape(b * s, d)
        out = _routed_moe(x, gate_w, w0, w1, wo)
        return out.reshape(b, s, d)
    x = L0_attn_x
    xn = _layernorm(x, axis=-1)
    x = x + _L0_attn_ref(xn, L0_attn_A, L0_attn_B, L0_attn_C_w, L0_attn_C_b, L0_attn_D_w, L0_attn_D_b, L0_attn_log_delta) + _L0_ffn_ref(xn, L0_ffn_in_gamma, L0_ffn_in_beta, L0_ffn_agg_w, L0_ffn_agg_b, L0_ffn_pn_gamma, L0_ffn_pn_beta, L0_ffn_d1_w, L0_ffn_d1_b, L0_ffn_d2_w, L0_ffn_d2_b, L0_ffn_bc_w, L0_ffn_bc_b, L0_ffn_gate_w, L0_ffn_gate_b, L0_ffn_out_gamma, L0_ffn_out_beta)
    xn = _layernorm(x, axis=-1)
    x = x + _L1_attn_ref(xn) + _L1_ffn_ref(xn, L1_ffn_gate_w, L1_ffn_gate_b, L1_ffn_w_gate, L1_ffn_b_gate, L1_ffn_w_up, L1_ffn_b_up, L1_ffn_w_down, L1_ffn_b_down)
    xn = _layernorm(x, axis=-1)
    x = x + _L2_attn_ref(xn, L2_attn_Wq, L2_attn_Wk, L2_attn_Wv, L2_attn_Wg, L2_attn_Ws, L2_attn_Wo, L2_attn_g_norm_weight) + _L2_ffn_ref(xn, L2_ffn_ln1_w, L2_ffn_ln2_w, L2_ffn_kv_d_w, L2_ffn_q_d_w, L2_ffn_k_u_w, L2_ffn_v_u_w, L2_ffn_q_u_w, L2_ffn_rope_k_w, L2_ffn_rope_q_w, L2_ffn_o_w, L2_ffn_sh_gate, L2_ffn_sh_up, L2_ffn_sh_down, L2_ffn_r_gate, L2_ffn_r_up, L2_ffn_r_down, L2_ffn_router_w, L2_ffn_router_b)
    xn = _layernorm(x, axis=-1)
    x = x + _L3_attn_ref(xn, L3_attn_qkv, L3_attn_o_proj, L3_attn_gamma, L3_attn_beta) + _L3_ffn_ref(xn, L3_ffn_gate_w, L3_ffn_w0, L3_ffn_w1, L3_ffn_wo, L3_ffn_decoder_segment_ids, L3_ffn_decoder_positions)
    return x

_drawn_inputs = setup_inputs


def setup_inputs(seed=0):
    import zlib

    import numpy as np

    out = dict(_drawn_inputs(seed))
    spreads = {'L0_attn_log_delta': (0.0, 0.1),
     'L0_ffn_in_gamma': (1.0, 0.6),
     'L0_ffn_in_beta': (0.0, 0.8),
     'L0_ffn_agg_b': (0.0, 0.743),
     'L0_ffn_pn_gamma': (1.0, 0.6),
     'L0_ffn_pn_beta': (0.0, 0.8),
     'L0_ffn_d1_b': (0.0, 0.8),
     'L0_ffn_d2_b': (0.0, 0.333),
     'L0_ffn_bc_b': (0.0, 0.452),
     'L0_ffn_gate_b': (0.0, 0.8),
     'L0_ffn_out_gamma': (1.0, 0.2),
     'L0_ffn_out_beta': (0.0, 0.1),
     'L1_ffn_gate_b': (0.0, 0.768),
     'L1_ffn_b_gate': (0.0, 0.8),
     'L1_ffn_b_up': (0.0, 0.8),
     'L1_ffn_b_down': (0.0, 0.51),
     'L2_attn_g_norm_weight': (1.0, 0.6),
     'L2_ffn_ln1_w': (1.0, 0.6),
     'L2_ffn_ln2_w': (1.0, 0.6),
     'L2_ffn_router_b': (0.0, 0.8),
     'L3_attn_gamma': (1.0, 0.6),
     'L3_attn_beta': (0.0, 0.8)}
    factors = {'L0_attn_D_b': 3.422,
     'L0_ffn_gate_w': 7.658,
     'L1_ffn_gate_w': 3.773,
     'L1_ffn_w_gate': 7.959,
     'L1_ffn_w_up': 8.0,
     'L1_ffn_w_down': 7.528,
     'L2_attn_Wq': 64.0,
     'L2_attn_Wk': 64.0,
     'L2_attn_Wv': 8.0,
     'L2_attn_Wg': 8.0,
     'L2_attn_Ws': 30.828,
     'L2_attn_Wo': 8.0,
     'L2_ffn_sh_gate': 3.182,
     'L2_ffn_sh_up': 2.969,
     'L2_ffn_sh_down': 2.935,
     'L2_ffn_r_gate': 4.322,
     'L2_ffn_r_up': 4.121,
     'L2_ffn_r_down': 4.015,
     'L2_ffn_router_w': 4.77,
     'L3_attn_qkv': 4.574,
     'L3_attn_o_proj': 4.54,
     'L3_ffn_gate_w': 2.685}
    for name, (base, spread) in spreads.items():
        noise = np.random.default_rng([zlib.crc32(name.encode()), seed]).standard_normal(out[name].shape)
        drawn = base * np.exp(spread * noise) if base else spread * noise
        out[name] = jnp.asarray(drawn.astype(out[name].dtype))
    for name, factor in factors.items():
        out[name] = (out[name] * factor).astype(out[name].dtype)
    return out
```

```python
from contextlib import ExitStack

import numpy as np

import concourse.bass as bass
from concourse import mybir

F32 = mybir.dt.float32
ALU = mybir.AluOpType
ACT = mybir.ActivationFunctionType
AX = mybir.AxisListType

P = 128
B, T, D = 4, 512, 256
TOK = B * T
TILES = TOK // P
DC = D // P
GROUPS = TILES // 2
TB = T // P
NEG = -1e30

C_ID, C_TRI, C_NEG, C_BLK, C_EVEN, C_HALF, C_ONE, C_COUNT = 0, 128, 256, 384, 512, 514, 530, 531
C_KEYS = C_COUNT + 32
C_END = C_KEYS + 2


class Steps:

    def __init__(self, eng, sem, base=0, total=None):
        self.eng, self.sem, self.base, self.total, self.n = eng, sem, base, total, 0

    def __call__(self, instruction):
        instruction.then_inc(self.sem, 1)
        self.n += 1
        self.eng.wait_ge(self.sem, self.base + self.n)

    def close(self):
        assert self.total is None or self.n == self.total, self.n


def wait_apart(eng, sem, value, waited):
    eng.wait_ge(sem, value)
    eng.sem_inc(waited, 1)


class Stage:

    def __init__(self, nc, keep, scope, name):
        self.nc, self.keep, self.scope, self.name = nc, keep, scope, name

    def sem(self, name):
        handle = self.nc.alloc_semaphore(name=f"{self.name}_{name}")
        self.keep.append(handle)
        return handle

    def sb(self, name, shape):
        return self.scope.enter_context(self.nc.sbuf_tensor(f"{self.name}_{name}", shape, F32))

    def ps(self, name, shape):
        return self.scope.enter_context(self.nc.psum_tensor(f"{self.name}_{name}", shape, F32))


class Core:
    pass


def release(nc, used):
    nc.clear_and_free_semaphores(used)
    nc.all_engine_barrier()
    used.clear()


def in_chunks(w):
    if len(w.shape) == 1:
        return w.rearrange("(c p) -> p c", p=P)
    return w.rearrange("(c p) n -> p c n", p=P)


def on_all_partitions(row, n):
    return row.unsqueeze(0).to_broadcast([n] + list(row.shape))


def token_rows(x, p):
    return x.rearrange("b t d -> (b t) d").rearrange("(g q p) d -> q g p d", q=P, p=2)[:, :, p, :]


def col_group(t, g, p):
    return t[:].rearrange("d c (g q p) -> d c g q p", q=P, p=2)[:, :, g, :, p]


def setup(nc, st, core, dram):
    sem = st.sem
    consts_in, x_in = sem("consts_in"), sem("x_in")
    with nc.Block() as block:
        @block.sync
        def _(sp):
            sp.dma_start(core.consts[:], dram["consts"]).then_inc(consts_in, 16)
            for p in range(2):
                sp.dma_start(core.x[:, p::2, :], token_rows(dram["L0_attn_x"], p)).then_inc(x_in, 16)
            sp.wait_ge(consts_in, 16)
            sp.wait_ge(x_in, 32)


def small_stats(do, eng, raw, mean, var, eps, rms):
    me, mo = raw[:, :, 1], raw[:, :, 4]
    do(eng.tensor_tensor(mean[:], me, mo, ALU.add))
    do(eng.tensor_tensor(var[:], me, mo, ALU.subtract))
    do(eng.tensor_tensor(var[:], var[:], var[:], ALU.mult))
    do(eng.scalar_tensor_tensor(out=var[:], in0=raw[:, :, 2], scalar=4.0 / D, in1=var[:],
                                op0=ALU.mult, op1=ALU.add))
    do(eng.scalar_tensor_tensor(out=var[:], in0=raw[:, :, 5], scalar=4.0 / D, in1=var[:],
                                op0=ALU.mult, op1=ALU.add))
    if rms:
        do(eng.tensor_tensor(raw[:, :, 0], mean[:], mean[:], ALU.mult))
        do(eng.tensor_tensor(var[:], var[:], raw[:, :, 0], ALU.add))
    do(eng.tensor_scalar(mean[:], mean[:], 0.5, None, ALU.mult))
    do(eng.tensor_scalar(var[:], var[:], 0.25, eps, ALU.mult, ALU.add))


def normalise(nc, st, core, src, tok_out, out_T, eps, rms=False, gain=None, shift=None):
    sem = st.sem
    raw = st.sb("raw", [P, TILES, 6])
    mean, var, rstd = (st.sb(n, [P, TILES]) for n in ("mean", "var", "rstd"))
    row = st.sb("row", [P, 2, D])
    turned = st.ps("turned", [P, 2, 512])
    gs = st.sb("gain_shift", [P, 2, DC])
    gain_in, stats, dve_step = sem("gain_in"), sem("stats"), sem("dve_step")
    rstd_ready = sem("rstd_ready")
    rows_ready, rows_free, rows_turned = sem("rows_ready"), sem("rows_free"), sem("rows_turned")
    n_gain = (gain is not None) + (shift is not None)
    with nc.Block() as block:
        @block.sync
        def _(sp):
            if gain is not None:
                sp.dma_start(gs[:, 0, :], in_chunks(gain), allow_slow_non_contiguous=True).then_inc(gain_in, 16)
            if shift is not None:
                sp.dma_start(gs[:, 1, :], in_chunks(shift), allow_slow_non_contiguous=True).then_inc(gain_in, 16)

        @block.vector
        def _(dve):
            with dve.Fori(0, TILES) as i:
                dve.bn_stats(raw[:, i, :], src[:, i, :]).then_inc(stats, 1)
            dve.wait_ge(stats, TILES)
            do = Steps(dve, dve_step)
            small_stats(do, dve, raw, mean, var, eps, rms)
            dve.wait_ge(rstd_ready, 1)
            with dve.Fori(0, GROUPS) as g:
                for p in range(2):
                    dve.wait_ge(rows_free, 2 * g + p + 1)
                    t = 2 * g + p
                    if rms:
                        dve.tensor_scalar(row[:, p, :], src[:, t, :], rstd[:, bass.ds(t, 1)], None,
                                          ALU.mult).then_inc(rows_ready, 1)
                    else:
                        dve.tensor_scalar(row[:, p, :], src[:, t, :], mean[:, bass.ds(t, 1)],
                                          rstd[:, bass.ds(t, 1)], ALU.subtract,
                                          ALU.mult).then_inc(rows_ready, 1)

        @block.gpsimd
        def _(pool):
            pool.wait_ge(dve_step, 9 if rms else 7)
            pool.tensor_tensor(rstd[:], var[:], core.consts[:, C_HALF:C_HALF + TILES],
                               ALU.pow).then_inc(rstd_ready, 1)

        @block.tensor
        def _(pe):
            with pe.Fori(0, GROUPS) as g:
                for p in range(2):
                    pe.wait_ge(rows_ready, 2 * g + p + 1)
                    for c in range(DC):
                        ins = pe.transpose(turned[:, p, c * P:(c + 1) * P], row[:, p, c * P:(c + 1) * P],
                                           core.ident)
                    ins.then_inc(rows_turned, 1)

        @block.scalar
        def _(act):
            act.preload_act_table(ACT.Identity)
            act.sem_inc(rows_free, 2)
            if n_gain:
                act.wait_ge(gain_in, 16 * n_gain)
            with act.Fori(0, GROUPS) as g:
                for p in range(2):
                    act.wait_ge(rows_turned, 2 * g + p + 1)
                    if tok_out is not None:
                        act.activation(tok_out[:, 2 * g + p, :], row[:, p, :], ACT.Copy)
                    out = col_group(out_T, g, p)
                    if not n_gain:
                        act.activation(out, turned[:, p, 0:D].rearrange("p (c q) -> p c q", c=DC),
                                       ACT.Copy).then_inc(rows_free, 1)
                        continue
                    for c in range(DC):
                        ins = act.activation(out[:, c, :], turned[:, p, c * P:(c + 1) * P], ACT.Identity,
                                             bias=gs[:, 1, c:c + 1] if shift is not None else 0.0,
                                             scale=gs[:, 0, c:c + 1])
                    ins.then_inc(rows_free, 1)


def layer0_mix(nc, st, core, dram, gsT, gateT, last_rows):
    sem = st.sem
    H = 1024
    HC = H // P
    KS = 4
    w_c, w_d, w_g = (st.sb(n, [P, DC, D]) for n in ("w_c", "w_d", "w_g"))
    w_agg, w_bc = st.sb("w_agg", [P, DC, D]), st.sb("w_bc", [P, DC, D])
    w1, w2 = st.sb("w1", [P, DC, H]), st.sb("w2", [P, HC, D])
    cols = st.sb("cols", [P, 5, DC])
    b1 = st.sb("b1", [P, HC])
    rows = st.sb("rows", [B, 6, D])
    ab = st.sb("ab", [P, 2, DC, 64])
    ab_sum = core.ab_sum
    decay_col, decay = st.sb("decay_col", [P, DC]), st.sb("decay", [P, DC, T])
    sig = st.sb("sig", [P, 2, T])
    drive = st.sb("drive", [P, 2, T])
    thought, tnorm = st.sb("thought", [B, D]), st.sb("tnorm", [B, D])
    tT, hT = st.sb("tT", [P, DC, B]), st.sb("hT", [P, HC, B])
    raw, mean, var, rstd = st.sb("traw", [B, 6]), st.sb("tmean", [B, 1]), st.sb("tvar", [B, 1]), st.sb("trstd", [B, 1])
    pC, pD, pG = (st.ps(n, [P, 2, T]) for n in ("pC", "pD", "pG"))
    pS = st.ps("pS", [P, 512])
    pR = st.ps("pR", [P, 512])

    names = ("proj_w_in small_in agg_w_in mlp_w_in last_in c_ready d_ready g_ready sig_ready gate_ready "
             "proj_free sig_used scanned decay_ready setup_step dve_step t_turned t_copied h_ready h_biased h_act "
             "rows_done rstd_ready bc_ready bc_done out_step").split()
    s = {n: sem(n) for n in names}
    TSTEPS = 11

    with nc.Block() as block:
        @block.sync
        def _(sp):
            sp.dma_start(last_rows[:], core.xn[P - 1:P, 3::4, :]
                         ).then_inc(s["last_in"], 16)
            for w, n in ((w_c, "C_wT"), (w_d, "D_wT"), (w_g, "L0_ffn_gate_w")):
                sp.dma_start(w[:], in_chunks(dram[n])).then_inc(s["proj_w_in"], 16)
            for k, n in enumerate(("L0_attn_C_b", "L0_attn_D_b", "L0_ffn_gate_b", "L0_ffn_bc_b",
                                   "L0_attn_log_delta")):
                sp.dma_start(cols[:, k, :], in_chunks(dram[n]),
                             allow_slow_non_contiguous=True).then_inc(s["small_in"], 16)
            sp.dma_start(b1[:], in_chunks(dram["L0_ffn_d1_b"]),
                         allow_slow_non_contiguous=True).then_inc(s["small_in"], 16)
            for k, n in enumerate(("in_gamma", "in_beta", "agg_b", "pn_gamma", "pn_beta", "d2_b")):
                sp.dma_start(rows[:, k, :], on_all_partitions(dram["L0_ffn_" + n], B)).then_inc(s["small_in"], 16)
            for k, n in enumerate("AB"):
                sp.dma_start(ab[:, k, :, :], in_chunks(dram["L0_attn_" + n])).then_inc(s["small_in"], 16)
            for w, n in ((w_agg, "agg_w"), (w_bc, "bc_w")):
                sp.dma_start(w[:], in_chunks(dram["L0_ffn_" + n])).then_inc(s["agg_w_in"], 16)
            for w, n in ((w1, "d1_w"), (w2, "d2_w")):
                sp.dma_start(w[:], in_chunks(dram["L0_ffn_" + n])).then_inc(s["mlp_w_in"], 16)

        SMALL = 16 * 14

        @block.tensor
        def _(pe):
            def turn_rows(n):
                pe.wait_ge(s["dve_step"], (n + 1) * TSTEPS)
                for c in range(DC):
                    ins = pe.transpose(pS[:, B * c:B * c + B], tnorm[:, c * P:(c + 1) * P],
                                       core.ident[0:B, 0:B])
                ins.then_inc(s["t_turned"], 1)
                pe.wait_ge(s["t_copied"], n + 1)

            def add_rows(w, lhs, n_c):
                for c in range(n_c):
                    ins = pe.matmul(pR[0:B, 0:D], lhs[:, c, :], w[:, c, :], start=(c == 0), stop=(c == n_c - 1))
                ins.then_inc(s["rows_done"], 1)

            pe.wait_ge(s["agg_w_in"], 32)
            turn_rows(0)
            add_rows(w_agg, tT, DC)
            pe.wait_ge(s["proj_w_in"], 48)
            pe.wait_ge(s["mlp_w_in"], 32)
            with pe.Fori(0, B) as b:
                for o in range(DC):
                    pe.wait_ge(s["proj_free"], 2 * b + o + 1)
                    for ps, w, name in ((pD, w_d, "d_ready"), (pC, w_c, "c_ready"), (pG, w_g, "g_ready")):
                        for c in range(DC):
                            ins = pe.matmul(ps[:, o, :], w[:, c, o * P:(o + 1) * P],
                                            core.xnT[:, c, bass.ds(b * T, T)], start=(c == 0), stop=(c == DC - 1))
                        ins.then_inc(s[name], 1)
                pe.wait_ge(s["dve_step"], (b + 2) * TSTEPS)
                for c in range(DC):
                    ins = pe.matmul(pS[:, B * c:B * c + B], tnorm[:, c * P:(c + 1) * P],
                                    core.ident[0:B, 0:B], start=True, stop=True)
                ins.then_inc(s["t_turned"], 1)
                pe.wait_ge(s["t_copied"], b + 2)
                for h in range(HC):
                    for c in range(DC):
                        ins = pe.matmul(pS[:, 64 + B * h:64 + B * h + B], w1[:, c, h * P:(h + 1) * P], tT[:, c, :],
                                        start=(c == 0), stop=(c == DC - 1))
                ins.then_inc(s["h_ready"], 1)
                pe.wait_ge(s["h_act"], b + 1)
                add_rows(w2, hT, HC)
            pe.wait_ge(s["out_step"], 1 + 2 * KS)
            for c in range(DC):
                ins = pe.transpose(pS[:, B * c:B * c + B], thought[:, c * P:(c + 1) * P], core.ident[0:B, 0:B])
            ins.then_inc(s["t_turned"], 1)
            pe.wait_ge(s["t_copied"], KS + 2)
            for o in range(DC):
                for c in range(DC):
                    ins = pe.matmul(pR[:, 256 + B * o:256 + B * o + B], w_bc[:, c, o * P:(o + 1) * P], tT[:, c, :],
                                    start=(c == 0), stop=(c == DC - 1))
            ins.then_inc(s["bc_ready"], 1)

        @block.scalar
        def _(act):
            act.wait_ge(s["small_in"], SMALL)
            act.activation(decay_col[:], cols[:, 4, :], ACT.Sigmoid, scale=-1.0).then_inc(s["decay_ready"], 1)
            act.sem_inc(s["sig_used"], 2)
            with act.Fori(0, B) as b:
                for o in range(DC):
                    act.wait_ge(s["d_ready"], 2 * b + o + 1)
                    act.wait_ge(s["sig_used"], 2 * b + o + 3)
                    act.activation(sig[:, o, :], pD[:, o, :], ACT.Sigmoid,
                                   bias=cols[:, 1, o:o + 1]).then_inc(s["sig_ready"], 1)
                    act.wait_ge(s["g_ready"], 2 * b + o + 1)
                    act.activation(gateT[:, o, bass.ds(b * T, T)], pG[:, o, :], ACT.Sigmoid,
                                   bias=cols[:, 2, o:o + 1]).then_inc(s["gate_ready"], 1)
                act.wait_ge(s["h_biased"], b + 1)
                act.activation(hT[:], hT[:], ACT.Gelu).then_inc(s["h_act"], 1)

        @block.gpsimd
        def _(pool):
            for n in range(KS + 1):
                pool.wait_ge(s["dve_step"], n * TSTEPS + 8)
                pool.tensor_tensor(rstd[:], var[:], core.consts[0:B, C_HALF:C_HALF + 1],
                                   ALU.pow).then_inc(s["rstd_ready"], 1)

        @block.vector
        def _(dve):
            dve.sem_inc(s["proj_free"], 2)
            dve.sem_inc(s["sig_used"], 2)
            dve.wait_ge(s["small_in"], SMALL)
            setup_do = Steps(dve, s["setup_step"])
            setup_do(dve.tensor_tensor(ab[:, 0, :, :], ab[:, 0, :, :], ab[:, 1, :, :], ALU.mult))
            setup_do(dve.reduce_sum(ab_sum[:], ab[:, 0, :, :], AX.X))
            setup_do(dve.memset(decay[:], 1.0))
            dve.wait_ge(s["decay_ready"], 1)
            for c in range(DC):
                setup_do(dve.tensor_scalar(decay[:, c, :], decay[:, c, :], decay_col[:, c:c + 1], None, ALU.mult))

            def thought_norm(src, n, gamma, beta, after_stats=None):
                do = Steps(dve, s["dve_step"], n * TSTEPS, TSTEPS)
                do(dve.bn_stats(raw[:], src))
                do(dve.tensor_tensor(mean[:], raw[:, 1:2], raw[:, 4:5], ALU.add))
                do(dve.tensor_tensor(var[:], raw[:, 1:2], raw[:, 4:5], ALU.subtract))
                do(dve.tensor_tensor(var[:], var[:], var[:], ALU.mult))
                do(dve.scalar_tensor_tensor(out=var[:], in0=raw[:, 2:3], scalar=4.0 / D, in1=var[:],
                                            op0=ALU.mult, op1=ALU.add))
                do(dve.scalar_tensor_tensor(out=var[:], in0=raw[:, 5:6], scalar=4.0 / D, in1=var[:],
                                            op0=ALU.mult, op1=ALU.add))
                do(dve.tensor_scalar(mean[:], mean[:], 0.5, None, ALU.mult))
                do(dve.tensor_scalar(var[:], var[:], 0.25, 1e-6, ALU.mult, ALU.add))
                dve.wait_ge(s["rstd_ready"], n + 1)
                do(dve.tensor_scalar(tnorm[:], src, mean[:, 0:1], rstd[:, 0:1], ALU.subtract, ALU.mult))
                do(dve.tensor_tensor(tnorm[:], tnorm[:], rows[:, gamma, :], ALU.mult))
                do(dve.tensor_tensor(tnorm[:], tnorm[:], rows[:, beta, :], ALU.add))
                do.close()

            dve.wait_ge(s["last_in"], 16)
            thought_norm(last_rows[:], 0, 0, 1)
            dve.wait_ge(s["t_turned"], 1)
            dve.tensor_copy(tT[:], pS[:, 0:DC * B].rearrange("p (c b) -> p c b", b=B)).then_inc(s["t_copied"], 1)
            dve.wait_ge(s["rows_done"], 1)
            out_do = Steps(dve, s["out_step"], 0, 1)
            out_do(dve.tensor_tensor(thought[:], pR[0:B, 0:D], rows[:, 2, :], ALU.add))
            with dve.Fori(0, B) as b:
                thought_norm(thought[:], b + 1, 3, 4)
                for o in range(DC):
                    dve.wait_ge(s["c_ready"], 2 * b + o + 1)
                    dve.wait_ge(s["sig_ready"], 2 * b + o + 1)
                    dve.scalar_tensor_tensor(out=drive[:, o, :], in0=pC[:, o, :], scalar=cols[:, 0, o:o + 1],
                                             in1=sig[:, o, :], op0=ALU.add, op1=ALU.mult).then_inc(s["sig_used"], 1)
                    dve.wait_ge(s["sig_used"], 2 * b + o + 5)
                    dve.wait_ge(s["gate_ready"], 2 * b + o + 1)
                    dve.tensor_tensor_scan(gsT[:, o, bass.ds(b * T, T)], decay[:, o, :], drive[:, o, :], 0.0,
                                           ALU.mult, ALU.add).then_inc(s["proj_free"], 1)
                dve.wait_ge(s["t_turned"], b + 2)
                dve.tensor_copy(tT[:], pS[:, 0:DC * B].rearrange("p (c b) -> p c b", b=B)).then_inc(s["t_copied"], 1)
                dve.wait_ge(s["h_ready"], b + 1)
                dve.tensor_tensor(hT[:], pS[:, 64:64 + HC * B].rearrange("p (h b) -> p h b", b=B),
                                  b1[:].unsqueeze(2).to_broadcast([P, HC, B]), ALU.add).then_inc(s["h_biased"], 1)
                dve.wait_ge(s["rows_done"], b + 2)
                out_b = Steps(dve, s["out_step"], 1 + 2 * b, 2)
                out_b(dve.tensor_tensor(thought[:], pR[0:B, 0:D], thought[:], ALU.add))
                out_b(dve.tensor_tensor(thought[:], thought[:], rows[:, 5, :], ALU.add))
                out_b.close()
            dve.wait_ge(s["t_turned"], KS + 2)
            dve.tensor_copy(tT[:], pS[:, 0:DC * B].rearrange("p (c b) -> p c b", b=B)).then_inc(s["t_copied"], 1)
            dve.wait_ge(s["bc_ready"], 1)
            dve.tensor_tensor(core.bcT[:], pR[:, 256:256 + DC * B].rearrange("p (c b) -> p c b", b=B),
                              cols[:, 3, :].unsqueeze(2).to_broadcast([P, DC, B]), ALU.add
                              ).then_inc(s["bc_done"], 1)
            dve.wait_ge(s["bc_done"], 1)
            for c in range(DC):
                for b in range(B):
                    dve.scalar_tensor_tensor(out=gateT[:, c, b * T:(b + 1) * T], in0=gateT[:, c, b * T:(b + 1) * T],
                                             scalar=core.bcT[:, c, b:b + 1], in1=core.xnT[:, c, b * T:(b + 1) * T],
                                             op0=ALU.mult, op1=ALU.add)


def layer0_join(nc, st, core, dram, gsT, ffT):
    sem = st.sem
    y = core.xn
    slot = st.sb("slot", [P, 2, 2 * DC, P])
    gb = st.sb("gb", [P, 2, D])
    raw = st.sb("raw", [P, TILES, 6])
    mean, var, rstd = (st.sb(n, [P, TILES]) for n in ("mean", "var", "rstd"))
    back = st.ps("back", [P, 2, 512])
    gb_in, slot_ready, slot_free, turned = (sem(n) for n in ("gb_in", "slot_ready", "slot_free", "turned"))
    dve_step, rstd_ready = sem("dve_step"), sem("rstd_ready")
    scaled, gained, shifted = (sem(n) for n in ("scaled", "gained", "shifted"))
    with nc.Block() as block:
        @block.sync
        def _(sp):
            for k, n in enumerate(("L0_ffn_out_gamma", "L0_ffn_out_beta")):
                sp.dma_start(gb[:, k, :], on_all_partitions(dram[n], P)).then_inc(gb_in, 16)

        @block.gpsimd
        def _(pool):
            with pool.Fori(0, GROUPS) as g:
                for p in range(2):
                    pool.wait_ge(slot_free, 2 * g + p + 1)
                    for c in range(DC):
                        pool.tensor_tensor(slot[:, p, c, :], col_group(gsT, g, p)[:, c, :],
                                           core.ab_sum[:, c:c + 1].to_broadcast([P, P]), ALU.mult)
                    pool.tensor_copy(slot[:, p, DC:2 * DC, :], col_group(ffT, g, p)).then_inc(slot_ready, 1)
            pool.wait_ge(dve_step, 7)
            pool.tensor_tensor(rstd[:], var[:], core.consts[:, C_HALF:C_HALF + TILES],
                               ALU.pow).then_inc(rstd_ready, 1)

        @block.tensor
        def _(pe):
            with pe.Fori(0, GROUPS) as g:
                for p in range(2):
                    pe.wait_ge(slot_ready, 2 * g + p + 1)
                    for k in range(2 * DC):
                        ins = pe.transpose(back[:, p, k * P:(k + 1) * P], slot[:, p, k, :], core.ident)
                    ins.then_inc(turned, 1)

        @block.vector
        def _(dve):
            dve.sem_inc(slot_free, 2)
            with dve.Fori(0, GROUPS) as g:
                for p in range(2):
                    t = 2 * g + p
                    dve.wait_ge(turned, t + 1)
                    dve.tensor_tensor(core.x[:, t, :], back[:, p, 0:D], core.x[:, t, :], ALU.add)
                    dve.bn_stats(raw[:, t, :], back[:, p, D:2 * D])
                    dve.tensor_copy(y[:, t, :], back[:, p, D:2 * D]).then_inc(slot_free, 1)
            dve.wait_ge(slot_free, TILES + 2)
            do = Steps(dve, dve_step)
            small_stats(do, dve, raw, mean, var, 1e-6, False)
            dve.wait_ge(rstd_ready, 1)
            dve.wait_ge(gb_in, 32)
            with dve.Fori(0, GROUPS) as g:
                for p in range(2):
                    t = 2 * g + p
                    dve.tensor_scalar(y[:, t, :], y[:, t, :], mean[:, bass.ds(t, 1)], rstd[:, bass.ds(t, 1)],
                                      ALU.subtract, ALU.mult).then_inc(scaled, 1)
                pair = y[:, bass.ds(2 * g, 2), :]
                dve.wait_ge(scaled, 2 * g + 2)
                dve.tensor_tensor(pair, pair, gb[:, 0, :].unsqueeze(1).to_broadcast([P, 2, D]),
                                  ALU.mult).then_inc(gained, 1)
                dve.wait_ge(gained, g + 1)
                dve.tensor_tensor(pair, pair, gb[:, 1, :].unsqueeze(1).to_broadcast([P, 2, D]),
                                  ALU.add).then_inc(shifted, 1)
                dve.wait_ge(shifted, g + 1)
                dve.tensor_tensor(core.x[:, bass.ds(2 * g, 2), :], pair, core.x[:, bass.ds(2 * g, 2), :], ALU.add)


def layer1_attention(nc, st, core):
    sem = st.sem
    HD, H2 = 16, 8
    keys = st.sb("keys", [P, 2, DC, P])
    vals = st.sb("vals", [P, 2, H2, HD + 1])
    e = st.sb("e", [P, 2, H2, P])
    inv, part = st.sb("inv", [P, 2, H2]), st.sb("part", [P, 2, H2, HD])
    ps = st.ps("scores", [P, 4, 2, DC, P])
    po = st.ps("out", [P, 2, 512])
    ones, keys_ready, vals_ready, scores_ready = (sem(n) for n in ("ones", "keys_ready", "vals_ready", "scores_ready"))
    exp_ready, masked, out_ready, inv_ready, scaled, tile_done = (sem(n) for n in (
        "exp_ready", "masked", "out_ready", "inv_ready", "scaled", "tile_done"))
    heads = [(c, j) for c in range(DC) for j in range(4)]

    def own(t, p):
        return t.rearrange("q (h two d) -> q h two d", two=2, d=HD)[:, :, p, :]

    with nc.Block() as block:
        @block.gpsimd
        def _(pool):
            pool.memset(vals[:], 1.0).then_inc(ones, 1)
            pool.wait_ge(ones, 1)
            with pool.Fori(0, GROUPS) as g:
                for p in range(2):
                    pool.wait_ge(tile_done, 2 * g + p + 1)
                    pool.tensor_tensor(keys[:, p, :, :], col_group(core.xnT, g, p),
                                       core.consts[:, C_EVEN + p:C_EVEN + p + 1].unsqueeze(2).to_broadcast([P, DC, P]),
                                       ALU.mult).then_inc(keys_ready, 1)
                    pool.tensor_copy(vals[:, p, :, 0:HD],
                                     own(core.xn[:, bass.ds(2 * g + p, 1), :].rearrange("q t d -> q (t d)"), p)
                                     ).then_inc(vals_ready, 1)

        @block.tensor
        def _(pe):
            with pe.Fori(0, GROUPS) as g:
                for p in range(2):
                    n = 2 * g + p
                    pe.wait_ge(keys_ready, n + 1)
                    for h, (c, j) in enumerate(heads):
                        rows = keys[32 * j:32 * j + 32, p, c, :]
                        ins = pe.matmul(ps[:, j, p, c, :], rows, rows, start=True, stop=True)
                    ins.then_inc(scores_ready, 1)
                    pe.wait_ge(masked, n + 1)
                    pe.wait_ge(vals_ready, n + 1)
                    for h in range(H2):
                        ins = pe.matmul(po[:, p, h * (HD + 1):(h + 1) * (HD + 1)], e[:, p, h, :], vals[:, p, h, :],
                                        start=True, stop=True)
                    ins.then_inc(out_ready, 1)

        @block.scalar
        def _(act):
            act.preload_act_table(ACT.Exp)
            with act.Fori(0, GROUPS) as g:
                for p in range(2):
                    act.wait_ge(scores_ready, 2 * g + p + 1)
                    act.activation(e[:, p, :, :].rearrange("q (c j) k -> q j c k", c=DC), ps[:, :, p, :, :], ACT.Exp,
                                   scale=HD ** -0.5).then_inc(exp_ready, 1)

        @block.vector
        def _(dve):
            dve.sem_inc(tile_done, 2)
            with dve.Fori(0, GROUPS) as g:
                for p in range(2):
                    n = 2 * g + p
                    dve.wait_ge(exp_ready, n + 1)
                    dve.tensor_tensor(e[:, p, :, :], e[:, p, :, :], core.blk.unsqueeze(1).to_broadcast([P, H2, P]),
                                      ALU.mult).then_inc(masked, 1)
                    dve.wait_ge(out_ready, n + 1)
                    o = po[:, p, 0:H2 * (HD + 1)].rearrange("q (h d) -> q h d", h=H2)
                    dve.reciprocal(inv[:, p, :], o[:, :, HD]).then_inc(inv_ready, 1)
                    dve.wait_ge(inv_ready, n + 1)
                    dve.tensor_tensor(part[:, p, :, :], o[:, :, 0:HD],
                                      inv[:, p, :].unsqueeze(2).to_broadcast([P, H2, HD]), ALU.mult
                                      ).then_inc(scaled, 1)
                    dve.wait_ge(scaled, n + 1)
                    x = own(core.x[:, bass.ds(n, 1), :].rearrange("q t d -> q (t d)"), p)
                    dve.tensor_tensor(x, x, part[:, p, :, :], ALU.add).then_inc(tile_done, 1)


def layer2_abc(nc, st, core, dram):
    sem = st.sem
    HP, DK, DV, NCH = 8, 64, 128, TB
    PV = 2 * DV
    here, ones = st.sb("here", [P, DC, T]), st.sb("ones", [P, T])
    w_qks, w_vg, w_o = st.sb("w_qks", [P, 2, 3, DC, P]), st.sb("w_vg", [P, 2, 2, DC, PV]), st.sb("w_o", [P, 2, 2, D])
    gnorm = st.sb("gnorm", [P, 1])
    qT, kT, sT, eT, cT, rT = (st.sb(n, [P, T]) for n in ("qT", "kT", "sT", "eT", "cT", "rT"))
    k_tok, e_tok, r_tok = (st.sb(n, [P, NCH, P]) for n in ("k_tok", "e_tok", "r_tok"))
    v, th, gate = (st.sb(n, [P, NCH, PV]) for n in ("v", "th", "gate"))
    sm, am = st.sb("sm", [P, 2, NCH, P]), st.sb("am", [P, 2, NCH, P])
    hk, hv = st.sb("hk", [P, 3, P]), st.sb("hv", [P, 3, DV])
    lg, ex, wt = (st.sb(n, [P, NCH, P]) for n in ("lg", "ex", "wt"))
    wT = st.sb("wT", [P, T])
    mx, den = st.sb("mx", [P, 8]), st.sb("den", [P, 8])
    sq, on, gr = st.sb("sq", [P, 2, NCH, DV]), st.sb("on", [P, 2, NCH, DV]), st.sb("gr", [P, 2, NCH, DV])
    ms, rstd = st.sb("ms", [P, 8]), st.sb("rstd", [P, 8])
    oT = st.sb("oT", [P, 2, T])
    pa, pt = st.ps("pa", [P, 3, T]), st.ps("pt", [P, T])
    pv, pg = st.ps("pv", [P, 2, T]), st.ps("pg", [P, 2, T])
    names = ("once_in here_ready q_ready k_ready s_ready v_ready g_ready q_copied k_copied s_clipped e_ready "
             "c_ready r_ready v_copied tanh_ready gate_ready k_turned e_turned r_turned k_tok_ready e_tok_ready "
             "r_tok_ready scores_ready sm_ready hk_sums hk_step ok_ready hv_sums hv_step zeros logit_step ex_ready "
             "er_ready den_step wt_ready w_turned wT_ready am_sums am_ready ov_ready sq_ready ms_step rstd_ready "
             "gr_ready on_ready o_turned oT_ready y_ready y_added pe_waited").split()
    s = {n: sem(n) for n in names}
    w_in = [sem("w0_in"), sem("w1_in")]
    tok4 = pt[:].rearrange("t (c m) -> t c m", c=NCH)
    pst = pv[:].rearrange("j h (c t) -> j h c t", c=NCH)
    pov = pg[:].rearrange("t h (c v) -> t h c v", c=NCH)
    pvv = pv[:].rearrange("t b (c v) -> t (b c) v", v=PV)
    pgg = pg[:].rearrange("t b (c v) -> t (b c) v", v=PV)
    poT = pa[:, 0:2, :]
    heads8 = lambda a: a.rearrange("t c (h m) -> t (c h) m", h=2)

    def load(sp, slot, hp):
        for k, n in enumerate(("Wq", "Wk", "Ws")):
            sp.dma_start(w_qks[:, slot, k, :, :], in_chunks(dram["L2_attn_" + n])[:, :, bass.ds(hp * P, P)]
                         ).then_inc(w_in[slot], 16)
        for k, n in enumerate(("Wv", "Wg")):
            sp.dma_start(w_vg[:, slot, k, :, :], in_chunks(dram["L2_attn_" + n])[:, :, bass.ds(hp * PV, PV)]
                         ).then_inc(w_in[slot], 16)
        sp.dma_start(w_o[:, slot, :, :], in_chunks(dram["L2_attn_Wo"])[:, bass.ds(hp * 2, 2), :]
                     ).then_inc(w_in[slot], 16)

    def units(eng, unit, before=None):
        with eng.Fori(0, HP // 2) as i:
            for slot in range(2):
                if before is not None:
                    before(i, slot)
                with eng.Fori(0, B) as b:
                    unit(i * (2 * B) + slot * B + b, b, slot)

    with nc.Block() as block:
        @block.sync
        def _(sp):
            sp.dma_start(gnorm[:], dram["L2_attn_g_norm_weight"].unsqueeze(1),
                         allow_slow_non_contiguous=True).then_inc(s["once_in"], 16)
            for slot in range(2):
                load(sp, slot, slot)
            with sp.Fori(1, HP // 2) as i:
                for slot in range(2):
                    sp.wait_ge(s["y_added"], (i - 1) * (2 * B) + (slot + 1) * B + 1)
                    load(sp, slot, i * 2 + slot)

        @block.gpsimd
        def _(pool):
            pool.memset(ones[:], 1.0).then_inc(s["zeros"], 1)
            pool.memset(hk[:], 0.0).then_inc(s["zeros"], 1)
            pool.sem_inc(s["g_ready"], 1)

            def unit(u, b, slot):
                pool.wait_ge(s["g_ready"], u + 1)
                pool.tensor_copy(here[:], core.xnT[:, :, bass.ds(b * T, T)]).then_inc(s["here_ready"], 1)
                pool.wait_ge(s["ex_ready"], u + 1)
                pool.wait_ge(s["r_tok_ready"], u + 1)
                pool.tensor_tensor(wt[:], ex[:], r_tok[:], ALU.mult).then_inc(s["er_ready"], 1)
                pool.wait_ge(s["ms_step"], 2 * (u + 1))
                pool.tensor_tensor(rstd[:], ms[:], core.consts[:, C_HALF:C_HALF + 8], ALU.pow
                                   ).then_inc(s["rstd_ready"], 1)
                pool.wait_ge(s["rstd_ready"], u + 1)
                pool.wait_ge(s["gate_ready"], u + 1)
                pool.tensor_tensor(gr[:].rearrange("t h c v -> t c h v"),
                                   gate[:].rearrange("t c (h v) -> t c h v", h=2),
                                   rstd[:].rearrange("t (h c) -> t c h", h=2).unsqueeze(3).to_broadcast(
                                       [P, NCH, 2, DV]), ALU.mult).then_inc(s["gr_ready"], 1)

            units(pool, unit)

        @block.tensor
        def _(pe):
            pe.wait_ge(s["zeros"], 2)

            def before(i, slot):
                wait_apart(pe, w_in[slot], 96 * (i + 1), s["pe_waited"])

            def unit(u, b, slot):
                pe.wait_ge(s["here_ready"], u + 1)
                for k, n in enumerate(("q_ready", "k_ready", "s_ready")):
                    for c in range(DC):
                        ins = pe.matmul(pa[:, k, :], w_qks[:, slot, k, c, :], here[:, c, :],
                                        start=(c == 0), stop=(c == DC - 1))
                    ins.then_inc(s[n], 1)
                pe.wait_ge(s["y_added"], u + 1)
                for k, (ps, n) in enumerate(((pvv, "v_ready"), (pgg, "g_ready"))):
                    for t in range(NCH):
                        for c in range(DC):
                            ins = pe.matmul(ps[:, t, :], here[:, c, t * P:(t + 1) * P], w_vg[:, slot, k, c, :],
                                            start=(c == 0), stop=(c == DC - 1))
                    ins.then_inc(s[n], 1)
                pe.wait_ge(s["k_copied"], u + 1)
                for t in range(NCH):
                    ins = pe.transpose(pt[:, t * P:(t + 1) * P], kT[:, t * P:(t + 1) * P], core.ident)
                ins.then_inc(s["k_turned"], 1)
                pe.wait_ge(s["q_copied"], u + 1)
                pe.wait_ge(s["e_ready"], u + 1)
                for t in range(NCH):
                    ins = pe.transpose(pa[:, 0, t * P:(t + 1) * P], eT[:, t * P:(t + 1) * P], core.ident)
                ins.then_inc(s["e_turned"], 1)
                pe.wait_ge(s["v_copied"], u + 1)
                for c in range(NCH):
                    for h in range(2):
                        rows, cols = slice(DK * h, DK * h + DK), slice(c * P, (c + 1) * P)
                        ins = pe.matmul(pst[:, h, c, :], kT[rows, cols], qT[rows, cols], start=True, stop=True)
                ins.then_inc(s["scores_ready"], 1)
                pe.wait_ge(s["s_clipped"], u + 1)
                pe.wait_ge(s["k_tok_ready"], u + 1)
                pe.wait_ge(s["e_tok_ready"], u + 1)
                for c in range(3):
                    ins = pe.matmul(pa[:, 2, c * P:(c + 1) * P], k_tok[:, c, :], e_tok[:, c, :], start=True, stop=True)
                ins.then_inc(s["hk_sums"], 1)
                for c in range(3):
                    for h in range(2):
                        ins = pe.matmul(pa[DK * h:DK * h + DK, 0, c * DV:(c + 1) * DV],
                                        e_tok[:, c, DK * h:DK * h + DK], v[:, c, DV * h:DV * h + DV],
                                        start=True, stop=True)
                ins.then_inc(s["hv_sums"], 1)
                pe.wait_ge(s["r_ready"], u + 1)
                for t in range(NCH):
                    ins = pe.transpose(pa[:, 1, t * P:(t + 1) * P], rT[:, t * P:(t + 1) * P], core.ident)
                ins.then_inc(s["r_turned"], 1)
                pe.wait_ge(s["sm_ready"], u + 1)
                pe.wait_ge(s["hk_step"], 6 * (u + 1))
                for c in range(NCH):
                    if c:
                        pe.matmul(tok4[:, c, :], qT[:, c * P:(c + 1) * P], hk[:, c - 1, :], start=True, stop=False,
                                  skip_group_check=True)
                    for h in range(2):
                        m = slice(DK * h, DK * h + DK)
                        ins = pe.matmul(tok4[:, c, m], sm[:, h, c, :], e_tok[:, c, m], start=(c == 0), stop=True,
                                        skip_group_check=True)
                ins.then_inc(s["ok_ready"], 1)
                pe.wait_ge(s["wt_ready"], u + 1)
                pe.wait_ge(s["r_tok_ready"], u + 1)
                for t in range(NCH):
                    ins = pe.transpose(pa[:, 1, t * P:(t + 1) * P], wt[:, t, :], core.ident)
                ins.then_inc(s["w_turned"], 1)
                pe.wait_ge(s["wT_ready"], u + 1)
                for c in range(NCH):
                    for h in range(2):
                        rows, cols = slice(DK * h, DK * h + DK), slice(c * P, (c + 1) * P)
                        ins = pe.matmul(pst[:, h, c, :], eT[rows, cols], wT[rows, cols], start=True, stop=True)
                ins.then_inc(s["am_sums"], 1)
                pe.wait_ge(s["gate_ready"], u + 1)
                pe.wait_ge(s["hv_step"], 3 * (u + 1))
                pe.wait_ge(s["am_ready"], u + 1)
                for c in range(NCH):
                    for h in range(2):
                        rows = slice(DK * h, DK * h + DK)
                        if c:
                            pe.matmul(pov[:, h, c, :], wT[rows, c * P:(c + 1) * P], hv[rows, c - 1, :],
                                      start=True, stop=False)
                        ins = pe.matmul(pov[:, h, c, :], am[:, h, c, :], v[:, c, DV * h:DV * h + DV],
                                        start=(c == 0), stop=True)
                ins.then_inc(s["ov_ready"], 1)
                pe.wait_ge(s["on_ready"], u + 1)
                for h in range(2):
                    for c in range(NCH):
                        ins = pe.transpose(poT[:, h, c * P:(c + 1) * P], on[:, h, c, :], core.ident)
                ins.then_inc(s["o_turned"], 1)
                pe.wait_ge(s["oT_ready"], u + 1)
                for t in range(NCH):
                    for h in range(2):
                        cols = oT[:, h, :].rearrange("d (g q p) -> d g p q", q=P, p=2)[:, t // 2, t % 2, :]
                        ins = pe.matmul(pvv[:, t, :], cols, w_o[:, slot, h, :], start=(h == 0), stop=(h == 1))
                ins.then_inc(s["y_ready"], 1)

            units(pe, unit, before)

        @block.scalar
        def _(act):
            act.preload_act_table(ACT.Exp)
            act.wait_ge(s["once_in"], 16)

            def unit(u, b, slot):
                def copy(ready, out, in_, done, **kw):
                    act.wait_ge(s[ready], u + 1)
                    act.activation(out, in_, ACT.Copy, **kw).then_inc(s[done], 1)

                copy("q_ready", qT[:], pa[:, 0, :], "q_copied", scale=DK ** -0.5)
                act.wait_ge(s["s_clipped"], u + 1)
                act.activation(eT[:], sT[:], ACT.Exp).then_inc(s["e_ready"], 1)
                copy("v_ready", v[:], pvv, "v_copied")
                copy("k_turned", k_tok[:], tok4, "k_tok_ready")
                copy("e_turned", e_tok[:], pa[:, 0, :].rearrange("t (c m) -> t c m", c=NCH), "e_tok_ready")
                act.wait_ge(s["g_ready"], u + 2)
                act.activation(th[:], pgg, ACT.Tanh, scale=0.5).then_inc(s["tanh_ready"], 1)
                copy("r_turned", r_tok[:], pa[:, 1, :].rearrange("t (c m) -> t c m", c=NCH), "r_tok_ready")
                act.wait_ge(s["logit_step"], 3 * (u + 1))
                act.activation(ex[:], lg[:], ACT.Exp).then_inc(s["ex_ready"], 1)
                copy("w_turned", wT[:], pa[:, 1, :], "wT_ready")
                act.wait_ge(s["ov_ready"], u + 1)
                act.activation(sq[:], pov, ACT.Square).then_inc(s["sq_ready"], 1)
                act.wait_ge(s["o_turned"], u + 1)
                act.activation(oT[:], poT, ACT.Copy, scale=gnorm[:, 0:1]).then_inc(s["oT_ready"], 1)

            units(act, unit)

        @block.vector
        def _(dve):
            dve.sem_inc(s["y_added"], 1)
            dve.wait_ge(s["zeros"], 2)

            def unit(u, b, slot):
                tri8 = core.tri.unsqueeze(1).to_broadcast([P, NCH, P])
                dve.wait_ge(s["k_ready"], u + 1)
                dve.tensor_copy(kT[:], pa[:, 1, :]).then_inc(s["k_copied"], 1)
                dve.wait_ge(s["s_ready"], u + 1)
                dve.tensor_scalar(sT[:], pa[:, 2, :], 32.0, -32.0, ALU.min, ALU.max).then_inc(s["s_clipped"], 1)
                dve.wait_ge(s["e_ready"], u + 1)
                dve.tensor_tensor_scan(cT[:], ones[:], eT[:], 0.0, ALU.mult, ALU.add).then_inc(s["c_ready"], 1)
                dve.wait_ge(s["c_ready"], u + 1)
                dve.reciprocal(rT[:], cT[:]).then_inc(s["r_ready"], 1)
                dve.wait_ge(s["scores_ready"], u + 1)
                for h in range(2):
                    ins = dve.tensor_tensor(sm[:, h, :, :], pst[:, h, :, :], tri8, ALU.mult)
                ins.then_inc(s["sm_ready"], 1)
                dve.wait_ge(s["hk_sums"], u + 1)
                do = Steps(dve, s["hk_step"], 6 * u, 6)
                for c in range(3):
                    for h in range(2):
                        r, m = slice(DK * h, DK * h + DK), slice(DK * h, DK * h + DK)
                        new = pa[r, 2, c * P + DK * h:c * P + DK * h + DK]
                        if c:
                            do(dve.tensor_tensor(hk[r, c, m], new, hk[r, c - 1, m], ALU.add))
                        else:
                            do(dve.tensor_copy(hk[r, c, m], new))
                do.close()
                dve.wait_ge(s["hv_sums"], u + 1)
                do = Steps(dve, s["hv_step"], 3 * u, 3)
                for c in range(3):
                    new = pa[:, 0, c * DV:(c + 1) * DV]
                    if c:
                        do(dve.tensor_tensor(hv[:, c, :], new, hv[:, c - 1, :], ALU.add))
                    else:
                        do(dve.tensor_copy(hv[:, c, :], new))
                do.close()
                dve.wait_ge(s["tanh_ready"], u + 1)
                dve.scalar_tensor_tensor(out=gate[:], in0=th[:], scalar=1.0, in1=pgg, op0=ALU.add, op1=ALU.mult
                                         ).then_inc(s["gate_ready"], 1)
                dve.wait_ge(s["ok_ready"], u + 1)
                dve.wait_ge(s["r_tok_ready"], u + 1)
                do = Steps(dve, s["logit_step"], 3 * u, 3)
                do(dve.tensor_tensor(lg[:], tok4, r_tok[:], ALU.mult))
                do(dve.tensor_reduce(mx[:], heads8(lg[:]), AX.X, ALU.max))
                do(dve.tensor_tensor(heads8(lg[:]), heads8(lg[:]), mx[:].unsqueeze(2).to_broadcast([P, 8, DK]),
                                     ALU.subtract))
                do.close()
                dve.wait_ge(s["ex_ready"], u + 1)
                do = Steps(dve, s["den_step"], 2 * u, 2)
                do(dve.reduce_sum(den[:], heads8(ex[:]), AX.X))
                do(dve.reciprocal(den[:], den[:]))
                do.close()
                dve.wait_ge(s["er_ready"], u + 1)
                dve.tensor_tensor(heads8(wt[:]), heads8(wt[:]), den[:].unsqueeze(2).to_broadcast([P, 8, DK]),
                                  ALU.mult).then_inc(s["wt_ready"], 1)
                dve.wait_ge(s["am_sums"], u + 1)
                for h in range(2):
                    ins = dve.tensor_tensor(am[:, h, :, :], pst[:, h, :, :], tri8, ALU.mult)
                ins.then_inc(s["am_ready"], 1)
                dve.wait_ge(s["sq_ready"], u + 1)
                do = Steps(dve, s["ms_step"], 2 * u, 2)
                do(dve.reduce_sum(ms[:], sq[:].rearrange("t h c v -> t (h c) v"), AX.X))
                do(dve.tensor_scalar(ms[:], ms[:], 4.0 / DV, 4e-5, ALU.mult, ALU.add))
                do.close()
                dve.wait_ge(s["gr_ready"], u + 1)
                dve.tensor_tensor(on[:], pov, gr[:], ALU.mult).then_inc(s["on_ready"], 1)
                dve.wait_ge(s["y_ready"], u + 1)
                x = core.x[:, bass.ds(4 * b, 4), :]
                dve.tensor_tensor(x, pvv, x, ALU.add).then_inc(s["y_added"], 1)

            units(dve, unit)


def layer2_attention(nc, st, core, dram, aT):
    sem = st.sem
    H, LAT = 16, 64
    w_kvq = st.sb("w_kvq", [P, DC, P])
    w_low = st.sb("w_low", [P, 2, D])
    w_kr, w_kt = st.sb("w_kr", [P, DC, D]), st.sb("w_kt", [P, DC, D])
    w_o = st.sb("w_o", [P, DC, D])
    rope = st.sb("rope", [P, 2, T])
    low = st.sb("low", [P, T])
    turn = st.sb("turn", [P, 2, T])
    qT, kT = st.sb("qT", [P, DC, T]), st.sb("kT", [P, DC, T])
    keys = st.sb("keys", [P, 2, DC, T])
    v = st.sb("v", [P, TB, D])
    pr, prT = st.sb("pr", [P, 2, TB, T]), st.sb("prT", [P, 2, TB, T])
    nmax = st.sb("nmax", [P, 2, TB])
    total = st.sb("total", [P, H, TB])
    o, oT = st.sb("o", [P, TB, D]), st.sb("oT", [P, DC, T])
    pa, pw, po = st.ps("pa", [P, 4, T]), st.ps("pw", [P, 2, T]), st.ps("po", [P, TB, D])
    (w_in, low_ready, low_copied, rot_ready, rot_step, rot_done, keys_ready, v_ready, v_copied, scores_ready,
     score_masked, max_ready, exp_ready, turned, turned_copied, heads_out, norm_step, o_turned, o_copied, y_ready,
     y_added, joined) = (
        sem(n) for n in ("w_in low_ready low_copied rot_ready rot_step rot_done keys_ready v_ready v_copied "
                         "scores_ready score_masked max_ready exp_ready turned turned_copied heads_out norm_step "
                         "o_turned o_copied y_ready y_added joined").split())
    loads = [(w_kvq[:], in_chunks(dram["L2_kvq_d"])), (w_low[0:LAT, 0, :], dram["L2_k_plain"]),
             (w_low[0:LAT, 1, :], dram["L2_ffn_v_u_w"]), (w_low[LAT:P, 0, :], dram["L2_q_both"]),
             (w_low[LAT:P, 1, :], dram["L2_q_turned"]), (w_kr[:], in_chunks(dram["L2_k_rope"])),
             (w_kt[:], in_chunks(dram["L2_k_turned"])), (w_o[:], in_chunks(dram["L2_ffn_o_w"])),
             (rope[:], dram["rope"].rearrange("k p t -> p k t"))]
    py = po
    with nc.Block() as block:
        @block.sync
        def _(sp):
            for dst, src in loads:
                sp.dma_start(dst, src).then_inc(w_in, 16)

        @block.tensor
        def _(pe):
            pe.wait_ge(w_in, 16 * len(loads))

            def scores(b, h, k):
                q = QB_ORDER[k]
                c, j, other = h // 8, (h % 8) // 2, h % 2
                rows = slice(32 * j, 32 * j + 32)
                n = (q + 1) * P
                if h:
                    pe.wait_ge(exp_ready, TB * H * b + TB * (h - 1) + k + 1)
                pe.matmul(pa[:, q, 0:n], qT[rows, c, q * P:(q + 1) * P], keys[rows, other, c, 0:n],
                          start=True, stop=True).then_inc(scores_ready, 1)

            with pe.Fori(0, B) as b:
                x = [aT[:, c, bass.ds(b * T, T)] for c in range(DC)]
                for c in range(DC):
                    ins = pe.matmul(pw[:, 0, :], w_kvq[:, c, :], x[c], start=(c == 0), stop=(c == DC - 1))
                ins.then_inc(low_ready, 1)
                pe.wait_ge(low_copied, b + 1)
                for o_ in range(DC):
                    cols = slice(o_ * P, (o_ + 1) * P)
                    pe.matmul(pa[:, 2 * o_, :], w_low[0:LAT, 0, cols], low[0:LAT, :], start=True, stop=False)
                    for c in range(DC):
                        pe.matmul(pa[:, 2 * o_, :], w_kr[:, c, cols], x[c], start=False, stop=(c == DC - 1))
                    for c in range(DC):
                        ins = pe.matmul(pa[:, 2 * o_ + 1, :], w_kt[:, c, cols], x[c], start=(c == 0),
                                        stop=(c == DC - 1))
                    ins.then_inc(rot_ready, 1)
                pe.wait_ge(y_added, b + 1)
                for t in range(TB):
                    ins = pe.matmul(po[:, t, :], low[0:LAT, t * P:(t + 1) * P], w_low[0:LAT, 1, :],
                                    start=True, stop=True)
                ins.then_inc(v_ready, 1)
                for o_ in range(DC):
                    cols = slice(o_ * P, (o_ + 1) * P)
                    pe.wait_ge(rot_done, 4 * b + o_ + 1)
                    for k in range(2):
                        ins = pe.matmul(pa[:, 2 * o_ + k, :], w_low[LAT:P, k, cols], low[LAT:P, :],
                                        start=True, stop=True)
                    ins.then_inc(rot_ready, 1)
                pe.wait_ge(keys_ready, 2 * (b + 1))
                pe.wait_ge(rot_done, 4 * (b + 1))
                pe.wait_ge(v_copied, b + 1)
                for k in range(TB):
                    scores(b, 0, k)
                for h in range(H):
                    for k in range(TB):
                        if h + 1 < H:
                            scores(b, h + 1, k)
                    if h + 1 == H:
                        pe.wait_ge(exp_ready, TB * H * (b + 1))
                    n = TB * H * b + TB * h
                    for k in range(TB):
                        pe.wait_ge(turned_copied, n + k + 1)
                        for q in range(k, TB):
                            ins = pe.transpose(pw[:, k % 2, q * P:(q + 1) * P], pr[:, h % 2, q, k * P:(k + 1) * P],
                                               core.ident)
                        ins.then_inc(turned, 1)
                    pe.wait_ge(turned_copied, n + TB + 2)
                    ch = slice(16 * h, 16 * h + 16)
                    for q in range(TB):
                        for k in range(q + 1):
                            ins = pe.matmul(po[:, q, ch], prT[:, h % 2, k, q * P:(q + 1) * P], v[:, k, ch],
                                            start=(k == 0), stop=(k == q))
                    ins.then_inc(heads_out, 1)
                pe.wait_ge(norm_step, 2 * (b + 1))
                for t in range(TB):
                    for c in range(DC):
                        ins = pe.transpose(pw[:, c, t * P:(t + 1) * P], o[:, t, c * P:(c + 1) * P], core.ident)
                ins.then_inc(o_turned, 1)
                pe.wait_ge(o_copied, b + 1)
                for t in range(TB):
                    for c in range(DC):
                        cols = oT[:, c, :].rearrange("d (g q p) -> d g p q", q=P, p=2)[:, t // 2, t % 2, :]
                        ins = pe.matmul(py[:, t, :], cols, w_o[:, c, :], start=(c == 0), stop=(c == DC - 1))
                ins.then_inc(y_ready, 1)

        @block.gpsimd
        def _(pool):
            with pool.Fori(0, B) as b:
                pool.wait_ge(rot_done, 4 * b + 2)
                for k in range(2):
                    pool.tensor_tensor(keys[:, k, :, :], kT[:], core.consts[:, C_KEYS + k:C_KEYS + k + 1].unsqueeze(
                        2).to_broadcast([P, DC, T]), ALU.mult).then_inc(keys_ready, 1)

        @block.scalar
        def _(act):
            act.preload_act_table(ACT.Exp)
            with act.Fori(0, B) as b:
                act.wait_ge(low_ready, b + 1)
                act.activation(low[:], pw[:, 0, :], ACT.Copy).then_inc(low_copied, 1)
                act.wait_ge(v_ready, b + 1)
                act.activation(v[:], po[:], ACT.Copy).then_inc(v_copied, 1)
                for h in range(H):
                    if h >= 2:
                        act.wait_ge(turned, TB * H * b + TB * (h - 1))
                    for k, q in enumerate(QB_ORDER):
                        n = (q + 1) * P
                        act.wait_ge(max_ready, TB * H * b + TB * h + k + 1)
                        act.activation(pr[:, h % 2, q, 0:n], pa[:, q, 0:n], ACT.Exp, bias=nmax[:, h % 2, q:q + 1],
                                       accum_out=total[:, h, q:q + 1]).then_inc(exp_ready, 1)
                act.wait_ge(o_turned, b + 1)
                act.activation(oT[:], pw[:], ACT.Copy).then_inc(o_copied, 1)

        @block.vector
        def _(dve):
            dve.sem_inc(y_added, 1)
            dve.sem_inc(turned_copied, 2)
            dve.wait_ge(w_in, 16 * len(loads))
            with dve.Fori(0, B) as b:
                for which, dst in enumerate((kT, qT)):
                    for o_ in range(DC):
                        n = 4 * b + 2 * which + o_
                        dve.wait_ge(rot_ready, n + 1)
                        dve.tensor_tensor(turn[:, 0, :], pa[:, 2 * o_, :], rope[:, 0, :], ALU.mult)
                        dve.tensor_tensor(turn[:, 1, :], pa[:, 2 * o_ + 1, :], rope[:, 1, :],
                                          ALU.mult).then_inc(rot_step, 1)
                        dve.wait_ge(rot_step, n + 1)
                        dve.tensor_tensor(dst[:, o_, :], turn[:, 0, :], turn[:, 1, :], ALU.add).then_inc(rot_done, 1)
                        dve.wait_ge(rot_done, n + 1)
                for h in range(H + 1):
                    n = TB * H * b + TB * h
                    if h < H:
                        for k, q in enumerate(QB_ORDER):
                            w = (q + 1) * P
                            dve.wait_ge(scores_ready, n + k + 1)
                            dve.tensor_tensor(pa[:, q, q * P:w], pa[:, q, q * P:w], core.neg,
                                              ALU.add).then_inc(score_masked, 1)
                            dve.wait_ge(score_masked, n + k + 1)
                            dve.tensor_reduce(nmax[:, h % 2, q:q + 1], pa[:, q, 0:w], AX.X, ALU.max, negate=True
                                              ).then_inc(max_ready, 1)
                    if h:
                        n -= TB
                        if h > 2:
                            dve.wait_ge(heads_out, H * b + h - 2)
                        for k in range(TB):
                            dve.wait_ge(turned, n + k + 1)
                            dve.tensor_copy(prT[:, (h - 1) % 2, k, k * P:T], pw[:, k % 2, k * P:T]
                                            ).then_inc(turned_copied, 1)
                dve.wait_ge(heads_out, H * (b + 1))
                inv = Steps(dve, norm_step, 2 * b, 2)
                inv(dve.reciprocal(total[:], total[:]))
                inv(dve.tensor_tensor(o[:].rearrange("q t (h d) -> q t h d", d=16),
                                      po[:].rearrange("q t (h d) -> q t h d", d=16),
                                      total[:].rearrange("q h t -> q t h").unsqueeze(3).to_broadcast([P, TB, H, 16]),
                                      ALU.mult))
                inv.close()
                xn = core.xn[:, bass.ds(4 * b, 4), :]
                x = core.x[:, bass.ds(4 * b, 4), :]
                dve.wait_ge(y_ready, b + 1)
                dve.tensor_tensor(xn, py[:], xn, ALU.add).then_inc(y_added, 1)
                dve.wait_ge(y_added, b + 2)
                dve.tensor_tensor(x, x, xn, ALU.add).then_inc(joined, 1)


class Spec:
    pass


def layer1_spec(dram):
    s = Spec()
    s.router, s.router_bias = dram["L1_gate_wT"], dram["L1_ffn_gate_b"]
    s.gate, s.up, s.down = dram["L1_ffn_w_gate"], dram["L1_ffn_w_up"], dram["L1_ffn_w_down"]
    s.gate_bT, s.up_bT, s.down_b = dram["L1_b_gateT"], dram["L1_b_upT"], dram["L1_ffn_b_down"]
    s.routed, s.experts, s.top, s.kind, s.weigh, s.unroll = 32, 32, 4, "swiglu", "softmax", 4
    s.alpha, s.limit = 1.702, 7.0
    s.factor = 1.0 / s.alpha
    return s


def layer2_spec(dram):
    s = Spec()
    s.router, s.router_bias = dram["L2_ffn_router_w"], dram["L2_ffn_router_b"]
    s.gate, s.up, s.down, s.down_b = dram["L2_gate"], dram["L2_up"], dram["L2_down"], None
    s.routed, s.experts, s.top, s.kind, s.weigh, s.unroll = 7, 8, 2, "silu", "sigmoid", 4
    s.factor = 1.0 / 8.0
    return s


def layer3_spec(dram):
    s = Spec()
    s.router, s.router_bias = dram["L3_ffn_gate_w"], None
    s.gate, s.up, s.down, s.down_b = dram["L3_ffn_w0"], dram["L3_ffn_w1"], dram["L3_ffn_wo"], None
    s.routed, s.experts, s.top, s.kind, s.weigh, s.unroll = 8, 8, 2, "silu", "softmax", 2
    s.factor = 1.0
    return s


def route(nc, st, core, spec, aT, cw):
    sem = st.sem
    R, K = spec.routed, spec.top
    E8 = max(R, 8)
    w, bias = st.sb("w", [P, DC, R]), st.sb("bias", [P, R])
    scores = st.sb("scores", [P, TILES, E8])
    top = st.sb("top", [P, TILES, 8])
    which = st.scope.enter_context(nc.sbuf_tensor(st.name + "_which", [P, TILES, 8], mybir.dt.uint32))
    weight, hit = st.sb("weight", [P, TILES, K]), st.sb("hit", [P, TILES, R])
    total = st.sb("total", [P, TILES])
    logits = st.ps("logits", [P, TILES, 32])
    w_in, products, step, act_done = sem("w_in"), sem("products"), sem("step"), sem("act_done")
    picked, at_score = sem("picked"), sem("at_score")
    n_in = 16 * (1 + (spec.router_bias is not None))
    if spec.down_b is not None:
        db, cwT = st.sb("down_b", [R, D]), st.sb("cwT", [R, TILES, P])
        pT, pb = st.ps("cwT_p", [P, 4, P]), st.ps("bias_p", [P, 4, D])
        cw_turned, cwT_ready, bias_ready, bias_added = (sem(n) for n in (
            "cw_turned", "cwT_ready", "bias_ready", "bias_added"))
        n_in += 16
    with nc.Block() as block:
        @block.sync
        def _(sp):
            sp.dma_start(w[:], in_chunks(spec.router)).then_inc(w_in, 16)
            if spec.router_bias is not None:
                sp.dma_start(bias[:], on_all_partitions(spec.router_bias, P)).then_inc(w_in, 16)
            if spec.down_b is not None:
                sp.dma_start(db[:], spec.down_b).then_inc(w_in, 16)

        @block.tensor
        def _(pe):
            pe.wait_ge(w_in, n_in)
            for t in range(TILES):
                for c in range(DC):
                    ins = pe.matmul(logits[:, t, 0:R], col_group(aT, t // 2, t % 2)[:, c, :], w[:, c, :],
                                    start=(c == 0), stop=(c == DC - 1))
            ins.then_inc(products, 1)
            if spec.down_b is not None:
                pe.wait_ge(at_score, 1)
                for t in range(TILES):
                    if t % 4 == 0 and t:
                        pe.wait_ge(cwT_ready, t // 4)
                    ins = pe.transpose(pT[0:R, t % 4, :], cw[:, t, 0:R], core.ident)
                    if t % 4 == 3:
                        ins.then_inc(cw_turned, 1)
                pe.wait_ge(cwT_ready, TILES // 4)
                for t in range(TILES):
                    if t % 4 == 0 and t:
                        pe.wait_ge(bias_added, t // 4)
                    ins = pe.matmul(pb[:, t % 4, :], cwT[:, t, :], db[:], start=True, stop=True)
                    if t % 4 == 3:
                        ins.then_inc(bias_ready, 1)

        @block.scalar
        def _(act):
            if spec.weigh == "sigmoid":
                act.wait_ge(step, 2)
                act.activation(scores[:, :, 0:R], scores[:, :, 0:R], ACT.Sigmoid).then_inc(act_done, 1)
            else:
                act.wait_ge(step, 2)
                act.activation(weight[:], weight[:], ACT.Exp).then_inc(act_done, 1)

        @block.vector
        def _(dve):
            do = Steps(dve, step)
            dve.wait_ge(w_in, n_in)
            dve.wait_ge(products, 1)
            if spec.weigh == "sigmoid":
                do(dve.memset(scores[:, :, R:E8], -1.0))
            if spec.router_bias is not None:
                ins = dve.tensor_tensor(scores[:, :, 0:R], logits[:, :, 0:R],
                                        bias[:].unsqueeze(1).to_broadcast([P, TILES, R]), ALU.add)
            else:
                ins = dve.tensor_copy(scores[:, :, 0:R], logits[:, :, 0:R])
            do(ins)
            if spec.weigh == "sigmoid":
                dve.wait_ge(act_done, 1)
            for t in range(TILES):
                dve.max(top[:, t, :], scores[:, t, :]).then_inc(picked, 1)
            for t in range(TILES):
                dve.wait_ge(picked, t + 1)
                ins = dve.max_index(which[:, t, :], top[:, t, :], scores[:, t, :])
                ins.then_inc(picked, 1)
            dve.wait_ge(picked, 2 * TILES)
            if spec.weigh == "softmax":
                do(dve.tensor_tensor(weight[:], top[:, :, 0:K], top[:, :, 0:1].to_broadcast([P, TILES, K]),
                                     ALU.subtract))
                dve.wait_ge(act_done, 1)
            else:
                do(dve.tensor_copy(weight[:], top[:, :, 0:K]))
            do(dve.reduce_sum(total[:], weight[:], AX.X))
            do(dve.reciprocal(total[:], total[:]))
            do(dve.tensor_scalar(total[:], total[:], spec.factor, None, ALU.mult))
            do(dve.tensor_tensor(weight[:], weight[:], total[:].unsqueeze(2).to_broadcast([P, TILES, K]),
                                 ALU.mult))
            numbers = core.consts[:, C_COUNT:C_COUNT + R].unsqueeze(1).to_broadcast([P, TILES, R])
            if spec.experts > R:
                do(dve.memset(cw[:, :, R:spec.experts], spec.factor))
            for k in range(K):
                to = cw[:, :, 0:R] if k == 0 else hit[:]
                do(dve.tensor_tensor(to, numbers, which[:, :, k:k + 1].to_broadcast([P, TILES, R]), ALU.is_equal))
                do(dve.tensor_tensor(to, to, weight[:, :, k:k + 1].to_broadcast([P, TILES, R]), ALU.mult))
                if k:
                    do(dve.tensor_tensor(cw[:, :, 0:R], cw[:, :, 0:R], hit[:], ALU.add))
            if spec.down_b is not None:
                assert spec.factor != 1.0
                dve.sem_inc(at_score, 1)
                for k in range(TILES // 4):
                    dve.wait_ge(cw_turned, k + 1)
                    dve.tensor_scalar(cwT[:, 4 * k:4 * k + 4, :], pT[0:R, :, :], 1.0 / spec.factor, None,
                                      ALU.mult).then_inc(cwT_ready, 1)
                for k in range(TILES // 4):
                    dve.wait_ge(bias_ready, k + 1)
                    x = core.x[:, 4 * k:4 * k + 4, :]
                    dve.tensor_tensor(x, pb[:], x, ALU.add).then_inc(bias_added, 1)


def experts(nc, st, core, spec, aT):
    sem = st.sem
    E, U = spec.experts, spec.unroll
    I = spec.gate.shape[2]
    MC = I // P
    ITER = E // U
    BLOCKS = TB
    assert TOK == BLOCKS * 512
    STEPS = U * BLOCKS * MC
    LAG = 2
    RB = 4 if MC == 1 else 2
    RING = RB * MC
    cw = st.sb("cw", [P, TILES, max(E, 8)])
    with ExitStack() as scope:
        route(nc, Stage(nc, st.keep, scope, st.name + "r"), core, spec, aT, cw)

    swiglu = spec.kind == "swiglu"
    wg, wu = st.sb("wg", [P, U, DC, I]), st.sb("wu", [P, U, DC, I])
    wd = st.sb("wd", [P, U, MC, D])
    hidden = st.sb("hidden", [P, RING, 512])
    silu = st.sb("silu", [P, 2, 512])
    if swiglu:
        bg, bu = st.sb("bg", [P, E]), st.sb("bu", [P, E])
        gate, up = st.sb("gate", [P, 2, 512]), st.sb("up", [P, 2, 512])
    pg, pu = st.ps("pg", [P, 2, 512]), st.ps("pu", [P, 2, 512])
    py = st.ps("py", [P, 2, 4, D])
    w_in = [sem(f"w{u}_in") for u in range(U)]
    bias_in = sem("bias_in")
    g_ready, u_ready, g_taken, u_taken = (sem(n) for n in ("g_ready", "u_ready", "g_taken", "u_taken"))
    silu_ready, up_clipped = sem("silu_ready"), sem("up_clipped")
    hidden_ready, y_ready, y_taken = sem("hidden_ready"), sem("y_ready"), sem("y_taken")
    act_waited, pool_waited = sem("act_waited"), sem("pool_waited")
    if not swiglu:
        u_taken = hidden_ready
    order = [(u, tb, m) for u in range(U) for tb in range(BLOCKS) for m in range(MC)]

    def load(sp, u, e):
        for dst, src in ((wg, spec.gate), (wu, spec.up)):
            sp.dma_start(dst[:, u, :, :], src[e].rearrange("(c p) i -> p c i", p=P)).then_inc(w_in[u], 16)
        sp.dma_start(wd[:, u, :, :], spec.down[e].rearrange("(m p) d -> p m d", p=P)).then_inc(w_in[u], 16)

    with nc.Block() as block:
        @block.sync
        def _(sp):
            if swiglu:
                sp.dma_start(bg[:], spec.gate_bT).then_inc(bias_in, 16)
                sp.dma_start(bu[:], spec.up_bT).then_inc(bias_in, 16)
            for u in range(U):
                load(sp, u, u)
            with sp.Fori(1, ITER) as i:
                for u in range(U):
                    sp.wait_ge(y_ready, RB + (i - 1) * U * BLOCKS + (u + 1) * BLOCKS)
                    for dst, src in ((wg, spec.gate), (wu, spec.up)):
                        sp.dma_start(dst[:, u, :, :], src[bass.ds(i * U + u, 1)].rearrange(
                            "e (c p) i -> p (e c) i", p=P)).then_inc(w_in[u], 16)
                    sp.dma_start(wd[:, u, :, :], spec.down[bass.ds(i * U + u, 1)].rearrange(
                        "e (m p) d -> p (e m) d", p=P)).then_inc(w_in[u], 16)

        @block.tensor
        def _(pe):
            pe.sem_inc(y_ready, RB)

            def up_and_gate(i, k):
                u, tb, m = order[k]
                n = i * STEPS + k
                if tb == 0 and m == 0:
                    pe.wait_ge(w_in[u], 48 * (i + 1))
                for ps, w, taken, ready in ((pg, wg, g_taken, g_ready), (pu, wu, u_taken, u_ready)):
                    pe.wait_ge(taken, n + 1)
                    for c in range(DC):
                        ins = pe.matmul(ps[:, k % 2, :], w[:, u, c, m * P:(m + 1) * P],
                                        aT[:, c, tb * 512:(tb + 1) * 512], start=(c == 0), stop=(c == DC - 1))
                    ins.then_inc(ready, 1)

            def down(i, k):
                u, tb, m = order[k]
                nb = i * U * BLOCKS + u * BLOCKS + tb
                pe.wait_ge(hidden_ready, i * STEPS + k + 3)
                if m == 0:
                    pe.wait_ge(y_taken, nb + 1)
                for q in range(4):
                    cols = hidden[:, k % RING, :].rearrange("h (g q p) -> h g p q", q=P, p=2)[:, q // 2, q % 2, :]
                    ins = pe.matmul(py[:, (k // MC) % 2, q, :], cols, wd[:, u, m, :], start=(m == 0 and q % 2 == 0),
                                    stop=(m == MC - 1), skip_group_check=True)
                if m == MC - 1:
                    ins.then_inc(y_ready, 1)

            with pe.Fori(0, ITER) as i:
                for k in range(STEPS + LAG):
                    if k < STEPS:
                        up_and_gate(i, k)
                    if k >= LAG:
                        down(i, k - LAG)

        @block.scalar
        def _(act):
            act.preload_act_table(ACT.Silu)
            if swiglu:
                act.wait_ge(bias_in, 32)
                act.sem_inc(u_taken, 2)
            else:
                act.sem_inc(g_taken, 2)
            with act.Fori(0, ITER) as i:
                for k in range(STEPS):
                    n = i * STEPS + k
                    e = i * U + order[k][0]
                    act.wait_ge(hidden_ready, n + 1)
                    if swiglu:
                        wait_apart(act, u_ready, n + 1, act_waited)
                        act.activation(up[:, k % 2, :], pu[:, k % 2, :], ACT.Identity,
                                       bias=bu[:, bass.ds(e, 1)]).then_inc(u_taken, 1)
                        act.wait_ge(g_taken, n + 3)
                        act.activation(silu[:, k % 2, :], gate[:, k % 2, :], ACT.Silu,
                                       scale=spec.alpha).then_inc(silu_ready, 1)
                    else:
                        act.wait_ge(g_ready, n + 1)
                        act.activation(silu[:, k % 2, :], pg[:, k % 2, :], ACT.Silu).then_inc(g_taken, 1)

        if swiglu:
            @block.gpsimd
            def _(pool):
                with pool.Fori(0, ITER) as i:
                    for k in range(STEPS):
                        wait_apart(pool, u_taken, i * STEPS + k + 3, pool_waited)
                        pool.tensor_scalar(up[:, k % 2, :], up[:, k % 2, :], spec.limit, -spec.limit, ALU.min,
                                           ALU.max).then_inc(up_clipped, 1)

        @block.vector
        def _(dve):
            dve.sem_inc(y_taken, 2)
            dve.sem_inc(hidden_ready, 2)
            if swiglu:
                dve.sem_inc(g_taken, 2)
                dve.wait_ge(bias_in, 32)

            def clamp_gate(i, k):
                n = i * STEPS + k
                dve.wait_ge(g_ready, n + 1)
                dve.wait_ge(hidden_ready, n + 1)
                dve.tensor_scalar(gate[:, k % 2, :], pg[:, k % 2, :], bg[:, bass.ds(i * U + order[k][0], 1)],
                                  spec.limit, ALU.add, ALU.min).then_inc(g_taken, 1)

            def hide(i, k):
                n = i * STEPS + k
                nb = i * U * BLOCKS + k // MC
                dve.wait_ge(y_ready, nb + 1)
                if swiglu:
                    dve.wait_ge(silu_ready, n + 1)
                    dve.wait_ge(up_clipped, n + 1)
                    dve.scalar_tensor_tensor(out=hidden[:, k % RING, :], in0=up[:, k % 2, :], scalar=1.0,
                                             in1=silu[:, k % 2, :], op0=ALU.add, op1=ALU.mult
                                             ).then_inc(hidden_ready, 1)
                else:
                    dve.wait_ge(g_taken, n + 3)
                    dve.wait_ge(u_ready, n + 1)
                    dve.tensor_tensor(hidden[:, k % RING, :], pu[:, k % 2, :], silu[:, k % 2, :],
                                      ALU.mult).then_inc(hidden_ready, 1)

            def weigh(i, nb_in):
                u, tb = nb_in // BLOCKS, nb_in % BLOCKS
                dve.wait_ge(y_ready, i * U * BLOCKS + nb_in + 1 + RB)
                for q in range(4):
                    t = 4 * tb + q
                    ins = dve.scalar_tensor_tensor(out=core.x[:, t, :], in0=py[:, nb_in % 2, q, :],
                                                   scalar=cw[:, t, bass.ds(i * U + u, 1)], in1=core.x[:, t, :],
                                                   op0=ALU.mult, op1=ALU.add)
                ins.then_inc(y_taken, 1)

            with dve.Fori(0, ITER) as i:
                for k in range(STEPS + LAG + 1):
                    if k < STEPS and swiglu:
                        clamp_gate(i, k)
                    if swiglu and 1 <= k <= STEPS:
                        hide(i, k - 1)
                    if not swiglu and k < STEPS:
                        hide(i, k)
                    done = k - LAG - 1
                    if done >= 0 and done % MC == MC - 1:
                        weigh(i, done // MC)


QB_ORDER = (3, 2, 1, 0)


def layer3_attention(nc, st, core, dram, aT):
    sem = st.sem
    SCALE = D ** -0.5
    w, wo = st.sb("w", [P, DC, 3 * D]), st.sb("wo", [P, DC, D])
    here = st.sb("here", [P, DC, T])
    qT, kT, v = st.sb("qT", [P, DC, T]), st.sb("kT", [P, DC, T]), st.sb("v", [P, TB, D])
    pr, prT = st.sb("pr", [P, TB, T]), st.sb("prT", [P, TB, T])
    oT = st.sb("oT", [P, DC, T])
    nmax, total, inv = (st.sb(n, [P, TB]) for n in ("nmax", "total", "inv"))
    pa = st.ps("pa", [P, 4, T])
    pv = st.ps("pv", [P, TB, D])
    pw = st.ps("pw", [P, 2, T])
    (w_in, here_ready, qk_ready, q_copied, k_copied, v_ready, v_copied, scores_ready, score_masked, max_ready,
     exp_ready, inv_ready, prob_ready, turned, turned_copied, o_ready, o_copied, y_ready, y_added, x_residual) = (
        sem(n) for n in ("w_in here_ready qk_ready q_copied k_copied v_ready v_copied scores_ready score_masked "
                         "max_ready exp_ready inv_ready prob_ready turned turned_copied o_ready o_copied y_ready "
                         "y_added x_residual").split())
    poT = pv[:].rearrange("d (c h) n -> d c (h n)", c=DC)
    py = pw[:].rearrange("q b (k n) -> q (b k) n", n=D)
    with nc.Block() as block:
        @block.sync
        def _(sp):
            sp.dma_start(w[:], in_chunks(dram["L3_attn_qkv"])).then_inc(w_in, 16)
            sp.dma_start(wo[:], in_chunks(dram["L3_attn_o_proj"])).then_inc(w_in, 16)

        @block.gpsimd
        def _(pool):
            with pool.Fori(0, B) as b:
                pool.wait_ge(v_copied, b + 1)
                pool.tensor_copy(here[:], aT[:, :, bass.ds(b * T, T)]).then_inc(here_ready, 1)
                for k, q in enumerate(QB_ORDER):
                    n = (q + 1) * P
                    pool.wait_ge(inv_ready, TB * b + k + 1)
                    pool.tensor_tensor(pr[:, q, 0:n], pr[:, q, 0:n], inv[:, q:q + 1].to_broadcast([P, n]),
                                       ALU.mult).then_inc(prob_ready, 1)

        @block.tensor
        def _(pe):
            pe.wait_ge(w_in, 32)
            with pe.Fori(0, B) as b:
                pe.wait_ge(here_ready, b + 1)
                for o in range(4):
                    for c in range(DC):
                        ins = pe.matmul(pa[:, o, :], w[:, c, o * P:(o + 1) * P], here[:, c, :],
                                        start=(c == 0), stop=(c == DC - 1))
                ins.then_inc(qk_ready, 1)
                for t in range(TB):
                    for c in range(DC):
                        ins = pe.matmul(pv[:, t, :], here[:, c, t * P:(t + 1) * P], w[:, c, 2 * D:3 * D],
                                        start=(c == 0), stop=(c == DC - 1))
                ins.then_inc(v_ready, 1)
                pe.wait_ge(q_copied, b + 1)
                pe.wait_ge(k_copied, b + 1)
                for q in QB_ORDER:
                    n = (q + 1) * P
                    for c in range(DC):
                        ins = pe.matmul(pa[:, q, 0:n], qT[:, c, q * P:(q + 1) * P], kT[:, c, 0:n],
                                        start=(c == 0), stop=(c == DC - 1))
                    ins.then_inc(scores_ready, 1)
                pe.wait_ge(prob_ready, TB * (b + 1))
                pe.wait_ge(y_added, b + 1)
                for k in range(TB):
                    if k >= 2:
                        pe.wait_ge(turned_copied, TB * b + k - 1)
                    for q in range(k, TB):
                        ins = pe.transpose(pw[:, k % 2, q * P:(q + 1) * P], pr[:, q, k * P:(k + 1) * P], core.ident)
                    ins.then_inc(turned, 1)
                pe.wait_ge(v_copied, b + 2)
                for k in range(TB):
                    pe.wait_ge(turned_copied, TB * b + k + 1)
                    for c in range(DC):
                        ins = pe.matmul(poT[:, c, k * P:T], v[:, k, c * P:(c + 1) * P], prT[:, k, k * P:T],
                                        start=(k == 0), stop=(k == TB - 1), skip_group_check=True)
                ins.then_inc(o_ready, 1)
                pe.wait_ge(o_copied, b + 1)
                for t in range(TB):
                    for c in range(DC):
                        cols = oT[:, c, :].rearrange("d (g q p) -> d g p q", q=P, p=2)[:, t // 2, t % 2, :]
                        ins = pe.matmul(py[:, t, :], cols, wo[:, c, :], start=(c == 0), stop=(c == DC - 1))
                ins.then_inc(y_ready, 1)

        @block.scalar
        def _(act):
            act.preload_act_table(ACT.Exp)
            act.sem_inc(v_copied, 1)
            with act.Fori(0, B) as b:
                act.wait_ge(qk_ready, b + 1)
                act.activation(qT[:], pa[:, 0:2, :], ACT.Copy, scale=SCALE).then_inc(q_copied, 1)
                act.wait_ge(v_ready, b + 1)
                act.activation(v[:], pv[:], ACT.Copy).then_inc(v_copied, 1)
                for k, q in enumerate(QB_ORDER):
                    n = (q + 1) * P
                    act.wait_ge(max_ready, TB * b + k + 1)
                    act.activation(pr[:, q, 0:n], pa[:, q, 0:n], ACT.Exp, bias=nmax[:, q:q + 1],
                                   accum_out=total[:, q:q + 1]).then_inc(exp_ready, 1)
                for k in range(1, TB, 2):
                    act.wait_ge(turned, TB * b + k + 1)
                    act.wait_ge(turned_copied, TB * b + k)
                    act.activation(prT[:, k, k * P:T], pw[:, k % 2, k * P:T], ACT.Copy).then_inc(turned_copied, 1)
                act.wait_ge(o_ready, b + 1)
                act.activation(oT[:], poT, ACT.Copy).then_inc(o_copied, 1)

        @block.vector
        def _(dve):
            dve.sem_inc(y_added, 1)
            with dve.Fori(0, B) as b:
                dve.wait_ge(qk_ready, b + 1)
                dve.tensor_copy(kT[:], pa[:, 2:4, :]).then_inc(k_copied, 1)
                for k, q in enumerate(QB_ORDER):
                    n = (q + 1) * P
                    dve.wait_ge(scores_ready, TB * b + k + 1)
                    dve.tensor_tensor(pa[:, q, q * P:n], pa[:, q, q * P:n], core.neg, ALU.add).then_inc(score_masked, 1)
                    dve.wait_ge(score_masked, TB * b + k + 1)
                    dve.tensor_reduce(nmax[:, q:q + 1], pa[:, q, 0:n], AX.X, ALU.max, negate=True
                                      ).then_inc(max_ready, 1)
                for k, q in enumerate(QB_ORDER):
                    dve.wait_ge(exp_ready, TB * b + k + 1)
                    dve.reciprocal(inv[:, q:q + 1], total[:, q:q + 1]).then_inc(inv_ready, 1)
                x, xn = core.x[:, bass.ds(4 * b, 4), :], core.xn[:, bass.ds(4 * b, 4), :]
                dve.tensor_tensor(x, x, xn, ALU.add).then_inc(x_residual, 1)
                for k in range(0, TB, 2):
                    dve.wait_ge(turned, TB * b + k + 1)
                    if k:
                        dve.wait_ge(turned_copied, TB * b + k)
                    dve.tensor_copy(prT[:, k, k * P:T], pw[:, k % 2, k * P:T]).then_inc(turned_copied, 1)
                dve.wait_ge(x_residual, b + 1)
                dve.wait_ge(y_ready, b + 1)
                dve.tensor_tensor(x, py, x, ALU.add).then_inc(y_added, 1)


LAYERS = (0, 1, 2, 3)


def build(nc, dram, out):
    with ExitStack() as keep:
        core, used = Core(), []

        def resident(name, shape):
            return keep.enter_context(nc.sbuf_tensor(name, shape, F32))

        core.x, core.xn = resident("x", [P, TILES, D]), resident("xn", [P, TILES, D])
        core.xnT = resident("xnT", [P, DC, TOK])
        core.consts = resident("consts", [P, C_END])
        core.ab_sum, core.bcT = resident("ab_sum", [P, DC]), resident("bcT", [P, DC, B])
        core.ident = core.consts[:, C_ID:C_ID + P]
        core.tri = core.consts[:, C_TRI:C_TRI + P]
        core.neg = core.consts[:, C_NEG:C_NEG + P]
        core.blk = core.consts[:, C_BLK:C_BLK + P]

        def run(name, f, *args, **kw):
            with ExitStack() as scope:
                f(nc, Stage(nc, used, scope, name), core, *args, **kw)

        run("s", setup, dram)
        if 0 in LAYERS:
            run("n0", normalise, core.x, core.xn, core.xnT, 1e-5)
            with ExitStack() as scope:
                st = Stage(nc, used, scope, "l0")
                gsT, gateT, last_rows = st.sb("gsT", [P, DC, TOK]), st.sb("gateT", [P, DC, TOK]), st.sb("last", [B, D])
                run("m0", layer0_mix, dram, gsT, gateT, last_rows)
                run("j0", layer0_join, dram, gsT, gateT)
        if 1 in LAYERS:
            run("n1", normalise, core.x, core.xn, core.xnT, 1e-5)
            run("a1", layer1_attention)
            run("f1", experts, layer1_spec(dram), core.xnT)
        if 2 in LAYERS:
            release(nc, used)
            run("n2", normalise, core.x, core.xn, core.xnT, 1e-5)
            run("a2", layer2_abc, dram)
            with ExitStack() as scope:
                st = Stage(nc, used, scope, "l2")
                aT = st.sb("aT", [P, DC, TOK])
                run("r2", normalise, core.xn, None, aT, 1e-5, rms=True, gain=dram["L2_ffn_ln1_w"])
                run("b2", layer2_attention, dram, aT)
                run("q2", normalise, core.xn, None, aT, 1e-5, rms=True, gain=dram["L2_ffn_ln2_w"])
                run("f2", experts, layer2_spec(dram), aT)
        if 3 in LAYERS:
            release(nc, used)
            run("n3", normalise, core.x, core.xn, core.xnT, 1e-5)
            with ExitStack() as scope:
                st = Stage(nc, used, scope, "l3")
                aT = st.sb("aT", [P, DC, TOK])
                run("r3", normalise, core.xn, None, aT, 1e-5, gain=dram["L3_attn_gamma"],
                    shift=dram["L3_attn_beta"])
                run("a3", layer3_attention, dram, aT)
            run("f3", experts, layer3_spec(dram), core.xnT)

        stored = nc.alloc_semaphore(name="stored")
        with nc.Block() as block:
            @block.sync
            def _(sp):
                for p in range(2):
                    sp.dma_start(token_rows(out, p), core.x[:, p::2, :]).then_inc(stored, 16)
                sp.wait_ge(stored, 32)


def constants():
    c = np.zeros((P, C_END), np.float32)
    i = np.arange(P)
    c[:, C_ID:C_ID + P] = np.eye(P)
    c[:, C_TRI:C_TRI + P] = i[None, :] >= i[:, None]
    c[:, C_NEG:C_NEG + P] = np.where(i[None, :] > i[:, None], NEG, 0.0)
    c[:, C_BLK:C_BLK + P] = i[None, :] // 32 == i[:, None] // 32
    for p in range(2):
        c[:, C_EVEN + p] = (i // 16) % 2 == p
        c[:, C_KEYS + p] = 0.25 * c[:, C_EVEN + p]
    c[:, C_HALF:C_HALF + TILES] = -0.5
    c[:, C_ONE] = 1.0
    c[:, C_COUNT:C_COUNT + 32] = np.arange(32)
    half = 4
    inv = 1.0 / 10000.0 ** (np.arange(0, 8, 2, dtype=np.float32) / np.float32(8))
    angle = np.arange(T, dtype=np.float32)[None, :] * inv.astype(np.float32)[:, None]
    cos, sin = np.ones((P, T), np.float32), np.zeros((P, T), np.float32)
    for q in range(P):
        r = q % 16 - 8
        if r >= 0:
            cos[q] = np.cos(angle[r % half])
            sin[q] = np.sin(angle[r % half]) * (-1.0 if r < half else 1.0)
    return c, np.stack([cos, sin])


def lay_out(inputs):
    a = {n: np.ascontiguousarray(v) for n, v in inputs.items() if not n.startswith("L3_ffn_decoder")}
    a["consts"], a["rope"] = constants()
    a["C_wT"] = np.ascontiguousarray(a.pop("L0_attn_C_w").T)
    a["D_wT"] = np.ascontiguousarray(a.pop("L0_attn_D_w").T)
    a["L1_gate_wT"] = np.ascontiguousarray(a.pop("L1_ffn_gate_w").T)
    for n in ("b_gate", "b_up"):
        a["L1_%sT" % n] = np.ascontiguousarray(a.pop("L1_ffn_" + n).T)
    for n in ("gate", "up", "down"):
        a["L2_" + n] = np.concatenate([a.pop("L2_ffn_r_" + n), a.pop("L2_ffn_sh_" + n)[None]])
    nh, rd = 16, 8

    def slots(w, first):
        w = w.reshape(w.shape[0], nh, rd)
        z = np.zeros_like(w)
        return np.concatenate([w, z] if first else [z, w], axis=2).reshape(w.shape[0], -1)

    def turned(w):
        w = w.reshape(w.shape[0], nh, 2, rd // 2)[:, :, ::-1]
        return np.ascontiguousarray(w).reshape(w.shape[0], -1)

    for q in "kq":
        up, rope = a.pop("L2_ffn_%s_u_w" % q), a.pop("L2_ffn_rope_%s_w" % q)
        a["L2_%s_turned" % q] = slots(turned(rope), False)
        if q == "k":
            a["L2_k_plain"], a["L2_k_rope"] = slots(up, True), slots(rope, False)
        else:
            both = [w.reshape(w.shape[0], nh, rd) for w in (up, rope)]
            a["L2_q_both"] = np.concatenate(both, axis=2).reshape(up.shape[0], -1)
    a["L2_kvq_d"] = np.concatenate([a.pop("L2_ffn_kv_d_w"), a.pop("L2_ffn_q_d_w")], axis=1)
    return a


def kernel(**inputs):
    import concourse.bacc as bacc
    from concourse.bass_utils import run_bass_kernel_spmd

    nc = bacc.Bacc("TRN2", target_bir_lowering=False, num_devices=1)
    arrays = lay_out(inputs)
    dram = {n: nc.dram_tensor(n + "_dram", a.shape, mybir.dt.from_np(a.dtype), kind="ExternalInput").ap()
            for n, a in arrays.items()}
    out = nc.dram_tensor("out_dram", (B, T, D), F32, kind="ExternalOutput").ap()
    build(nc, dram, out)
    r = run_bass_kernel_spmd(nc, [{n + "_dram": a for n, a in arrays.items()}], core_ids=[0])
    return r.results[0]["out_dram"]
```

```python
from contextlib import ExitStack

import numpy as np

import concourse.bass as bass
from concourse import mybir

F32 = mybir.dt.float32
ALU = mybir.AluOpType
ACT = mybir.ActivationFunctionType
AX = mybir.AxisListType

P = 128
B, T, D = 4, 512, 256
TOK = B * T
TILES = TOK // P
DC = D // P
GROUPS = TILES // 2
TB = T // P
NEG = -1e30

C_ID, C_TRI, C_NEG, C_BLK, C_EVEN, C_HALF, C_ONE, C_COUNT = 0, 128, 256, 384, 512, 514, 530, 531
C_KEYS = C_COUNT + 32
C_END = C_KEYS + 2


class Steps:

    def __init__(self, eng, sem, base=0, total=None):
        self.eng, self.sem, self.base, self.total, self.n = eng, sem, base, total, 0

    def __call__(self, instruction):
        instruction.then_inc(self.sem, 1)
        self.n += 1
        self.eng.wait_ge(self.sem, self.base + self.n)

    def close(self):
        assert self.total is None or self.n == self.total, self.n


def wait_apart(eng, sem, value, waited):
    eng.wait_ge(sem, value)
    eng.sem_inc(waited, 1)


class Stage:

    def __init__(self, nc, keep, scope, name):
        self.nc, self.keep, self.scope, self.name = nc, keep, scope, name

    def sem(self, name):
        handle = self.nc.alloc_semaphore(name=f"{self.name}_{name}")
        self.keep.append(handle)
        return handle

    def sb(self, name, shape):
        return self.scope.enter_context(self.nc.sbuf_tensor(f"{self.name}_{name}", shape, F32))

    def sb_parts(self, name, shape):
        r = mybir.dt.float32r
        return Split(*(self.scope.enter_context(self.nc.sbuf_tensor(f"{self.name}_{name}_{x}", shape, r))
                       for x in ("hi", "lo")))

    def ps(self, name, shape):
        return self.scope.enter_context(self.nc.psum_tensor(f"{self.name}_{name}", shape, F32))


class Split:

    def __init__(self, hi, lo):
        self.hi, self.lo = hi, lo

    def view(self, f):
        return Split(f(self.hi), f(self.lo))


def split_matmul(pe, out, left, right, start, stop, **kw):
    for k, (a, b) in enumerate(((left.hi, right.hi), (left.hi, right.lo), (left.lo, right.hi))):
        ins = pe.matmul(out, a, b, start=start and k == 0, stop=stop and k == 2, **kw)
    return ins


class Core:
    pass


def release(nc, used):
    nc.clear_and_free_semaphores(used)
    nc.all_engine_barrier()
    used.clear()


def in_chunks(w):
    if len(w.shape) == 1:
        return w.rearrange("(c p) -> p c", p=P)
    return w.rearrange("(c p) n -> p c n", p=P)


def on_all_partitions(row, n):
    return row.unsqueeze(0).to_broadcast([n] + list(row.shape))


def token_rows(x, p):
    return x.rearrange("b t d -> (b t) d").rearrange("(g q p) d -> q g p d", q=P, p=2)[:, :, p, :]


def col_group(t, g, p):
    return t[:].rearrange("d c (g q p) -> d c g q p", q=P, p=2)[:, :, g, :, p]


def setup(nc, st, core, dram):
    sem = st.sem
    consts_in, x_in = sem("consts_in"), sem("x_in")
    with nc.Block() as block:
        @block.sync
        def _(sp):
            sp.dma_start(core.consts[:], dram["consts"]).then_inc(consts_in, 16)
            for p in range(2):
                sp.dma_start(core.x[:, p::2, :], token_rows(dram["L0_attn_x"], p)).then_inc(x_in, 16)
            sp.wait_ge(consts_in, 16)
            sp.wait_ge(x_in, 32)


def small_stats(do, eng, raw, mean, var, eps, rms):
    me, mo = raw[:, :, 1], raw[:, :, 4]
    do(eng.tensor_tensor(mean[:], me, mo, ALU.add))
    do(eng.tensor_tensor(var[:], me, mo, ALU.subtract))
    do(eng.tensor_tensor(var[:], var[:], var[:], ALU.mult))
    do(eng.scalar_tensor_tensor(out=var[:], in0=raw[:, :, 2], scalar=4.0 / D, in1=var[:],
                                op0=ALU.mult, op1=ALU.add))
    do(eng.scalar_tensor_tensor(out=var[:], in0=raw[:, :, 5], scalar=4.0 / D, in1=var[:],
                                op0=ALU.mult, op1=ALU.add))
    if rms:
        do(eng.tensor_tensor(raw[:, :, 0], mean[:], mean[:], ALU.mult))
        do(eng.tensor_tensor(var[:], var[:], raw[:, :, 0], ALU.add))
    do(eng.tensor_scalar(mean[:], mean[:], 0.5, None, ALU.mult))
    do(eng.tensor_scalar(var[:], var[:], 0.25, eps, ALU.mult, ALU.add))


def normalise(nc, st, core, src, tok_out, out_T, eps, rms=False, gain=None, shift=None):
    sem = st.sem
    raw = st.sb("raw", [P, TILES, 6])
    mean, var, rstd = (st.sb(n, [P, TILES]) for n in ("mean", "var", "rstd"))
    row = st.sb("row", [P, 2, D])
    turned = st.ps("turned", [P, 2, 512])
    gs = st.sb("gain_shift", [P, 2, DC])
    gain_in, stats, dve_step = sem("gain_in"), sem("stats"), sem("dve_step")
    rstd_ready = sem("rstd_ready")
    rows_ready, rows_free, rows_turned = sem("rows_ready"), sem("rows_free"), sem("rows_turned")
    n_gain = (gain is not None) + (shift is not None)
    with nc.Block() as block:
        @block.sync
        def _(sp):
            if gain is not None:
                sp.dma_start(gs[:, 0, :], in_chunks(gain), allow_slow_non_contiguous=True).then_inc(gain_in, 16)
            if shift is not None:
                sp.dma_start(gs[:, 1, :], in_chunks(shift), allow_slow_non_contiguous=True).then_inc(gain_in, 16)

        @block.vector
        def _(dve):
            with dve.Fori(0, TILES) as i:
                dve.bn_stats(raw[:, i, :], src[:, i, :]).then_inc(stats, 1)
            dve.wait_ge(stats, TILES)
            do = Steps(dve, dve_step)
            small_stats(do, dve, raw, mean, var, eps, rms)
            dve.wait_ge(rstd_ready, 1)
            with dve.Fori(0, GROUPS) as g:
                for p in range(2):
                    dve.wait_ge(rows_free, 2 * g + p + 1)
                    t = 2 * g + p
                    if rms:
                        dve.tensor_scalar(row[:, p, :], src[:, t, :], rstd[:, bass.ds(t, 1)], None,
                                          ALU.mult).then_inc(rows_ready, 1)
                    else:
                        dve.tensor_scalar(row[:, p, :], src[:, t, :], mean[:, bass.ds(t, 1)],
                                          rstd[:, bass.ds(t, 1)], ALU.subtract,
                                          ALU.mult).then_inc(rows_ready, 1)

        @block.gpsimd
        def _(pool):
            pool.wait_ge(dve_step, 9 if rms else 7)
            pool.tensor_tensor(rstd[:], var[:], core.consts[:, C_HALF:C_HALF + TILES],
                               ALU.pow).then_inc(rstd_ready, 1)

        @block.tensor
        def _(pe):
            with pe.Fori(0, GROUPS) as g:
                for p in range(2):
                    pe.wait_ge(rows_ready, 2 * g + p + 1)
                    for c in range(DC):
                        ins = pe.transpose(turned[:, p, c * P:(c + 1) * P], row[:, p, c * P:(c + 1) * P],
                                           core.ident)
                    ins.then_inc(rows_turned, 1)

        @block.scalar
        def _(act):
            act.preload_act_table(ACT.Identity)
            act.sem_inc(rows_free, 2)
            if n_gain:
                act.wait_ge(gain_in, 16 * n_gain)
            with act.Fori(0, GROUPS) as g:
                for p in range(2):
                    act.wait_ge(rows_turned, 2 * g + p + 1)
                    if tok_out is not None:
                        act.activation(tok_out[:, 2 * g + p, :], row[:, p, :], ACT.Copy)
                    out = col_group(out_T, g, p)
                    if not n_gain:
                        act.activation(out, turned[:, p, 0:D].rearrange("p (c q) -> p c q", c=DC),
                                       ACT.Copy).then_inc(rows_free, 1)
                        continue
                    for c in range(DC):
                        ins = act.activation(out[:, c, :], turned[:, p, c * P:(c + 1) * P], ACT.Identity,
                                             bias=gs[:, 1, c:c + 1] if shift is not None else 0.0,
                                             scale=gs[:, 0, c:c + 1])
                    ins.then_inc(rows_free, 1)


def layer0_mix(nc, st, core, dram, gsT, gateT, last_rows):
    sem = st.sem
    H = 1024
    HC = H // P
    KS = 4
    w_c, w_d, w_g = (st.sb(n, [P, DC, D]) for n in ("w_c", "w_d", "w_g"))
    w_agg, w_bc = st.sb("w_agg", [P, DC, D]), st.sb("w_bc", [P, DC, D])
    w1, w2 = st.sb("w1", [P, DC, H]), st.sb("w2", [P, HC, D])
    cols = st.sb("cols", [P, 5, DC])
    b1 = st.sb("b1", [P, HC])
    rows = st.sb("rows", [B, 6, D])
    ab = st.sb("ab", [P, 2, DC, 64])
    ab_sum = core.ab_sum
    decay_col, decay = st.sb("decay_col", [P, DC]), st.sb("decay", [P, DC, T])
    sig = st.sb("sig", [P, 2, T])
    drive = st.sb("drive", [P, 2, T])
    thought, tnorm = st.sb("thought", [B, D]), st.sb("tnorm", [B, D])
    tT, hT = st.sb("tT", [P, DC, B]), st.sb("hT", [P, HC, B])
    raw, mean, var, rstd = st.sb("traw", [B, 6]), st.sb("tmean", [B, 1]), st.sb("tvar", [B, 1]), st.sb("trstd", [B, 1])
    pC, pD, pG = (st.ps(n, [P, 2, T]) for n in ("pC", "pD", "pG"))
    pS = st.ps("pS", [P, 512])
    pR = st.ps("pR", [P, 512])

    names = ("proj_w_in small_in agg_w_in mlp_w_in last_in c_ready d_ready g_ready sig_ready gate_ready "
             "proj_free sig_used scanned decay_ready setup_step dve_step t_turned t_copied h_ready h_biased h_act "
             "rows_done rstd_ready bc_ready bc_done out_step").split()
    s = {n: sem(n) for n in names}
    TSTEPS = 11

    with nc.Block() as block:
        @block.sync
        def _(sp):
            sp.dma_start(last_rows[:], core.xn[P - 1:P, 3::4, :]
                         ).then_inc(s["last_in"], 16)
            for w, n in ((w_c, "C_wT"), (w_d, "D_wT"), (w_g, "L0_ffn_gate_w")):
                sp.dma_start(w[:], in_chunks(dram[n])).then_inc(s["proj_w_in"], 16)
            for k, n in enumerate(("L0_attn_C_b", "L0_attn_D_b", "L0_ffn_gate_b", "L0_ffn_bc_b",
                                   "L0_attn_log_delta")):
                sp.dma_start(cols[:, k, :], in_chunks(dram[n]),
                             allow_slow_non_contiguous=True).then_inc(s["small_in"], 16)
            sp.dma_start(b1[:], in_chunks(dram["L0_ffn_d1_b"]),
                         allow_slow_non_contiguous=True).then_inc(s["small_in"], 16)
            for k, n in enumerate(("in_gamma", "in_beta", "agg_b", "pn_gamma", "pn_beta", "d2_b")):
                sp.dma_start(rows[:, k, :], on_all_partitions(dram["L0_ffn_" + n], B)).then_inc(s["small_in"], 16)
            for k, n in enumerate("AB"):
                sp.dma_start(ab[:, k, :, :], in_chunks(dram["L0_attn_" + n])).then_inc(s["small_in"], 16)
            for w, n in ((w_agg, "agg_w"), (w_bc, "bc_w")):
                sp.dma_start(w[:], in_chunks(dram["L0_ffn_" + n])).then_inc(s["agg_w_in"], 16)
            for w, n in ((w1, "d1_w"), (w2, "d2_w")):
                sp.dma_start(w[:], in_chunks(dram["L0_ffn_" + n])).then_inc(s["mlp_w_in"], 16)

        SMALL = 16 * 14

        @block.tensor
        def _(pe):
            def turn_rows(n):
                pe.wait_ge(s["dve_step"], (n + 1) * TSTEPS)
                for c in range(DC):
                    ins = pe.transpose(pS[:, B * c:B * c + B], tnorm[:, c * P:(c + 1) * P],
                                       core.ident[0:B, 0:B])
                ins.then_inc(s["t_turned"], 1)
                pe.wait_ge(s["t_copied"], n + 1)

            def add_rows(w, lhs, n_c):
                for c in range(n_c):
                    ins = pe.matmul(pR[0:B, 0:D], lhs[:, c, :], w[:, c, :], start=(c == 0), stop=(c == n_c - 1))
                ins.then_inc(s["rows_done"], 1)

            pe.wait_ge(s["agg_w_in"], 32)
            turn_rows(0)
            add_rows(w_agg, tT, DC)
            pe.wait_ge(s["proj_w_in"], 48)
            pe.wait_ge(s["mlp_w_in"], 32)
            with pe.Fori(0, B) as b:
                for o in range(DC):
                    pe.wait_ge(s["proj_free"], 2 * b + o + 1)
                    for ps, w, name in ((pD, w_d, "d_ready"), (pC, w_c, "c_ready"), (pG, w_g, "g_ready")):
                        for c in range(DC):
                            ins = pe.matmul(ps[:, o, :], w[:, c, o * P:(o + 1) * P],
                                            core.xnT[:, c, bass.ds(b * T, T)], start=(c == 0), stop=(c == DC - 1))
                        ins.then_inc(s[name], 1)
                pe.wait_ge(s["dve_step"], (b + 2) * TSTEPS)
                for c in range(DC):
                    ins = pe.matmul(pS[:, B * c:B * c + B], tnorm[:, c * P:(c + 1) * P],
                                    core.ident[0:B, 0:B], start=True, stop=True)
                ins.then_inc(s["t_turned"], 1)
                pe.wait_ge(s["t_copied"], b + 2)
                for h in range(HC):
                    for c in range(DC):
                        ins = pe.matmul(pS[:, 64 + B * h:64 + B * h + B], w1[:, c, h * P:(h + 1) * P], tT[:, c, :],
                                        start=(c == 0), stop=(c == DC - 1))
                ins.then_inc(s["h_ready"], 1)
                pe.wait_ge(s["h_act"], b + 1)
                add_rows(w2, hT, HC)
            pe.wait_ge(s["out_step"], 1 + 2 * KS)
            for c in range(DC):
                ins = pe.transpose(pS[:, B * c:B * c + B], thought[:, c * P:(c + 1) * P], core.ident[0:B, 0:B])
            ins.then_inc(s["t_turned"], 1)
            pe.wait_ge(s["t_copied"], KS + 2)
            for o in range(DC):
                for c in range(DC):
                    ins = pe.matmul(pR[:, 256 + B * o:256 + B * o + B], w_bc[:, c, o * P:(o + 1) * P], tT[:, c, :],
                                    start=(c == 0), stop=(c == DC - 1))
            ins.then_inc(s["bc_ready"], 1)

        @block.scalar
        def _(act):
            act.wait_ge(s["small_in"], SMALL)
            act.activation(decay_col[:], cols[:, 4, :], ACT.Sigmoid, scale=-1.0).then_inc(s["decay_ready"], 1)
            act.sem_inc(s["sig_used"], 2)
            with act.Fori(0, B) as b:
                for o in range(DC):
                    act.wait_ge(s["d_ready"], 2 * b + o + 1)
                    act.wait_ge(s["sig_used"], 2 * b + o + 3)
                    act.activation(sig[:, o, :], pD[:, o, :], ACT.Sigmoid,
                                   bias=cols[:, 1, o:o + 1]).then_inc(s["sig_ready"], 1)
                    act.wait_ge(s["g_ready"], 2 * b + o + 1)
                    act.activation(gateT[:, o, bass.ds(b * T, T)], pG[:, o, :], ACT.Sigmoid,
                                   bias=cols[:, 2, o:o + 1]).then_inc(s["gate_ready"], 1)
                act.wait_ge(s["h_biased"], b + 1)
                act.activation(hT[:], hT[:], ACT.Gelu).then_inc(s["h_act"], 1)

        @block.gpsimd
        def _(pool):
            for n in range(KS + 1):
                pool.wait_ge(s["dve_step"], n * TSTEPS + 8)
                pool.tensor_tensor(rstd[:], var[:], core.consts[0:B, C_HALF:C_HALF + 1],
                                   ALU.pow).then_inc(s["rstd_ready"], 1)

        @block.vector
        def _(dve):
            dve.sem_inc(s["proj_free"], 2)
            dve.sem_inc(s["sig_used"], 2)
            dve.wait_ge(s["small_in"], SMALL)
            setup_do = Steps(dve, s["setup_step"])
            setup_do(dve.tensor_tensor(ab[:, 0, :, :], ab[:, 0, :, :], ab[:, 1, :, :], ALU.mult))
            setup_do(dve.reduce_sum(ab_sum[:], ab[:, 0, :, :], AX.X))
            setup_do(dve.memset(decay[:], 1.0))
            dve.wait_ge(s["decay_ready"], 1)
            for c in range(DC):
                setup_do(dve.tensor_scalar(decay[:, c, :], decay[:, c, :], decay_col[:, c:c + 1], None, ALU.mult))

            def thought_norm(src, n, gamma, beta, after_stats=None):
                do = Steps(dve, s["dve_step"], n * TSTEPS, TSTEPS)
                do(dve.bn_stats(raw[:], src))
                do(dve.tensor_tensor(mean[:], raw[:, 1:2], raw[:, 4:5], ALU.add))
                do(dve.tensor_tensor(var[:], raw[:, 1:2], raw[:, 4:5], ALU.subtract))
                do(dve.tensor_tensor(var[:], var[:], var[:], ALU.mult))
                do(dve.scalar_tensor_tensor(out=var[:], in0=raw[:, 2:3], scalar=4.0 / D, in1=var[:],
                                            op0=ALU.mult, op1=ALU.add))
                do(dve.scalar_tensor_tensor(out=var[:], in0=raw[:, 5:6], scalar=4.0 / D, in1=var[:],
                                            op0=ALU.mult, op1=ALU.add))
                do(dve.tensor_scalar(mean[:], mean[:], 0.5, None, ALU.mult))
                do(dve.tensor_scalar(var[:], var[:], 0.25, 1e-6, ALU.mult, ALU.add))
                dve.wait_ge(s["rstd_ready"], n + 1)
                do(dve.tensor_scalar(tnorm[:], src, mean[:, 0:1], rstd[:, 0:1], ALU.subtract, ALU.mult))
                do(dve.tensor_tensor(tnorm[:], tnorm[:], rows[:, gamma, :], ALU.mult))
                do(dve.tensor_tensor(tnorm[:], tnorm[:], rows[:, beta, :], ALU.add))
                do.close()

            dve.wait_ge(s["last_in"], 16)
            thought_norm(last_rows[:], 0, 0, 1)
            dve.wait_ge(s["t_turned"], 1)
            dve.tensor_copy(tT[:], pS[:, 0:DC * B].rearrange("p (c b) -> p c b", b=B)).then_inc(s["t_copied"], 1)
            dve.wait_ge(s["rows_done"], 1)
            out_do = Steps(dve, s["out_step"], 0, 1)
            out_do(dve.tensor_tensor(thought[:], pR[0:B, 0:D], rows[:, 2, :], ALU.add))
            with dve.Fori(0, B) as b:
                thought_norm(thought[:], b + 1, 3, 4)
                for o in range(DC):
                    dve.wait_ge(s["c_ready"], 2 * b + o + 1)
                    dve.wait_ge(s["sig_ready"], 2 * b + o + 1)
                    dve.scalar_tensor_tensor(out=drive[:, o, :], in0=pC[:, o, :], scalar=cols[:, 0, o:o + 1],
                                             in1=sig[:, o, :], op0=ALU.add, op1=ALU.mult).then_inc(s["sig_used"], 1)
                    dve.wait_ge(s["sig_used"], 2 * b + o + 5)
                    dve.wait_ge(s["gate_ready"], 2 * b + o + 1)
                    dve.tensor_tensor_scan(gsT[:, o, bass.ds(b * T, T)], decay[:, o, :], drive[:, o, :], 0.0,
                                           ALU.mult, ALU.add).then_inc(s["proj_free"], 1)
                dve.wait_ge(s["t_turned"], b + 2)
                dve.tensor_copy(tT[:], pS[:, 0:DC * B].rearrange("p (c b) -> p c b", b=B)).then_inc(s["t_copied"], 1)
                dve.wait_ge(s["h_ready"], b + 1)
                dve.tensor_tensor(hT[:], pS[:, 64:64 + HC * B].rearrange("p (h b) -> p h b", b=B),
                                  b1[:].unsqueeze(2).to_broadcast([P, HC, B]), ALU.add).then_inc(s["h_biased"], 1)
                dve.wait_ge(s["rows_done"], b + 2)
                out_b = Steps(dve, s["out_step"], 1 + 2 * b, 2)
                out_b(dve.tensor_tensor(thought[:], pR[0:B, 0:D], thought[:], ALU.add))
                out_b(dve.tensor_tensor(thought[:], thought[:], rows[:, 5, :], ALU.add))
                out_b.close()
            dve.wait_ge(s["t_turned"], KS + 2)
            dve.tensor_copy(tT[:], pS[:, 0:DC * B].rearrange("p (c b) -> p c b", b=B)).then_inc(s["t_copied"], 1)
            dve.wait_ge(s["bc_ready"], 1)
            dve.tensor_tensor(core.bcT[:], pR[:, 256:256 + DC * B].rearrange("p (c b) -> p c b", b=B),
                              cols[:, 3, :].unsqueeze(2).to_broadcast([P, DC, B]), ALU.add
                              ).then_inc(s["bc_done"], 1)
            dve.wait_ge(s["bc_done"], 1)
            for c in range(DC):
                for b in range(B):
                    dve.scalar_tensor_tensor(out=gateT[:, c, b * T:(b + 1) * T], in0=gateT[:, c, b * T:(b + 1) * T],
                                             scalar=core.bcT[:, c, b:b + 1], in1=core.xnT[:, c, b * T:(b + 1) * T],
                                             op0=ALU.mult, op1=ALU.add)


def layer0_join(nc, st, core, dram, gsT, ffT):
    sem = st.sem
    y = core.xn
    slot = st.sb("slot", [P, 2, 2 * DC, P])
    gb = st.sb("gb", [P, 2, D])
    raw = st.sb("raw", [P, TILES, 6])
    mean, var, rstd = (st.sb(n, [P, TILES]) for n in ("mean", "var", "rstd"))
    back = st.ps("back", [P, 2, 512])
    gb_in, slot_ready, slot_free, turned = (sem(n) for n in ("gb_in", "slot_ready", "slot_free", "turned"))
    dve_step, rstd_ready = sem("dve_step"), sem("rstd_ready")
    scaled, gained, shifted = (sem(n) for n in ("scaled", "gained", "shifted"))
    with nc.Block() as block:
        @block.sync
        def _(sp):
            for k, n in enumerate(("L0_ffn_out_gamma", "L0_ffn_out_beta")):
                sp.dma_start(gb[:, k, :], on_all_partitions(dram[n], P)).then_inc(gb_in, 16)

        @block.gpsimd
        def _(pool):
            with pool.Fori(0, GROUPS) as g:
                for p in range(2):
                    pool.wait_ge(slot_free, 2 * g + p + 1)
                    for c in range(DC):
                        pool.tensor_tensor(slot[:, p, c, :], col_group(gsT, g, p)[:, c, :],
                                           core.ab_sum[:, c:c + 1].to_broadcast([P, P]), ALU.mult)
                    pool.tensor_copy(slot[:, p, DC:2 * DC, :], col_group(ffT, g, p)).then_inc(slot_ready, 1)
            pool.wait_ge(dve_step, 7)
            pool.tensor_tensor(rstd[:], var[:], core.consts[:, C_HALF:C_HALF + TILES],
                               ALU.pow).then_inc(rstd_ready, 1)

        @block.tensor
        def _(pe):
            with pe.Fori(0, GROUPS) as g:
                for p in range(2):
                    pe.wait_ge(slot_ready, 2 * g + p + 1)
                    for k in range(2 * DC):
                        ins = pe.transpose(back[:, p, k * P:(k + 1) * P], slot[:, p, k, :], core.ident)
                    ins.then_inc(turned, 1)

        @block.vector
        def _(dve):
            dve.sem_inc(slot_free, 2)
            with dve.Fori(0, GROUPS) as g:
                for p in range(2):
                    t = 2 * g + p
                    dve.wait_ge(turned, t + 1)
                    dve.tensor_tensor(core.x[:, t, :], back[:, p, 0:D], core.x[:, t, :], ALU.add)
                    dve.bn_stats(raw[:, t, :], back[:, p, D:2 * D])
                    dve.tensor_copy(y[:, t, :], back[:, p, D:2 * D]).then_inc(slot_free, 1)
            dve.wait_ge(slot_free, TILES + 2)
            do = Steps(dve, dve_step)
            small_stats(do, dve, raw, mean, var, 1e-6, False)
            dve.wait_ge(rstd_ready, 1)
            dve.wait_ge(gb_in, 32)
            with dve.Fori(0, GROUPS) as g:
                for p in range(2):
                    t = 2 * g + p
                    dve.tensor_scalar(y[:, t, :], y[:, t, :], mean[:, bass.ds(t, 1)], rstd[:, bass.ds(t, 1)],
                                      ALU.subtract, ALU.mult).then_inc(scaled, 1)
                pair = y[:, bass.ds(2 * g, 2), :]
                dve.wait_ge(scaled, 2 * g + 2)
                dve.tensor_tensor(pair, pair, gb[:, 0, :].unsqueeze(1).to_broadcast([P, 2, D]),
                                  ALU.mult).then_inc(gained, 1)
                dve.wait_ge(gained, g + 1)
                dve.tensor_tensor(pair, pair, gb[:, 1, :].unsqueeze(1).to_broadcast([P, 2, D]),
                                  ALU.add).then_inc(shifted, 1)
                dve.wait_ge(shifted, g + 1)
                dve.tensor_tensor(core.x[:, bass.ds(2 * g, 2), :], pair, core.x[:, bass.ds(2 * g, 2), :], ALU.add)


def layer1_attention(nc, st, core):
    sem = st.sem
    HD, H2 = 16, 8
    keys = st.sb("keys", [P, 2, DC, P])
    vals = st.sb("vals", [P, 2, H2, HD + 1])
    e = st.sb("e", [P, 2, H2, P])
    inv, part = st.sb("inv", [P, 2, H2]), st.sb("part", [P, 2, H2, HD])
    ps = st.ps("scores", [P, 4, 2, DC, P])
    po = st.ps("out", [P, 2, 512])
    ones, keys_ready, vals_ready, scores_ready = (sem(n) for n in ("ones", "keys_ready", "vals_ready", "scores_ready"))
    exp_ready, masked, out_ready, inv_ready, scaled, tile_done = (sem(n) for n in (
        "exp_ready", "masked", "out_ready", "inv_ready", "scaled", "tile_done"))
    heads = [(c, j) for c in range(DC) for j in range(4)]

    def own(t, p):
        return t.rearrange("q (h two d) -> q h two d", two=2, d=HD)[:, :, p, :]

    with nc.Block() as block:
        @block.gpsimd
        def _(pool):
            pool.memset(vals[:], 1.0).then_inc(ones, 1)
            pool.wait_ge(ones, 1)
            with pool.Fori(0, GROUPS) as g:
                for p in range(2):
                    pool.wait_ge(tile_done, 2 * g + p + 1)
                    pool.tensor_tensor(keys[:, p, :, :], col_group(core.xnT, g, p),
                                       core.consts[:, C_EVEN + p:C_EVEN + p + 1].unsqueeze(2).to_broadcast([P, DC, P]),
                                       ALU.mult).then_inc(keys_ready, 1)
                    pool.tensor_copy(vals[:, p, :, 0:HD],
                                     own(core.xn[:, bass.ds(2 * g + p, 1), :].rearrange("q t d -> q (t d)"), p)
                                     ).then_inc(vals_ready, 1)

        @block.tensor
        def _(pe):
            with pe.Fori(0, GROUPS) as g:
                for p in range(2):
                    n = 2 * g + p
                    pe.wait_ge(keys_ready, n + 1)
                    for h, (c, j) in enumerate(heads):
                        rows = keys[32 * j:32 * j + 32, p, c, :]
                        ins = pe.matmul(ps[:, j, p, c, :], rows, rows, start=True, stop=True)
                    ins.then_inc(scores_ready, 1)
                    pe.wait_ge(masked, n + 1)
                    pe.wait_ge(vals_ready, n + 1)
                    for h in range(H2):
                        ins = pe.matmul(po[:, p, h * (HD + 1):(h + 1) * (HD + 1)], e[:, p, h, :], vals[:, p, h, :],
                                        start=True, stop=True)
                    ins.then_inc(out_ready, 1)

        @block.scalar
        def _(act):
            act.preload_act_table(ACT.Exp)
            with act.Fori(0, GROUPS) as g:
                for p in range(2):
                    act.wait_ge(scores_ready, 2 * g + p + 1)
                    act.activation(e[:, p, :, :].rearrange("q (c j) k -> q j c k", c=DC), ps[:, :, p, :, :], ACT.Exp,
                                   scale=HD ** -0.5).then_inc(exp_ready, 1)

        @block.vector
        def _(dve):
            dve.sem_inc(tile_done, 2)
            with dve.Fori(0, GROUPS) as g:
                for p in range(2):
                    n = 2 * g + p
                    dve.wait_ge(exp_ready, n + 1)
                    dve.tensor_tensor(e[:, p, :, :], e[:, p, :, :], core.blk.unsqueeze(1).to_broadcast([P, H2, P]),
                                      ALU.mult).then_inc(masked, 1)
                    dve.wait_ge(out_ready, n + 1)
                    o = po[:, p, 0:H2 * (HD + 1)].rearrange("q (h d) -> q h d", h=H2)
                    dve.reciprocal(inv[:, p, :], o[:, :, HD]).then_inc(inv_ready, 1)
                    dve.wait_ge(inv_ready, n + 1)
                    dve.tensor_tensor(part[:, p, :, :], o[:, :, 0:HD],
                                      inv[:, p, :].unsqueeze(2).to_broadcast([P, H2, HD]), ALU.mult
                                      ).then_inc(scaled, 1)
                    dve.wait_ge(scaled, n + 1)
                    x = own(core.x[:, bass.ds(n, 1), :].rearrange("q t d -> q (t d)"), p)
                    dve.tensor_tensor(x, x, part[:, p, :, :], ALU.add).then_inc(tile_done, 1)


def layer2_abc(nc, st, core, dram):
    sem = st.sem
    HP, DK, DV, NCH = 8, 64, 128, TB
    PV = 2 * DV
    PER = 2 * B
    ROUNDS = HP // 2
    ones = st.sb("ones", [P, T])
    w_qks, w_vg, w_o = st.sb("w_qks", [P, 2, 3, DC, P]), st.sb("w_vg", [P, 2, 2, DC, PV]), st.sb("w_o", [P, 2, 2, D])
    gnorm = st.sb("gnorm", [P, 1])
    qT, kT, eT = (st.sb(n, [P, 2, T]) for n in ("qT", "kT", "eT"))
    sT, cT, rT = (st.sb(n, [P, T]) for n in ("sT", "cT", "rT"))
    k_tok, e_tok, r_tok = (st.sb(n, [P, 2, NCH, P]) for n in ("k_tok", "e_tok", "r_tok"))
    v, gate = (st.sb(n, [P, 2, NCH, PV]) for n in ("v", "gate"))
    th = st.sb("th", [P, NCH, PV])
    sm, am = st.sb("sm", [P, 2, NCH, P]), st.sb("am", [P, 2, NCH, P])
    hk, hv = st.sb("hk", [P, 3, P]), st.sb("hv", [P, 3, DV])
    lg, ex, wt = (st.sb(n, [P, NCH, P]) for n in ("lg", "ex", "wt"))
    wT = st.sb("wT", [P, T])
    mx, den = st.sb("mx", [P, 8]), st.sb("den", [P, 8])
    sq, on, gr = (st.sb(n, [P, 2, NCH, DV]) for n in ("sq", "on", "gr"))
    ms, rstd = st.sb("ms", [P, 8]), st.sb("rstd", [P, 8])
    oT = st.sb("oT", [P, 2, T])
    ring = [st.ps(f"ring{k}", [P, T]) for k in range(3)]
    pab = st.ps("pab", [P, 2, T])
    pc = st.ps("pc", [P, T])
    pde = st.ps("pde", [P, 2, T])
    names = ("once_in q_ready k_ready s_ready v_ready g_ready q_copied k_copied s_clipped e_ready "
             "c_ready r_ready v_copied tanh_ready gate_ready k_turned e_turned r_turned k_tok_ready e_tok_ready "
             "r_tok_ready scores_ready sm_ready hk_sums hk_step ok_ready hv_sums hv_step zeros logit_step ex_ready "
             "er_ready den_step wt_ready w_turned wT_ready am_sums am_ready ov_ready sq_ready ms_step rstd_ready "
             "gr_ready on_ready o_turned oT_ready y_ready y_added").split()
    s = {n: sem(n) for n in names}
    w_in = [sem("w0_in"), sem("w1_in")]
    FILL = {n: k for k, n in enumerate("q k s v0 v1 g0 g1 kt et rt hv".split())}
    taken_by = ("q_copied", "k_copied", "s_clipped", "v_copied", "v_copied", "gate_ready", "gate_ready",
                "k_tok_ready", "e_tok_ready", "r_tok_ready", "hv_step")
    per_unit = {"v_copied": 2, "gate_ready": 2, "hv_step": 3, "v_ready": 2, "g_ready": 2, "tanh_ready": 2}

    def bank(name):
        return ring[FILL[name] % 3]

    def chunks(a):
        return a.rearrange("t (c m) -> t c m", c=NCH)

    pst = pab[:].rearrange("j h (c t) -> j h c t", c=NCH)
    pov = pde[:].rearrange("t h (c v) -> t h c v", c=NCH)
    pyy = pab[:].rearrange("t b (c v) -> t (b c) v", v=PV)
    heads8 = lambda a: a.rearrange("t c (h m) -> t (c h) m", h=2)

    def load(sp, slot, hp):
        for k, n in enumerate(("Wq", "Wk", "Ws")):
            sp.dma_start(w_qks[:, slot, k, :, :], in_chunks(dram["L2_attn_" + n])[:, :, bass.ds(hp * P, P)]
                         ).then_inc(w_in[slot], 16)
        for k, n in enumerate(("Wv", "Wg")):
            sp.dma_start(w_vg[:, slot, k, :, :], in_chunks(dram["L2_attn_" + n])[:, :, bass.ds(hp * PV, PV)]
                         ).then_inc(w_in[slot], 16)
        sp.dma_start(w_o[:, slot, :, :], in_chunks(dram["L2_attn_Wo"])[:, bass.ds(hp * 2, 2), :]
                     ).then_inc(w_in[slot], 16)

    def rounds(eng, unit):
        for k in range(PER):
            unit(k, k, k == 0, False)
        with eng.Fori(1, ROUNDS - 1) as i:
            for k in range(PER):
                unit(i * PER + k, k, False, False)
        for k in range(PER):
            unit((ROUNDS - 1) * PER + k, k, False, k == PER - 1)

    with nc.Block() as block:
        @block.sync
        def _(sp):
            sp.dma_start(gnorm[:], dram["L2_attn_g_norm_weight"].unsqueeze(1),
                         allow_slow_non_contiguous=True).then_inc(s["once_in"], 16)
            for slot in range(2):
                load(sp, slot, slot)
            with sp.Fori(1, ROUNDS) as i:
                for slot in range(2):
                    sp.wait_ge(s["y_ready"], (i - 1) * PER + (slot + 1) * B)
                    load(sp, slot, i * 2 + slot)

        @block.gpsimd
        def _(pool):
            pool.memset(ones[:], 1.0).then_inc(s["zeros"], 1)
            pool.memset(hk[:], 0.0).then_inc(s["zeros"], 1)

            def unit(u, k, first, last):
                pool.wait_ge(s["ex_ready"], u + 1)
                pool.wait_ge(s["r_tok_ready"], u + 1)
                pool.tensor_tensor(wt[:], ex[:], r_tok[:, k % 2], ALU.mult).then_inc(s["er_ready"], 1)
                pool.wait_ge(s["ms_step"], 2 * (u + 1))
                pool.tensor_tensor(rstd[:], ms[:], core.consts[:, C_HALF:C_HALF + 8], ALU.pow
                                   ).then_inc(s["rstd_ready"], 1)
                pool.wait_ge(s["rstd_ready"], u + 1)
                pool.wait_ge(s["gate_ready"], 2 * (u + 1))
                pool.tensor_tensor(gr[:].rearrange("t h c v -> t c h v"),
                                   gate[:, k % 2].rearrange("t c (h v) -> t c h v", h=2),
                                   rstd[:].rearrange("t (h c) -> t c h", h=2).unsqueeze(3).to_broadcast(
                                       [P, NCH, 2, DV]), ALU.mult).then_inc(s["gr_ready"], 1)

            rounds(pool, unit)

        @block.tensor
        def _(pe):
            pe.wait_ge(s["zeros"], 2)

            def ring_free(name, u):
                n = FILL[name]
                if n >= 3:
                    by = taken_by[n - 3]
                    per = per_unit.get(by, 1)
                    step = 1 if n - 3 in (FILL["v0"], FILL["g0"]) else per
                    pe.wait_ge(s[by], per * u + step)
                else:
                    if isinstance(u, int) and u == 0:
                        return
                    by = {0: "r_tok_ready", 1: "hv_step", 2: "e_tok_ready"}[n]
                    per = per_unit.get(by, 1)
                    pe.wait_ge(s[by], per * u)

            def project_rows(name, u, k):
                b, slot = k % B, (k // B) % 2
                if name == "q" and b == 0:
                    pe.wait_ge(w_in[slot], ((u - k) // PER + 1) * 96 if isinstance(u, int) else weights_round(u, k))
                ring_free(name, u)
                for c in range(DC):
                    ins = pe.matmul(bank(name)[:], w_qks[:, slot, FILL[name], c, :],
                                    core.xnT[:, c, b * T:(b + 1) * T], start=(c == 0), stop=(c == DC - 1))
                ins.then_inc(s[name + "_ready"], 1)

            def project_tokens(name, half, u, k):
                b, slot = k % B, (k // B) % 2
                fill = name + str(half)
                ring_free(fill, u)
                for t in range(2):
                    at = b * T + (2 * half + t) * P
                    for c in range(DC):
                        ins = pe.matmul(bank(fill)[:, t * PV:(t + 1) * PV], core.xnT[:, c, at:at + P],
                                        w_vg[:, slot, "vg".index(name), c, :], start=(c == 0), stop=(c == DC - 1))
                ins.then_inc(s[name + "_ready"], 1)

            def turn(fill, src, need, done, u):
                ring_free(fill, u)
                pe.wait_ge(s[need], u + 1)
                for t in range(NCH):
                    ins = pe.transpose(bank(fill)[:, t * P:(t + 1) * P], src[:, t * P:(t + 1) * P], core.ident)
                ins.then_inc(s[done], 1)

            def scores(u, k):
                pe.wait_ge(s["k_copied"], u + 1)
                pe.wait_ge(s["q_copied"], u + 1)
                if not (isinstance(u, int) and u == 0):
                    pe.wait_ge(s["am_ready"], u)
                for c in range(NCH):
                    for h in range(2):
                        rows, cols = slice(DK * h, DK * h + DK), slice(c * P, (c + 1) * P)
                        ins = pe.matmul(pst[:, h, c, :], kT[rows, k % 2, cols], qT[rows, k % 2, cols],
                                        start=True, stop=True)
                ins.then_inc(s["scores_ready"], 1)

            def chunk_sums(u, k):
                pe.wait_ge(s["k_tok_ready"], u + 1)
                pe.wait_ge(s["e_tok_ready"], u + 1)
                if not (isinstance(u, int) and u == 0):
                    pe.wait_ge(s["wT_ready"], u)
                for c in range(3):
                    ins = pe.matmul(pc[:, c * P:(c + 1) * P], k_tok[:, k % 2, c, :], e_tok[:, k % 2, c, :],
                                    start=True, stop=True)
                ins.then_inc(s["hk_sums"], 1)
                pe.wait_ge(s["v_copied"], 2 * (u + 1))
                for c in range(3):
                    for h in range(2):
                        ins = pe.matmul(bank("hv")[DK * h:DK * h + DK, c * DV:(c + 1) * DV],
                                        e_tok[:, k % 2, c, DK * h:DK * h + DK],
                                        v[:, k % 2, c, DV * h:DV * h + DV], start=True, stop=True)
                ins.then_inc(s["hv_sums"], 1)

            def turn_out(u):
                pe.wait_ge(s["on_ready"], u + 1)
                for h in range(2):
                    for c in range(NCH):
                        ins = pe.transpose(pde[:, h, c * P:(c + 1) * P], on[:, h, c, :], core.ident)
                ins.then_inc(s["o_turned"], 1)

            def emit(u, k):
                slot = (k // B) % 2
                pe.wait_ge(s["oT_ready"], u + 1)
                for t in range(NCH):
                    for h in range(2):
                        cols = oT[:, h, :].rearrange("d (g q p) -> d g p q", q=P, p=2)[:, t // 2, t % 2, :]
                        ins = pe.matmul(pyy[:, t, :], cols, w_o[:, slot, h, :], start=(h == 0), stop=(h == 1))
                ins.then_inc(s["y_ready"], 1)

            def ok(u, k):
                pe.wait_ge(s["sm_ready"], u + 1)
                pe.wait_ge(s["hk_step"], 6 * (u + 1))
                tok4 = chunks(pc[:])
                for c in range(NCH):
                    if c:
                        pe.matmul(tok4[:, c, :], qT[:, k % 2, c * P:(c + 1) * P], hk[:, c - 1, :], start=True,
                                  stop=False, skip_group_check=True)
                    for h in range(2):
                        m = slice(DK * h, DK * h + DK)
                        ins = pe.matmul(tok4[:, c, m], sm[:, h, c, :], e_tok[:, k % 2, c, m], start=(c == 0),
                                        stop=True, skip_group_check=True)
                ins.then_inc(s["ok_ready"], 1)

            def turn_w(u):
                pe.wait_ge(s["wt_ready"], u + 1)
                for t in range(NCH):
                    ins = pe.transpose(pc[:, t * P:(t + 1) * P], wt[:, t, :], core.ident)
                ins.then_inc(s["w_turned"], 1)

            def weights(u, k):
                pe.wait_ge(s["wT_ready"], u + 1)
                if not (isinstance(u, int) and u == 0):
                    pe.wait_ge(s["y_added"], u)
                for c in range(NCH):
                    for h in range(2):
                        rows, cols = slice(DK * h, DK * h + DK), slice(c * P, (c + 1) * P)
                        ins = pe.matmul(pst[:, h, c, :], eT[rows, k % 2, cols], wT[rows, cols], start=True, stop=True)
                ins.then_inc(s["am_sums"], 1)

            def ov(u, k):
                pe.wait_ge(s["hv_step"], 3 * (u + 1))
                pe.wait_ge(s["am_ready"], u + 1)
                for c in range(NCH):
                    for h in range(2):
                        rows = slice(DK * h, DK * h + DK)
                        if c:
                            pe.matmul(pov[:, h, c, :], wT[rows, c * P:(c + 1) * P], hv[rows, c - 1, :],
                                      start=True, stop=False)
                        ins = pe.matmul(pov[:, h, c, :], am[:, h, c, :], v[:, k % 2, c, DV * h:DV * h + DV],
                                        start=(c == 0), stop=True)
                ins.then_inc(s["ov_ready"], 1)

            def weights_round(u, k):
                return u * (96 // PER) + (96 - k * (96 // PER))

            def part(steps, u, k):
                for x in steps.split():
                    if x in ("q", "k", "s"):
                        project_rows(x, u, k)
                    elif x[0] in "vg":
                        project_tokens(x[0], int(x[1]), u, k)
                    elif x == "kt":
                        turn("kt", kT[:, k % 2], "k_copied", "k_turned", u)
                    elif x == "et":
                        turn("et", eT[:, k % 2], "e_ready", "e_turned", u)
                    else:
                        turn("rt", rT[:], "r_ready", "r_turned", u)

            def unit(u, k, first, last):
                kn = (k + 1) % PER

                def project(steps):
                    if not last:
                        part(steps, u + 1, kn)

                scores(u, k)
                chunk_sums(u, k)
                project("q")
                if not first:
                    turn_out(u - 1)
                project("k s")
                if not first:
                    pe.wait_ge(s["sm_ready"], u + 1)
                    emit(u - 1, (k - 1) % PER)
                ok(u, k)
                project("v0 v1 g0")
                turn_w(u)
                project("g1")
                weights(u, k)
                project("kt et")
                ov(u, k)
                project("rt")

            part("q k s v0 v1 g0 g1 kt et rt", 0, 0)
            rounds(pe, unit)
            turn_out(HP * B - 1)
            emit(HP * B - 1, PER - 1)

        @block.scalar
        def _(act):
            act.preload_act_table(ACT.Exp)
            act.wait_ge(s["once_in"], 16)

            def copy(ready, n, out, in_, done, **kw):
                act.wait_ge(s[ready], n)
                act.activation(out, in_, ACT.Copy, **kw).then_inc(s[done], 1)

            def project_qe(u, k):
                copy("q_ready", u + 1, qT[:, k % 2], bank("q")[:], "q_copied", scale=DK ** -0.5)

            def project_e(u, k):
                act.wait_ge(s["s_clipped"], u + 1)
                act.activation(eT[:, k % 2], sT[:], ACT.Exp).then_inc(s["e_ready"], 1)

            def project_v(u, k):
                for half in range(2):
                    copy("v_ready", 2 * u + half + 1, v[:, k % 2, 2 * half:2 * half + 2],
                         bank(f"v{half}")[:].rearrange("t (c v) -> t c v", v=PV), "v_copied")

            def project_g(u, k, half):
                act.wait_ge(s["g_ready"], 2 * u + half + 1)
                act.activation(th[:, 2 * half:2 * half + 2], bank(f"g{half}")[:].rearrange("t (c v) -> t c v", v=PV),
                               ACT.Tanh, scale=0.5).then_inc(s["tanh_ready"], 1)

            def project_turned(u, k, names):
                for x, dst, n in (("kt", k_tok, "k"), ("et", e_tok, "e"), ("rt", r_tok, "r")):
                    if x in names:
                        copy(n + "_turned", u + 1, dst[:, k % 2], chunks(bank(x)[:]), n + "_tok_ready")

            def emit(u):
                act.wait_ge(s["o_turned"], u + 1)
                act.activation(oT[:], pde[:], ACT.Copy, scale=gnorm[:, 0:1]).then_inc(s["oT_ready"], 1)

            def unit(u, k, first, last):
                n, kn = u + 1, (k + 1) % PER
                if not last:
                    project_qe(n, kn)
                if not first:
                    emit(u - 1)
                if not last:
                    project_e(n, kn)
                act.wait_ge(s["logit_step"], 3 * (u + 1))
                act.activation(ex[:], lg[:], ACT.Exp).then_inc(s["ex_ready"], 1)
                if not last:
                    project_v(n, kn)
                    project_g(n, kn, 0)
                copy("w_turned", u + 1, wT[:], pc[:], "wT_ready")
                if not last:
                    project_g(n, kn, 1)
                    project_turned(n, kn, ("kt", "et"))
                act.wait_ge(s["ov_ready"], u + 1)
                act.activation(sq[:], pov, ACT.Square).then_inc(s["sq_ready"], 1)
                if not last:
                    project_turned(n, kn, ("rt",))

            project_qe(0, 0)
            project_e(0, 0)
            project_v(0, 0)
            project_g(0, 0, 0)
            project_g(0, 0, 1)
            project_turned(0, 0, ("kt", "et", "rt"))
            rounds(act, unit)
            emit(HP * B - 1)

        @block.vector
        def _(dve):
            dve.wait_ge(s["zeros"], 2)
            tri8 = core.tri.unsqueeze(1).to_broadcast([P, NCH, P])

            def project_ks(u, k):
                dve.wait_ge(s["k_ready"], u + 1)
                dve.tensor_copy(kT[:, k % 2], bank("k")[:]).then_inc(s["k_copied"], 1)
                dve.wait_ge(s["s_ready"], u + 1)
                dve.tensor_scalar(sT[:], bank("s")[:], 32.0, -32.0, ALU.min, ALU.max).then_inc(s["s_clipped"], 1)

            def project_c(u, k):
                dve.wait_ge(s["e_ready"], u + 1)
                dve.tensor_tensor_scan(cT[:], ones[:], eT[:, k % 2], 0.0, ALU.mult, ALU.add).then_inc(s["c_ready"], 1)
                dve.wait_ge(s["c_ready"], u + 1)
                dve.reciprocal(rT[:], cT[:]).then_inc(s["r_ready"], 1)

            def project_g(u, k, half):
                c = slice(2 * half, 2 * half + 2)
                dve.wait_ge(s["tanh_ready"], 2 * u + half + 1)
                dve.scalar_tensor_tensor(out=gate[:, k % 2, c], in0=th[:, c], scalar=1.0,
                                         in1=bank(f"g{half}")[:].rearrange("t (c v) -> t c v", v=PV),
                                         op0=ALU.add, op1=ALU.mult).then_inc(s["gate_ready"], 1)

            def mask(ready, dst, done, u):
                dve.wait_ge(s[ready], u + 1)
                for h in range(2):
                    ins = dve.tensor_tensor(dst[:, h], pst[:, h], tri8, ALU.mult)
                ins.then_inc(s[done], 1)

            def prefix(u):
                dve.wait_ge(s["hk_sums"], u + 1)
                do = Steps(dve, s["hk_step"], 6 * u, 6)
                for c in range(3):
                    for h in range(2):
                        r = slice(DK * h, DK * h + DK)
                        new = pc[r, c * P + DK * h:c * P + DK * h + DK]
                        if c:
                            do(dve.tensor_tensor(hk[r, c, r], new, hk[r, c - 1, r], ALU.add))
                        else:
                            do(dve.tensor_copy(hk[r, c, r], new))
                do.close()
                dve.wait_ge(s["hv_sums"], u + 1)
                do = Steps(dve, s["hv_step"], 3 * u, 3)
                for c in range(3):
                    new = bank("hv")[:, c * DV:(c + 1) * DV]
                    if c:
                        do(dve.tensor_tensor(hv[:, c, :], new, hv[:, c - 1, :], ALU.add))
                    else:
                        do(dve.tensor_copy(hv[:, c, :], new))
                do.close()

            def mean_square(u):
                dve.wait_ge(s["sq_ready"], u + 1)
                do = Steps(dve, s["ms_step"], 2 * u, 2)
                do(dve.reduce_sum(ms[:], sq[:].rearrange("t h c v -> t (h c) v"), AX.X))
                do(dve.tensor_scalar(ms[:], ms[:], 4.0 / DV, 4e-5, ALU.mult, ALU.add))
                do.close()

            def gated(u):
                dve.wait_ge(s["gr_ready"], u + 1)
                dve.tensor_tensor(on[:], pov, gr[:], ALU.mult).then_inc(s["on_ready"], 1)

            def emit(u, k):
                dve.wait_ge(s["y_ready"], u + 1)
                b = k % B
                x = core.x[:, 4 * b:4 * b + 4, :]
                dve.tensor_tensor(x, pyy, x, ALU.add).then_inc(s["y_added"], 1)

            def unit(u, k, first, last):
                n, kn = u + 1, (k + 1) % PER
                mask("scores_ready", sm, "sm_ready", u)
                prefix(u)
                if not first:
                    gated(u - 1)
                if not last:
                    project_ks(n, kn)
                dve.wait_ge(s["ok_ready"], u + 1)
                dve.wait_ge(s["r_tok_ready"], u + 1)
                do = Steps(dve, s["logit_step"], 3 * u, 3)
                do(dve.tensor_tensor(lg[:], chunks(pc[:]), r_tok[:, k % 2], ALU.mult))
                do(dve.tensor_reduce(mx[:], heads8(lg[:]), AX.X, ALU.max))
                do(dve.tensor_tensor(heads8(lg[:]), heads8(lg[:]), mx[:].unsqueeze(2).to_broadcast([P, 8, DK]),
                                     ALU.subtract))
                do.close()
                if not first:
                    emit(u - 1, (k - 1) % PER)
                dve.wait_ge(s["ex_ready"], u + 1)
                do = Steps(dve, s["den_step"], 2 * u, 2)
                do(dve.reduce_sum(den[:], heads8(ex[:]), AX.X))
                do(dve.reciprocal(den[:], den[:]))
                do.close()
                dve.wait_ge(s["er_ready"], u + 1)
                dve.tensor_tensor(heads8(wt[:]), heads8(wt[:]), den[:].unsqueeze(2).to_broadcast([P, 8, DK]),
                                  ALU.mult).then_inc(s["wt_ready"], 1)
                if not last:
                    project_g(n, kn, 0)
                    project_c(n, kn)
                    project_g(n, kn, 1)
                mask("am_sums", am, "am_ready", u)
                mean_square(u)

            project_ks(0, 0)
            project_c(0, 0)
            project_g(0, 0, 0)
            project_g(0, 0, 1)
            rounds(dve, unit)
            gated(HP * B - 1)
            emit(HP * B - 1, PER - 1)


def layer2_attention(nc, st, core, dram, aT):
    sem = st.sem
    H, LAT = 16, 64
    w_kvq = st.sb("w_kvq", [P, DC, P])
    w_low = st.sb("w_low", [P, 2, D])
    w_kr, w_kt = st.sb("w_kr", [P, DC, D]), st.sb("w_kt", [P, DC, D])
    w_o = st.sb("w_o", [P, DC, D])
    rope = st.sb("rope", [P, 2, T])
    low = st.sb("low", [P, T])
    turn = st.sb("turn", [P, 2, T])
    qT, kT = st.sb("qT", [P, DC, T]), st.sb("kT", [P, DC, T])
    keys = st.sb("keys", [P, 2, DC, T])
    v = st.sb("v", [P, 2, TB, D])
    r32 = mybir.dt.float32r
    mask = st.scope.enter_context(nc.sbuf_tensor(st.name + "_mask", [P, 2, P], r32))
    pr, prT = st.sb("pr", [P, 2, TB, T]), st.sb("prT", [P, 2, TB, T])
    nmax = st.sb("nmax", [P, 2, TB])
    total = st.sb("total", [P, H, TB])
    sums, o, oT = st.sb("sums", [P, DC, T]), st.sb("o", [P, TB, D]), st.sb("oT", [P, DC, T])
    pa, pw, po = st.ps("pa", [P, 4, T]), st.ps("pw", [P, 2, T]), st.ps("po", [P, DC, T])
    (w_in, low_ready, low_copied, rot_ready, rot_step, rot_done, keys_ready, v_ready, v_copied, scores_ready,
     max_ready, exp_ready, turned, even_copied, odd_copied, heads_out, zeros, mask_ready, sums_copied, sums_turned,
     norm_step, o_turned, o_copied, y_ready, y_added, joined) = (
        sem(n) for n in ("w_in low_ready low_copied rot_ready rot_step rot_done keys_ready v_ready v_copied "
                         "scores_ready max_ready exp_ready turned even_copied odd_copied heads_out zeros mask_ready "
                         "sums_copied sums_turned norm_step "
                         "o_turned o_copied y_ready y_added joined").split())
    loads = [(w_kvq[:], in_chunks(dram["L2_kvq_d"])), (w_low[0:LAT, 0, :], dram["L2_k_plain"]),
             (w_low[0:LAT, 1, :], dram["L2_ffn_v_u_w"]), (w_low[LAT:P, 0, :], dram["L2_q_both"]),
             (w_low[LAT:P, 1, :], dram["L2_q_turned"]), (w_kr[:], in_chunks(dram["L2_k_rope"])),
             (w_kt[:], in_chunks(dram["L2_k_turned"])), (w_o[:], in_chunks(dram["L2_ffn_o_w"])),
             (rope[:], dram["rope"].rearrange("k p t -> p k t"))]
    po_T, py = pa[:, 0:DC, :], pa[:, 2:4, :].rearrange("q a (t d) -> q (a t) d", d=D)
    po_v = po[:].rearrange("q a (t d) -> q (a t) d", d=D)
    pw_tok = pw[:].rearrange("q a (t d) -> q (a t) d", d=D)
    copied = (even_copied, odd_copied)

    def own(t, p):
        return t.rearrange("q t (h two d) -> q t h two d", two=2, d=16)[:, :, :, p, :]
    with nc.Block() as block:
        @block.sync
        def _(sp):
            for dst, src in loads:
                sp.dma_start(dst, src).then_inc(w_in, 16)

        @block.tensor
        def _(pe):
            pe.wait_ge(w_in, 16 * len(loads))

            def scores(b, h, k):
                q = QB_ORDER[k]
                c, j, other = h // 8, (h % 8) // 2, h % 2
                rows = slice(32 * j, 32 * j + 32)
                n = (q + 1) * P
                if h:
                    pe.wait_ge(exp_ready, TB * H * b + TB * (h - 1) + k + 1)
                pe.matmul(pa[:, q, 0:n], qT[rows, c, q * P:(q + 1) * P], keys[rows, other, c, 0:n],
                          start=True, stop=False, skip_group_check=True)
                pe.matmul(pa[:, q, n - P:n], mask[:, 0, :], mask[:, 1, :], start=False, stop=True,
                          skip_group_check=True).then_inc(scores_ready, 1)

            def turn(b, h, k):
                n = H * b + h
                pe.wait_ge(exp_ready, TB * (n + 1))
                pe.wait_ge(copied[k % 2], 2 * n + k // 2 + 1)
                for q in range(k, TB):
                    ins = pe.transpose(pw[:, k % 2, q * P:(q + 1) * P], pr[:, h % 2, q, k * P:(k + 1) * P], core.ident)
                ins.then_inc(turned, 1)

            def values(b, h, k):
                n = H * b + h
                pe.wait_ge(copied[k % 2], 2 * n + k // 2 + 2)
                pair = h // 2
                ins = pe.matmul(po[32 * (pair % 4):32 * (pair % 4) + 32, pair // 4, k * P:T],
                                v[:, h % 2, k, 32 * pair:32 * pair + 32], prT[:, h % 2, k, k * P:T],
                                start=(h % 2 == 0 and k == 0), stop=(h % 2 == 1 and k == TB - 1),
                                skip_group_check=True)
                if k == TB - 1:
                    ins.then_inc(heads_out, 1)

            with pe.Fori(0, B) as b:
                x = [aT[:, c, bass.ds(b * T, T)] for c in range(DC)]
                for c in range(DC):
                    ins = pe.matmul(pw[:, 0, :], w_kvq[:, c, :], x[c], start=(c == 0), stop=(c == DC - 1))
                ins.then_inc(low_ready, 1)
                pe.wait_ge(low_copied, b + 1)
                for o_ in range(DC):
                    cols = slice(o_ * P, (o_ + 1) * P)
                    if o_ == 1:
                        pe.wait_ge(y_added, b + 1)
                    pe.matmul(pa[:, 2 * o_, :], w_low[0:LAT, 0, cols], low[0:LAT, :], start=True, stop=False)
                    for c in range(DC):
                        pe.matmul(pa[:, 2 * o_, :], w_kr[:, c, cols], x[c], start=False, stop=(c == DC - 1))
                    for c in range(DC):
                        ins = pe.matmul(pa[:, 2 * o_ + 1, :], w_kt[:, c, cols], x[c], start=(c == 0),
                                        stop=(c == DC - 1))
                    ins.then_inc(rot_ready, 1)
                for t in range(TB):
                    ins = pe.matmul(po_v[:, t, :], low[0:LAT, t * P:(t + 1) * P], w_low[0:LAT, 1, :],
                                    start=True, stop=True)
                ins.then_inc(v_ready, 1)
                for o_ in range(DC):
                    cols = slice(o_ * P, (o_ + 1) * P)
                    pe.wait_ge(rot_done, 4 * b + o_ + 1)
                    for k in range(2):
                        ins = pe.matmul(pa[:, 2 * o_ + k, :], w_low[LAT:P, k, cols], low[LAT:P, :],
                                        start=True, stop=True)
                    ins.then_inc(rot_ready, 1)
                pe.wait_ge(keys_ready, 2 * (b + 1))
                pe.wait_ge(rot_done, 4 * (b + 1))
                pe.wait_ge(v_copied, b + 1)
                pe.wait_ge(mask_ready, 2)
                for h in range(H + 2):
                    if h < H:
                        for k in range(TB):
                            scores(b, h, k)
                    for k in range(0, TB, 2):
                        if 1 <= h <= H:
                            turn(b, h - 1, k)
                            turn(b, h - 1, k + 1)
                        if h >= 2:
                            values(b, h - 2, k)
                            values(b, h - 2, k + 1)
                pe.wait_ge(sums_copied, b + 1)
                for t in range(TB):
                    for c in range(DC):
                        ins = pe.transpose(pw_tok[:, t, c * P:(c + 1) * P], sums[:, c, t * P:(t + 1) * P], core.ident)
                ins.then_inc(sums_turned, 1)
                pe.wait_ge(norm_step, 2 * (b + 1))
                for t in range(TB):
                    for c in range(DC):
                        ins = pe.transpose(po_T[:, c, t * P:(t + 1) * P], o[:, t, c * P:(c + 1) * P], core.ident)
                ins.then_inc(o_turned, 1)
                pe.wait_ge(o_copied, b + 1)
                for t in range(TB):
                    for c in range(DC):
                        cols = oT[:, c, :].rearrange("d (g q p) -> d g p q", q=P, p=2)[:, t // 2, t % 2, :]
                        ins = pe.matmul(py[:, t, :], cols, w_o[:, c, :], start=(c == 0), stop=(c == DC - 1))
                ins.then_inc(y_ready, 1)

        @block.gpsimd
        def _(pool):
            pool.memset(v[:], 0.0).then_inc(zeros, 1)
            with pool.Fori(0, B) as b:
                pool.wait_ge(rot_done, 4 * b + 2)
                for k in range(2):
                    pool.tensor_tensor(keys[:, k, :, :], kT[:], core.consts[:, C_KEYS + k:C_KEYS + k + 1].unsqueeze(
                        2).to_broadcast([P, DC, T]), ALU.mult).then_inc(keys_ready, 1)

        @block.scalar
        def _(act):
            act.preload_act_table(ACT.Exp)
            act.activation(mask[:, 0, :], core.ident, ACT.Copy).then_inc(mask_ready, 1)
            act.activation(mask[:, 1, :], core.neg, ACT.Copy).then_inc(mask_ready, 1)
            act.sem_inc(odd_copied, 1)
            act.wait_ge(zeros, 1)

            def copy(b, h, k):
                act.wait_ge(turned, TB * (H * b + h) + k + 1)
                if h >= 2:
                    act.wait_ge(heads_out, H * b + h - 1)
                act.activation(prT[:, h % 2, k, k * P:T], pw[:, k % 2, k * P:T], ACT.Copy).then_inc(odd_copied, 1)

            with act.Fori(0, B) as b:
                act.wait_ge(low_ready, b + 1)
                act.activation(low[:], pw[:, 0, :], ACT.Copy).then_inc(low_copied, 1)
                act.wait_ge(v_ready, b + 1)
                for p in range(2):
                    ins = act.activation(own(v[:, p], p), own(po_v, p), ACT.Copy)
                ins.then_inc(v_copied, 1)
                for h in range(H + 1):
                    if h < H:
                        for k, q in enumerate(QB_ORDER):
                            n = (q + 1) * P
                            act.wait_ge(max_ready, TB * H * b + TB * h + k + 1)
                            act.activation(pr[:, h % 2, q, 0:n], pa[:, q, 0:n], ACT.Exp,
                                           bias=nmax[:, h % 2, q:q + 1],
                                           accum_out=total[:, h, q:q + 1]).then_inc(exp_ready, 1)
                    if h:
                        copy(b, h - 1, 1)
                        copy(b, h - 1, 3)
                act.wait_ge(heads_out, H * (b + 1))
                act.activation(sums[:], po[:], ACT.Copy).then_inc(sums_copied, 1)
                act.wait_ge(o_turned, b + 1)
                act.activation(oT[:], po_T, ACT.Copy).then_inc(o_copied, 1)

        @block.vector
        def _(dve):
            dve.sem_inc(y_added, 1)
            dve.sem_inc(even_copied, 1)
            dve.wait_ge(w_in, 16 * len(loads))
            with dve.Fori(0, B) as b:
                for which, dst in enumerate((kT, qT)):
                    for o_ in range(DC):
                        n = 4 * b + 2 * which + o_
                        dve.wait_ge(rot_ready, n + 1)
                        dve.tensor_tensor(turn[:, 0, :], pa[:, 2 * o_, :], rope[:, 0, :], ALU.mult)
                        dve.tensor_tensor(turn[:, 1, :], pa[:, 2 * o_ + 1, :], rope[:, 1, :],
                                          ALU.mult).then_inc(rot_step, 1)
                        dve.wait_ge(rot_step, n + 1)
                        dve.tensor_tensor(dst[:, o_, :], turn[:, 0, :], turn[:, 1, :], ALU.add).then_inc(rot_done, 1)
                        dve.wait_ge(rot_done, n + 1)
                for h in range(H + 1):
                    n = TB * H * b + TB * h
                    if h < H:
                        for k, q in enumerate(QB_ORDER):
                            dve.wait_ge(scores_ready, n + k + 1)
                            dve.tensor_reduce(nmax[:, h % 2, q:q + 1], pa[:, q, 0:(q + 1) * P], AX.X, ALU.max,
                                              negate=True).then_inc(max_ready, 1)
                    if h:
                        n -= TB
                        if h > 2:
                            dve.wait_ge(heads_out, H * b + h - 2)
                        for k in range(0, TB, 2):
                            dve.wait_ge(turned, n + k + 1)
                            dve.tensor_copy(prT[:, (h - 1) % 2, k, k * P:T], pw[:, k % 2, k * P:T]
                                            ).then_inc(even_copied, 1)
                dve.wait_ge(sums_turned, b + 1)
                inv = Steps(dve, norm_step, 2 * b, 2)
                inv(dve.reciprocal(total[:], total[:]))
                inv(dve.tensor_tensor(o[:].rearrange("q t (h d) -> q t h d", d=16),
                                      pw_tok.rearrange("q t (h d) -> q t h d", d=16),
                                      total[:].rearrange("q h t -> q t h").unsqueeze(3).to_broadcast([P, TB, H, 16]),
                                      ALU.mult))
                inv.close()
                xn = core.xn[:, bass.ds(4 * b, 4), :]
                x = core.x[:, bass.ds(4 * b, 4), :]
                dve.wait_ge(y_ready, b + 1)
                dve.tensor_tensor(xn, py[:], xn, ALU.add).then_inc(y_added, 1)
                dve.wait_ge(y_added, b + 2)
                dve.tensor_tensor(x, x, xn, ALU.add).then_inc(joined, 1)


class Spec:
    pass


def layer1_spec(dram):
    s = Spec()
    s.router, s.router_bias = dram["L1_gate_wT"], dram["L1_ffn_gate_b"]
    s.gate, s.up, s.down = dram["L1_ffn_w_gate"], dram["L1_ffn_w_up"], dram["L1_ffn_w_down"]
    s.gate_bT, s.up_bT, s.down_b = dram["L1_b_gateT"], dram["L1_b_upT"], dram["L1_ffn_b_down"]
    s.routed, s.experts, s.top, s.kind, s.weigh = 32, 32, 4, "swiglu", "softmax"
    s.alpha, s.limit = 1.702, 7.0
    s.factor = 1.0 / s.alpha
    return s


def layer2_spec(dram):
    s = Spec()
    s.router, s.router_bias = dram["L2_ffn_router_w"], dram["L2_ffn_router_b"]
    s.gate, s.up, s.down, s.down_b = dram["L2_gate"], dram["L2_up"], dram["L2_down"], None
    s.routed, s.experts, s.top, s.kind, s.weigh = 7, 8, 2, "silu", "sigmoid"
    s.factor = 1.0 / 8.0
    return s


def layer3_spec(dram):
    s = Spec()
    s.router, s.router_bias = dram["L3_ffn_gate_w"], None
    s.gate, s.up, s.down, s.down_b = dram["L3_ffn_w0"], dram["L3_ffn_w1"], dram["L3_ffn_wo"], None
    s.routed, s.experts, s.top, s.kind, s.weigh = 8, 8, 2, "silu", "softmax"
    s.factor = 1.0
    return s


def route(nc, st, core, spec, aT, cw, a):
    sem = st.sem
    a_hi = sem("a_hi")
    R, K = spec.routed, spec.top
    E8 = max(R, 8)
    w, bias = st.sb("w", [P, DC, R]), st.sb("bias", [P, R])
    scores = st.sb("scores", [P, TILES, E8])
    top = st.sb("top", [P, TILES, 8])
    which = st.scope.enter_context(nc.sbuf_tensor(st.name + "_which", [P, TILES, 8], mybir.dt.uint32))
    weight, hit = st.sb("weight", [P, TILES, K]), st.sb("hit", [P, TILES, R])
    total = st.sb("total", [P, TILES])
    logits = st.ps("logits", [P, TILES, 32])
    w_in, products, step, act_done = sem("w_in"), sem("products"), sem("step"), sem("act_done")
    picked, at_score = sem("picked"), sem("at_score")
    n_in = 16 * (1 + (spec.router_bias is not None))
    if spec.down_b is not None:
        db, cwT = st.sb("down_b", [R, D]), st.sb("cwT", [R, TILES, P])
        pT, pb = st.ps("cwT_p", [P, 4, P]), st.ps("bias_p", [P, 4, D])
        cw_turned, cwT_ready, bias_ready, bias_added = (sem(n) for n in (
            "cw_turned", "cwT_ready", "bias_ready", "bias_added"))
        n_in += 16
    with nc.Block() as block:
        @block.sync
        def _(sp):
            sp.dma_start(w[:], in_chunks(spec.router)).then_inc(w_in, 16)
            if spec.router_bias is not None:
                sp.dma_start(bias[:], on_all_partitions(spec.router_bias, P)).then_inc(w_in, 16)
            if spec.down_b is not None:
                sp.dma_start(db[:], spec.down_b).then_inc(w_in, 16)

        @block.tensor
        def _(pe):
            pe.wait_ge(w_in, n_in)
            for t in range(TILES):
                for c in range(DC):
                    ins = pe.matmul(logits[:, t, 0:R], col_group(aT, t // 2, t % 2)[:, c, :], w[:, c, :],
                                    start=(c == 0), stop=(c == DC - 1))
            ins.then_inc(products, 1)
            if spec.down_b is not None:
                pe.wait_ge(at_score, 1)
                for t in range(TILES):
                    if t % 4 == 0 and t:
                        pe.wait_ge(cwT_ready, t // 4)
                    ins = pe.transpose(pT[0:R, t % 4, :], cw[:, t, 0:R], core.ident)
                    if t % 4 == 3:
                        ins.then_inc(cw_turned, 1)
                pe.wait_ge(cwT_ready, TILES // 4)
                for t in range(TILES):
                    if t % 4 == 0 and t:
                        pe.wait_ge(bias_added, t // 4)
                    ins = pe.matmul(pb[:, t % 4, :], cwT[:, t, :], db[:], start=True, stop=True)
                    if t % 4 == 3:
                        ins.then_inc(bias_ready, 1)

        @block.gpsimd
        def _(pool):
            pool.wait_ge(a_hi, 1)
            pool.tensor_tensor(a.lo[:], aT[:], a.hi[:].bitcast(F32), ALU.subtract)

        @block.scalar
        def _(act):
            act.activation(a.hi[:], aT[:], ACT.Copy).then_inc(a_hi, 1)
            if spec.weigh == "sigmoid":
                act.wait_ge(step, 2)
                act.activation(scores[:, :, 0:R], scores[:, :, 0:R], ACT.Sigmoid).then_inc(act_done, 1)
            else:
                act.wait_ge(step, 2)
                act.activation(weight[:], weight[:], ACT.Exp).then_inc(act_done, 1)

        @block.vector
        def _(dve):
            do = Steps(dve, step)
            dve.wait_ge(w_in, n_in)
            dve.wait_ge(products, 1)
            if spec.weigh == "sigmoid":
                do(dve.memset(scores[:, :, R:E8], -1.0))
            if spec.router_bias is not None:
                ins = dve.tensor_tensor(scores[:, :, 0:R], logits[:, :, 0:R],
                                        bias[:].unsqueeze(1).to_broadcast([P, TILES, R]), ALU.add)
            else:
                ins = dve.tensor_copy(scores[:, :, 0:R], logits[:, :, 0:R])
            do(ins)
            if spec.weigh == "sigmoid":
                dve.wait_ge(act_done, 1)
            for t in range(TILES):
                dve.max(top[:, t, :], scores[:, t, :]).then_inc(picked, 1)
            for t in range(TILES):
                dve.wait_ge(picked, t + 1)
                ins = dve.max_index(which[:, t, :], top[:, t, :], scores[:, t, :])
                ins.then_inc(picked, 1)
            dve.wait_ge(picked, 2 * TILES)
            if spec.weigh == "softmax":
                do(dve.tensor_tensor(weight[:], top[:, :, 0:K], top[:, :, 0:1].to_broadcast([P, TILES, K]),
                                     ALU.subtract))
                dve.wait_ge(act_done, 1)
            else:
                do(dve.tensor_copy(weight[:], top[:, :, 0:K]))
            do(dve.reduce_sum(total[:], weight[:], AX.X))
            do(dve.reciprocal(total[:], total[:]))
            do(dve.tensor_scalar(total[:], total[:], spec.factor, None, ALU.mult))
            do(dve.tensor_tensor(weight[:], weight[:], total[:].unsqueeze(2).to_broadcast([P, TILES, K]),
                                 ALU.mult))
            numbers = core.consts[:, C_COUNT:C_COUNT + R].unsqueeze(1).to_broadcast([P, TILES, R])
            if spec.experts > R:
                do(dve.memset(cw[:, :, R:spec.experts], spec.factor))
            for k in range(K):
                to = cw[:, :, 0:R] if k == 0 else hit[:]
                do(dve.tensor_tensor(to, numbers, which[:, :, k:k + 1].to_broadcast([P, TILES, R]), ALU.is_equal))
                do(dve.tensor_tensor(to, to, weight[:, :, k:k + 1].to_broadcast([P, TILES, R]), ALU.mult))
                if k:
                    do(dve.tensor_tensor(cw[:, :, 0:R], cw[:, :, 0:R], hit[:], ALU.add))
            if spec.down_b is not None:
                assert spec.factor != 1.0
                dve.sem_inc(at_score, 1)
                for k in range(TILES // 4):
                    dve.wait_ge(cw_turned, k + 1)
                    dve.tensor_scalar(cwT[:, 4 * k:4 * k + 4, :], pT[0:R, :, :], 1.0 / spec.factor, None,
                                      ALU.mult).then_inc(cwT_ready, 1)
                for k in range(TILES // 4):
                    dve.wait_ge(bias_ready, k + 1)
                    x = core.x[:, 4 * k:4 * k + 4, :]
                    dve.tensor_tensor(x, pb[:], x, ALU.add).then_inc(bias_added, 1)


def experts(nc, st, core, spec, aT):
    sem = st.sem
    E = spec.experts
    I = spec.gate.shape[2]
    MC = I // P
    U = 4 if MC == 1 else 2
    ROUNDS = E // U
    BLOCKS = TB
    assert TOK == BLOCKS * 512 and ROUNDS > 1 and E % U == 0
    PER = BLOCKS * MC
    STEPS = U * PER
    LAG = 3 if spec.kind == "swiglu" else 2
    RING = 4
    GI, WC = DC * I, 2 * DC * I + MC * D
    PIECE = 768
    PIECES = WC // PIECE
    assert STEPS % RING == 0 and WC % PIECE == 0 and (PIECES == 1 or 3 * PIECES + LAG <= PER)
    cw = st.sb("cw", [P, TILES, max(E, 8)])
    a = st.sb_parts("a", [P, DC, TOK])
    with ExitStack() as scope:
        route(nc, Stage(nc, st.keep, scope, st.name + "r"), core, spec, aT, cw, a)

    swiglu = spec.kind == "swiglu"
    w_raw, w = st.sb("w_raw", [P, U, WC]), st.sb_parts("w", [P, U, WC])
    raw, hidden = st.sb("raw", [P, 2, 512]), st.sb_parts("hidden", [P, RING, 512])
    silu = st.sb("silu", [P, 2, 512])
    if swiglu:
        bg, bu = st.sb("bg", [P, E]), st.sb("bu", [P, E])
        gate, up = st.sb("gate", [P, 2, 512]), st.sb("up", [P, 2, 512])
    pg, pu = st.ps("pg", [P, 2, 512]), st.ps("pu", [P, 2, 512])
    py = st.ps("py", [P, 2, 4, D])
    w_in = [sem(f"w{u}_in") for u in range(U)]
    bias_in, w_hi, w_split = sem("bias_in"), sem("w_hi"), sem("w_split")
    g_ready, u_ready, g_taken, u_taken = (sem(n) for n in ("g_ready", "u_ready", "g_taken", "u_taken"))
    silu_ready, up_clipped = sem("silu_ready"), sem("up_clipped")
    raw_ready, hi_ready, hidden_ready = sem("raw_ready"), sem("hi_ready"), sem("hidden_ready")
    y_ready, y_taken = sem("y_ready"), sem("y_taken")
    act_waited, pool_waited = sem("act_waited"), sem("pool_waited")
    if not swiglu:
        u_taken = raw_ready

    def gate_w(t, u):
        return t[:, u, 0:GI].rearrange("p (c i) -> p c i", c=DC)

    def up_w(t, u):
        return t[:, u, GI:2 * GI].rearrange("p (c i) -> p c i", c=DC)

    def down_w(t, u):
        return t[:, u, 2 * GI:WC].rearrange("p (m d) -> p m d", m=MC)

    def piece_after(k):
        u, r = k // PER, k % PER
        first = LAG if U == 2 else 0
        step = 3 if PIECES > 1 else 1
        if r >= first and (r - first) % step == 0 and (r - first) // step < PIECES:
            return (u + 1) % U, (r - first) // step
        return None

    def rounds(eng, body):
        body(0, True, False)
        if ROUNDS > 2:
            with eng.Fori(1, ROUNDS - 1) as i:
                body(i, False, False)
        body(ROUNDS - 1, False, True)

    with nc.Block() as block:
        @block.sync
        def _(sp):
            def load(u, e):
                for view, src, pattern in ((gate_w, spec.gate, "e (c p) i -> p (e c) i"),
                                           (up_w, spec.up, "e (c p) i -> p (e c) i"),
                                           (down_w, spec.down, "e (m p) d -> p (e m) d")):
                    sp.dma_start(view(w_raw, u), src[bass.ds(e, 1)].rearrange(pattern, p=P)).then_inc(w_in[u], 16)

            load(0, 0)
            if swiglu:
                sp.dma_start(bg[:], spec.gate_bT).then_inc(bias_in, 16)
                sp.dma_start(bu[:], spec.up_bT).then_inc(bias_in, 16)
            for u in range(1, U):
                load(u, u)

            def body(i, first, last):
                for u in range(U):
                    if not last:
                        sp.wait_ge(w_split, PIECES * U * i + PIECES * (u + 1))
                        load(u, (i + 1) * U + u)

            rounds(sp, body)

        @block.tensor
        def _(pe):
            pe.sem_inc(y_ready, RING)

            def up_and_gate(i, k):
                u, tb, m = k // PER, k // MC % BLOCKS, k % MC
                if k % PER == 0:
                    pe.wait_ge(w_split, PIECES * U * i + PIECES * (u + 1))
                for ps, view, taken, ready in ((pg, gate_w, g_taken, g_ready), (pu, up_w, u_taken, u_ready)):
                    pe.wait_ge(taken, i * STEPS + k + 1)
                    for c in range(DC):
                        ins = split_matmul(pe, ps[:, k % 2, :],
                                           w.view(lambda t: view(t, u)[:, c, m * P:(m + 1) * P]),
                                           a.view(lambda t: t[:, c, tb * 512:(tb + 1) * 512]),
                                           start=(c == 0), stop=(c == DC - 1))
                    ins.then_inc(ready, 1)

            def down(i, k):
                u, m = k // PER % U, k % MC
                pe.wait_ge(hidden_ready, i * STEPS + k + 3)
                if m == 0:
                    pe.wait_ge(y_taken, i * U * BLOCKS + k // MC + 1)
                for q in range(4):
                    cols = hidden.view(lambda t: t[:, k % RING, :].rearrange(
                        "h (g q p) -> h g p q", q=P, p=2)[:, q // 2, q % 2, :])
                    ins = split_matmul(pe, py[:, (k // MC) % 2, q, :], cols, w.view(lambda t: down_w(t, u)[:, m, :]),
                                       start=(m == 0 and q % 2 == 0), stop=(m == MC - 1), skip_group_check=True)
                ins.then_inc(y_ready, 1)

            def body(i, first, last):
                for k in range(STEPS):
                    up_and_gate(i, k)
                    if not (first and k < LAG):
                        down(i, k - LAG)

            rounds(pe, body)
            for k in range(STEPS - LAG, STEPS):
                down(ROUNDS - 1, k)

        @block.scalar
        def _(act):
            act.preload_act_table(ACT.Silu)
            for p in range(PIECES):
                act.wait_ge(w_in[0], 48)
                cols = slice(p * PIECE, (p + 1) * PIECE)
                act.activation(w.hi[:, 0, cols], w_raw[:, 0, cols], ACT.Copy).then_inc(w_hi, 1)
            if swiglu:
                act.wait_ge(bias_in, 32)
                act.sem_inc(u_taken, 2)
            else:
                act.sem_inc(g_taken, 2)

            def split_hidden(i, k):
                act.wait_ge(raw_ready, i * STEPS + k + 3)
                act.activation(hidden.hi[:, k % RING, :], raw[:, k % 2, :], ACT.Copy).then_inc(hi_ready, 1)

            def split_weights(i, k, first):
                u, p = piece_after(k)
                cols = slice(p * PIECE, (p + 1) * PIECE)
                act.wait_ge(w_in[u], 48 * i + 48 * (2 if u == 0 else 1))
                if not (first and u):
                    act.wait_ge(y_ready, i * STEPS + (k // PER - U + 2) * PER + RING)
                act.activation(w.hi[:, u, cols], w_raw[:, u, cols], ACT.Copy).then_inc(w_hi, 1)

            def body(i, first, last):
                for k in range(STEPS):
                    n = i * STEPS + k
                    act.wait_ge(raw_ready, n + 1)
                    if swiglu:
                        wait_apart(act, u_ready, n + 1, act_waited)
                        act.activation(up[:, k % 2, :], pu[:, k % 2, :], ACT.Identity,
                                       bias=bu[:, bass.ds(i * U + k // PER, 1)]).then_inc(u_taken, 1)
                        act.wait_ge(g_taken, n + 3)
                        act.activation(silu[:, k % 2, :], gate[:, k % 2, :], ACT.Silu,
                                       scale=spec.alpha).then_inc(silu_ready, 1)
                    else:
                        act.wait_ge(g_ready, n + 1)
                        act.activation(silu[:, k % 2, :], pg[:, k % 2, :], ACT.Silu).then_inc(g_taken, 1)
                    if not (first and k == 0):
                        split_hidden(i, k - 1)
                    if piece_after(k) and not (last and k // PER == U - 1):
                        split_weights(i, k, first)

            rounds(act, body)
            split_hidden(ROUNDS - 1, STEPS - 1)

        @block.gpsimd
        def _(pool):
            def rest_of_weights(slot, p, n):
                cols = slice(p * PIECE, (p + 1) * PIECE)
                pool.wait_ge(w_hi, n)
                pool.tensor_tensor(w.lo[:, slot, cols], w_raw[:, slot, cols], w.hi[:, slot, cols].bitcast(F32),
                                   ALU.subtract).then_inc(w_split, 1)

            for p in range(PIECES):
                rest_of_weights(0, p, p + 1)

            def body(i, first, last):
                for k in range(STEPS):
                    if swiglu:
                        wait_apart(pool, u_taken, i * STEPS + k + 3, pool_waited)
                        pool.tensor_scalar(up[:, k % 2, :], up[:, k % 2, :], spec.limit, -spec.limit, ALU.min,
                                           ALU.max).then_inc(up_clipped, 1)
                    if piece_after(k) and not (last and k // PER == U - 1):
                        u, p = piece_after(k)
                        rest_of_weights(u, p, i * U * PIECES + (k // PER + 1) * PIECES + p + 1)

            rounds(pool, body)

        @block.vector
        def _(dve):
            dve.sem_inc(y_taken, 2)
            dve.sem_inc(raw_ready, 2)
            dve.sem_inc(hidden_ready, 2)
            if swiglu:
                dve.sem_inc(g_taken, 2)
                dve.wait_ge(bias_in, 32)

            def clamp_gate(i, k):
                n = i * STEPS + k
                dve.wait_ge(g_ready, n + 1)
                dve.wait_ge(raw_ready, n + 1)
                dve.tensor_scalar(gate[:, k % 2, :], pg[:, k % 2, :], bg[:, bass.ds(i * U + k // PER, 1)],
                                  spec.limit, ALU.add, ALU.min).then_inc(g_taken, 1)

            def hide(i, k):
                n = i * STEPS + k
                dve.wait_ge(hidden_ready, n + 1)
                if swiglu:
                    dve.wait_ge(silu_ready, n + 1)
                    dve.wait_ge(up_clipped, n + 1)
                    dve.scalar_tensor_tensor(out=raw[:, k % 2, :], in0=up[:, k % 2, :], scalar=1.0,
                                             in1=silu[:, k % 2, :], op0=ALU.add, op1=ALU.mult
                                             ).then_inc(raw_ready, 1)
                else:
                    dve.wait_ge(g_taken, n + 3)
                    dve.wait_ge(u_ready, n + 1)
                    dve.tensor_tensor(raw[:, k % 2, :], pu[:, k % 2, :], silu[:, k % 2, :],
                                      ALU.mult).then_inc(raw_ready, 1)

            def rest_of_hidden(i, k):
                dve.wait_ge(y_ready, i * STEPS + k + 1)
                dve.wait_ge(hi_ready, i * STEPS + k + 1)
                dve.tensor_tensor(hidden.lo[:, k % RING, :], raw[:, k % 2, :], hidden.hi[:, k % RING, :].bitcast(F32),
                                  ALU.subtract).then_inc(hidden_ready, 1)

            def weigh(i, nb):
                u, tb = nb // BLOCKS, nb % BLOCKS
                dve.wait_ge(y_ready, i * STEPS + MC * (nb + 1) + RING)
                for q in range(4):
                    t = 4 * tb + q
                    ins = dve.scalar_tensor_tensor(out=core.x[:, t, :], in0=py[:, nb % 2, q, :],
                                                   scalar=cw[:, t, bass.ds(i * U + u, 1)], in1=core.x[:, t, :],
                                                   op0=ALU.mult, op1=ALU.add)
                ins.then_inc(y_taken, 1)

            behind = 1 if swiglu else 0

            def body(i, first, last):
                for k in range(STEPS + (LAG + 1 if last else 0)):
                    if k < STEPS and swiglu:
                        clamp_gate(i, k)
                    if not (first and k < behind) and k - behind < STEPS:
                        hide(i, k - behind)
                    if not (first and k <= behind) and k - 1 - behind < STEPS:
                        rest_of_hidden(i, k - 1 - behind)
                    done = k - LAG - 1
                    if done % MC == MC - 1 and not (first and done < 0):
                        weigh(i, done // MC)

            rounds(dve, body)


QB_ORDER = (3, 2, 1, 0)


def layer3_attention(nc, st, core, dram, aT):
    sem = st.sem
    SCALE = D ** -0.5
    w, wo = st.sb("w", [P, DC, 3 * D]), st.sb("wo", [P, DC, D])
    here = st.sb("here", [P, DC, T])
    qT, kT, v = st.sb("qT", [P, DC, T]), st.sb("kT", [P, DC, T]), st.sb("v", [P, TB, D])
    pr, prT = st.sb("pr", [P, TB, T]), st.sb("prT", [P, TB, T])
    oT = st.sb("oT", [P, DC, T])
    nmax, total, inv = (st.sb(n, [P, TB]) for n in ("nmax", "total", "inv"))
    pa = st.ps("pa", [P, 4, T])
    pv = st.ps("pv", [P, TB, D])
    pw = st.ps("pw", [P, 2, T])
    (w_in, here_ready, qk_ready, q_copied, k_copied, v_ready, v_copied, scores_ready, score_masked, max_ready,
     exp_ready, inv_ready, prob_ready, turned, turned_copied, o_ready, o_copied, y_ready, y_added, x_residual) = (
        sem(n) for n in ("w_in here_ready qk_ready q_copied k_copied v_ready v_copied scores_ready score_masked "
                         "max_ready exp_ready inv_ready prob_ready turned turned_copied o_ready o_copied y_ready "
                         "y_added x_residual").split())
    poT = pv[:].rearrange("d (c h) n -> d c (h n)", c=DC)
    py = pw[:].rearrange("q b (k n) -> q (b k) n", n=D)
    with nc.Block() as block:
        @block.sync
        def _(sp):
            sp.dma_start(w[:], in_chunks(dram["L3_attn_qkv"])).then_inc(w_in, 16)
            sp.dma_start(wo[:], in_chunks(dram["L3_attn_o_proj"])).then_inc(w_in, 16)

        @block.gpsimd
        def _(pool):
            with pool.Fori(0, B) as b:
                pool.wait_ge(v_copied, b + 1)
                pool.tensor_copy(here[:], aT[:, :, bass.ds(b * T, T)]).then_inc(here_ready, 1)
                for k, q in enumerate(QB_ORDER):
                    n = (q + 1) * P
                    pool.wait_ge(inv_ready, TB * b + k + 1)
                    pool.tensor_tensor(pr[:, q, 0:n], pr[:, q, 0:n], inv[:, q:q + 1].to_broadcast([P, n]),
                                       ALU.mult).then_inc(prob_ready, 1)

        @block.tensor
        def _(pe):
            pe.wait_ge(w_in, 32)
            with pe.Fori(0, B) as b:
                pe.wait_ge(here_ready, b + 1)
                for o in range(4):
                    for c in range(DC):
                        ins = pe.matmul(pa[:, o, :], w[:, c, o * P:(o + 1) * P], here[:, c, :],
                                        start=(c == 0), stop=(c == DC - 1))
                ins.then_inc(qk_ready, 1)
                for t in range(TB):
                    for c in range(DC):
                        ins = pe.matmul(pv[:, t, :], here[:, c, t * P:(t + 1) * P], w[:, c, 2 * D:3 * D],
                                        start=(c == 0), stop=(c == DC - 1))
                ins.then_inc(v_ready, 1)
                pe.wait_ge(q_copied, b + 1)
                pe.wait_ge(k_copied, b + 1)
                for q in QB_ORDER:
                    n = (q + 1) * P
                    for c in range(DC):
                        ins = pe.matmul(pa[:, q, 0:n], qT[:, c, q * P:(q + 1) * P], kT[:, c, 0:n],
                                        start=(c == 0), stop=(c == DC - 1))
                    ins.then_inc(scores_ready, 1)
                pe.wait_ge(prob_ready, TB * (b + 1))
                pe.wait_ge(y_added, b + 1)
                for k in range(TB):
                    if k >= 2:
                        pe.wait_ge(turned_copied, TB * b + k - 1)
                    for q in range(k, TB):
                        ins = pe.transpose(pw[:, k % 2, q * P:(q + 1) * P], pr[:, q, k * P:(k + 1) * P], core.ident)
                    ins.then_inc(turned, 1)
                pe.wait_ge(v_copied, b + 2)
                for k in range(TB):
                    pe.wait_ge(turned_copied, TB * b + k + 1)
                    for c in range(DC):
                        ins = pe.matmul(poT[:, c, k * P:T], v[:, k, c * P:(c + 1) * P], prT[:, k, k * P:T],
                                        start=(k == 0), stop=(k == TB - 1), skip_group_check=True)
                ins.then_inc(o_ready, 1)
                pe.wait_ge(o_copied, b + 1)
                for t in range(TB):
                    for c in range(DC):
                        cols = oT[:, c, :].rearrange("d (g q p) -> d g p q", q=P, p=2)[:, t // 2, t % 2, :]
                        ins = pe.matmul(py[:, t, :], cols, wo[:, c, :], start=(c == 0), stop=(c == DC - 1))
                ins.then_inc(y_ready, 1)

        @block.scalar
        def _(act):
            act.preload_act_table(ACT.Exp)
            act.sem_inc(v_copied, 1)
            with act.Fori(0, B) as b:
                act.wait_ge(qk_ready, b + 1)
                act.activation(qT[:], pa[:, 0:2, :], ACT.Copy, scale=SCALE).then_inc(q_copied, 1)
                act.wait_ge(v_ready, b + 1)
                act.activation(v[:], pv[:], ACT.Copy).then_inc(v_copied, 1)
                for k, q in enumerate(QB_ORDER):
                    n = (q + 1) * P
                    act.wait_ge(max_ready, TB * b + k + 1)
                    act.activation(pr[:, q, 0:n], pa[:, q, 0:n], ACT.Exp, bias=nmax[:, q:q + 1],
                                   accum_out=total[:, q:q + 1]).then_inc(exp_ready, 1)
                for k in range(1, TB, 2):
                    act.wait_ge(turned, TB * b + k + 1)
                    act.wait_ge(turned_copied, TB * b + k)
                    act.activation(prT[:, k, k * P:T], pw[:, k % 2, k * P:T], ACT.Copy).then_inc(turned_copied, 1)
                act.wait_ge(o_ready, b + 1)
                act.activation(oT[:], poT, ACT.Copy).then_inc(o_copied, 1)

        @block.vector
        def _(dve):
            dve.sem_inc(y_added, 1)
            with dve.Fori(0, B) as b:
                dve.wait_ge(qk_ready, b + 1)
                dve.tensor_copy(kT[:], pa[:, 2:4, :]).then_inc(k_copied, 1)
                for k, q in enumerate(QB_ORDER):
                    n = (q + 1) * P
                    dve.wait_ge(scores_ready, TB * b + k + 1)
                    dve.tensor_tensor(pa[:, q, q * P:n], pa[:, q, q * P:n], core.neg, ALU.add).then_inc(score_masked, 1)
                    dve.wait_ge(score_masked, TB * b + k + 1)
                    dve.tensor_reduce(nmax[:, q:q + 1], pa[:, q, 0:n], AX.X, ALU.max, negate=True
                                      ).then_inc(max_ready, 1)
                for k, q in enumerate(QB_ORDER):
                    dve.wait_ge(exp_ready, TB * b + k + 1)
                    dve.reciprocal(inv[:, q:q + 1], total[:, q:q + 1]).then_inc(inv_ready, 1)
                x, xn = core.x[:, bass.ds(4 * b, 4), :], core.xn[:, bass.ds(4 * b, 4), :]
                dve.tensor_tensor(x, x, xn, ALU.add).then_inc(x_residual, 1)
                for k in range(0, TB, 2):
                    dve.wait_ge(turned, TB * b + k + 1)
                    if k:
                        dve.wait_ge(turned_copied, TB * b + k)
                    dve.tensor_copy(prT[:, k, k * P:T], pw[:, k % 2, k * P:T]).then_inc(turned_copied, 1)
                dve.wait_ge(x_residual, b + 1)
                dve.wait_ge(y_ready, b + 1)
                dve.tensor_tensor(x, py, x, ALU.add).then_inc(y_added, 1)


LAYERS = (0, 1, 2, 3)


def build(nc, dram, out):
    with ExitStack() as keep:
        core, used = Core(), []

        def resident(name, shape):
            return keep.enter_context(nc.sbuf_tensor(name, shape, F32))

        core.x, core.xn = resident("x", [P, TILES, D]), resident("xn", [P, TILES, D])
        core.xnT = resident("xnT", [P, DC, TOK])
        core.consts = resident("consts", [P, C_END])
        core.ab_sum, core.bcT = resident("ab_sum", [P, DC]), resident("bcT", [P, DC, B])
        core.ident = core.consts[:, C_ID:C_ID + P]
        core.tri = core.consts[:, C_TRI:C_TRI + P]
        core.neg = core.consts[:, C_NEG:C_NEG + P]
        core.blk = core.consts[:, C_BLK:C_BLK + P]

        def run(name, f, *args, **kw):
            with ExitStack() as scope:
                f(nc, Stage(nc, used, scope, name), core, *args, **kw)

        run("s", setup, dram)
        if 0 in LAYERS:
            run("n0", normalise, core.x, core.xn, core.xnT, 1e-5)
            with ExitStack() as scope:
                st = Stage(nc, used, scope, "l0")
                gsT, gateT, last_rows = st.sb("gsT", [P, DC, TOK]), st.sb("gateT", [P, DC, TOK]), st.sb("last", [B, D])
                run("m0", layer0_mix, dram, gsT, gateT, last_rows)
                run("j0", layer0_join, dram, gsT, gateT)
        if 1 in LAYERS:
            run("n1", normalise, core.x, core.xn, core.xnT, 1e-5)
            run("a1", layer1_attention)
            run("f1", experts, layer1_spec(dram), core.xnT)
        if 2 in LAYERS:
            release(nc, used)
            run("n2", normalise, core.x, core.xn, core.xnT, 1e-5)
            run("a2", layer2_abc, dram)
            with ExitStack() as scope:
                st = Stage(nc, used, scope, "l2")
                aT = st.sb("aT", [P, DC, TOK])
                run("r2", normalise, core.xn, None, aT, 1e-5, rms=True, gain=dram["L2_ffn_ln1_w"])
                run("b2", layer2_attention, dram, aT)
                run("q2", normalise, core.xn, None, aT, 1e-5, rms=True, gain=dram["L2_ffn_ln2_w"])
                run("f2", experts, layer2_spec(dram), aT)
        if 3 in LAYERS:
            release(nc, used)
            run("n3", normalise, core.x, core.xn, core.xnT, 1e-5)
            with ExitStack() as scope:
                st = Stage(nc, used, scope, "l3")
                aT = st.sb("aT", [P, DC, TOK])
                run("r3", normalise, core.xn, None, aT, 1e-5, gain=dram["L3_attn_gamma"],
                    shift=dram["L3_attn_beta"])
                run("a3", layer3_attention, dram, aT)
            run("f3", experts, layer3_spec(dram), core.xnT)

        stored = nc.alloc_semaphore(name="stored")
        with nc.Block() as block:
            @block.sync
            def _(sp):
                for p in range(2):
                    sp.dma_start(token_rows(out, p), core.x[:, p::2, :]).then_inc(stored, 16)
                sp.wait_ge(stored, 32)


def constants():
    c = np.zeros((P, C_END), np.float32)
    i = np.arange(P)
    c[:, C_ID:C_ID + P] = np.eye(P)
    c[:, C_TRI:C_TRI + P] = i[None, :] >= i[:, None]
    c[:, C_NEG:C_NEG + P] = np.where(i[None, :] > i[:, None], NEG, 0.0)
    c[:, C_BLK:C_BLK + P] = i[None, :] // 32 == i[:, None] // 32
    for p in range(2):
        c[:, C_EVEN + p] = (i // 16) % 2 == p
        c[:, C_KEYS + p] = 0.25 * c[:, C_EVEN + p]
    c[:, C_HALF:C_HALF + TILES] = -0.5
    c[:, C_ONE] = 1.0
    c[:, C_COUNT:C_COUNT + 32] = np.arange(32)
    half = 4
    inv = 1.0 / 10000.0 ** (np.arange(0, 8, 2, dtype=np.float32) / np.float32(8))
    angle = np.arange(T, dtype=np.float32)[None, :] * inv.astype(np.float32)[:, None]
    cos, sin = np.ones((P, T), np.float32), np.zeros((P, T), np.float32)
    for q in range(P):
        r = q % 16 - 8
        if r >= 0:
            cos[q] = np.cos(angle[r % half])
            sin[q] = np.sin(angle[r % half]) * (-1.0 if r < half else 1.0)
    return c, np.stack([cos, sin])


def lay_out(inputs):
    a = {n: np.ascontiguousarray(v) for n, v in inputs.items() if not n.startswith("L3_ffn_decoder")}
    a["consts"], a["rope"] = constants()
    a["C_wT"] = np.ascontiguousarray(a.pop("L0_attn_C_w").T)
    a["D_wT"] = np.ascontiguousarray(a.pop("L0_attn_D_w").T)
    a["L1_gate_wT"] = np.ascontiguousarray(a.pop("L1_ffn_gate_w").T)
    for n in ("b_gate", "b_up"):
        a["L1_%sT" % n] = np.ascontiguousarray(a.pop("L1_ffn_" + n).T)
    for n in ("gate", "up", "down"):
        a["L2_" + n] = np.concatenate([a.pop("L2_ffn_r_" + n), a.pop("L2_ffn_sh_" + n)[None]])
    nh, rd = 16, 8

    def slots(w, first):
        w = w.reshape(w.shape[0], nh, rd)
        z = np.zeros_like(w)
        return np.concatenate([w, z] if first else [z, w], axis=2).reshape(w.shape[0], -1)

    def turned(w):
        w = w.reshape(w.shape[0], nh, 2, rd // 2)[:, :, ::-1]
        return np.ascontiguousarray(w).reshape(w.shape[0], -1)

    for q in "kq":
        up, rope = a.pop("L2_ffn_%s_u_w" % q), a.pop("L2_ffn_rope_%s_w" % q)
        a["L2_%s_turned" % q] = slots(turned(rope), False)
        if q == "k":
            a["L2_k_plain"], a["L2_k_rope"] = slots(up, True), slots(rope, False)
        else:
            both = [w.reshape(w.shape[0], nh, rd) for w in (up, rope)]
            a["L2_q_both"] = np.concatenate(both, axis=2).reshape(up.shape[0], -1)
    a["L2_kvq_d"] = np.concatenate([a.pop("L2_ffn_kv_d_w"), a.pop("L2_ffn_q_d_w")], axis=1)
    return a


def kernel(**inputs):
    import concourse.bacc as bacc
    from concourse.bass_utils import run_bass_kernel_spmd

    nc = bacc.Bacc("TRN2", target_bir_lowering=False, num_devices=1)
    arrays = lay_out(inputs)
    dram = {n: nc.dram_tensor(n + "_dram", a.shape, mybir.dt.from_np(a.dtype), kind="ExternalInput").ap()
            for n, a in arrays.items()}
    out = nc.dram_tensor("out_dram", (B, T, D), F32, kind="ExternalOutput").ap()
    build(nc, dram, out)
    r = run_bass_kernel_spmd(nc, [{n + "_dram": a for n, a in arrays.items()}], core_ids=[0])
    return r.results[0]["out_dram"]
```

```python
from contextlib import ExitStack

import numpy as np

import concourse.bass as bass
from concourse import mybir

F32 = mybir.dt.float32
ALU = mybir.AluOpType
ACT = mybir.ActivationFunctionType
AX = mybir.AxisListType

P = 128
B, T, D = 4, 512, 256
TOK = B * T
TILES = TOK // P
DC = D // P
GROUPS = TILES // 2
TB = T // P
NEG = -1e30

C_ID, C_TRI, C_NEG, C_BLK, C_EVEN, C_HALF, C_ONE, C_COUNT = 0, 128, 256, 384, 512, 514, 530, 531
C_KEYS = C_COUNT + 32
C_END = C_KEYS + 2


class Steps:

    def __init__(self, eng, sem, base=0, total=None):
        self.eng, self.sem, self.base, self.total, self.n = eng, sem, base, total, 0

    def __call__(self, instruction):
        instruction.then_inc(self.sem, 1)
        self.n += 1
        self.eng.wait_ge(self.sem, self.base + self.n)

    def close(self):
        assert self.total is None or self.n == self.total, self.n


def wait_apart(eng, sem, value, waited):
    eng.wait_ge(sem, value)
    eng.sem_inc(waited, 1)


class Stage:

    def __init__(self, nc, keep, scope, name):
        self.nc, self.keep, self.scope, self.name = nc, keep, scope, name

    def sem(self, name):
        handle = self.nc.alloc_semaphore(name=f"{self.name}_{name}")
        self.keep.append(handle)
        return handle

    def sb(self, name, shape):
        return self.scope.enter_context(self.nc.sbuf_tensor(f"{self.name}_{name}", shape, F32))

    def sb_parts(self, name, shape):
        r = mybir.dt.float32r
        return Split(*(self.scope.enter_context(self.nc.sbuf_tensor(f"{self.name}_{name}_{x}", shape, r))
                       for x in ("hi", "lo")))

    def ps(self, name, shape):
        return self.scope.enter_context(self.nc.psum_tensor(f"{self.name}_{name}", shape, F32))


class Split:

    def __init__(self, hi, lo):
        self.hi, self.lo = hi, lo

    def view(self, f):
        return Split(f(self.hi), f(self.lo))


def split_matmul(pe, out, left, right, start, stop, **kw):
    for k, (a, b) in enumerate(((left.hi, right.hi), (left.hi, right.lo), (left.lo, right.hi))):
        ins = pe.matmul(out, a, b, start=start and k == 0, stop=stop and k == 2, **kw)
    return ins


class Core:
    pass


def release(nc, used):
    nc.clear_and_free_semaphores(used)
    nc.all_engine_barrier()
    used.clear()


def in_chunks(w):
    if len(w.shape) == 1:
        return w.rearrange("(c p) -> p c", p=P)
    return w.rearrange("(c p) n -> p c n", p=P)


def on_all_partitions(row, n):
    return row.unsqueeze(0).to_broadcast([n] + list(row.shape))


def token_rows(x, p):
    return x.rearrange("b t d -> (b t) d").rearrange("(g q p) d -> q g p d", q=P, p=2)[:, :, p, :]


def col_group(t, g, p):
    return t[:].rearrange("d c (g q p) -> d c g q p", q=P, p=2)[:, :, g, :, p]


def setup(nc, st, core, dram):
    sem = st.sem
    consts_in, x_in = sem("consts_in"), sem("x_in")
    with nc.Block() as block:
        @block.sync
        def _(sp):
            sp.dma_start(core.consts[:], dram["consts"]).then_inc(consts_in, 16)
            for p in range(2):
                sp.dma_start(core.x[:, p::2, :], token_rows(dram["L0_attn_x"], p)).then_inc(x_in, 16)
            sp.wait_ge(consts_in, 16)
            sp.wait_ge(x_in, 32)


def small_stats(do, eng, raw, mean, var, eps, rms):
    me, mo = raw[:, :, 1], raw[:, :, 4]
    do(eng.tensor_tensor(mean[:], me, mo, ALU.add))
    do(eng.tensor_tensor(var[:], me, mo, ALU.subtract))
    do(eng.tensor_tensor(var[:], var[:], var[:], ALU.mult))
    do(eng.scalar_tensor_tensor(out=var[:], in0=raw[:, :, 2], scalar=4.0 / D, in1=var[:],
                                op0=ALU.mult, op1=ALU.add))
    do(eng.scalar_tensor_tensor(out=var[:], in0=raw[:, :, 5], scalar=4.0 / D, in1=var[:],
                                op0=ALU.mult, op1=ALU.add))
    if rms:
        do(eng.tensor_tensor(raw[:, :, 0], mean[:], mean[:], ALU.mult))
        do(eng.tensor_tensor(var[:], var[:], raw[:, :, 0], ALU.add))
    do(eng.tensor_scalar(mean[:], mean[:], 0.5, None, ALU.mult))
    do(eng.tensor_scalar(var[:], var[:], 0.25, eps, ALU.mult, ALU.add))


def normalise(nc, st, core, src, tok_out, out_T, eps, rms=False, gain=None, shift=None):
    sem = st.sem
    raw = st.sb("raw", [P, TILES, 6])
    mean, var, rstd = (st.sb(n, [P, TILES]) for n in ("mean", "var", "rstd"))
    SLOTS = 4
    row = st.sb("row", [P, SLOTS, D])
    turned = st.ps("turned", [P, SLOTS, 512])
    gs = st.sb("gain_shift", [P, 2, DC])
    gain_in, stats, dve_step = sem("gain_in"), sem("stats"), sem("dve_step")
    rstd_ready = sem("rstd_ready")
    rows_ready, rows_free, rows_turned = sem("rows_ready"), sem("rows_free"), sem("rows_turned")
    n_gain = (gain is not None) + (shift is not None)
    with nc.Block() as block:
        @block.sync
        def _(sp):
            if gain is not None:
                sp.dma_start(gs[:, 0, :], in_chunks(gain), allow_slow_non_contiguous=True).then_inc(gain_in, 16)
            if shift is not None:
                sp.dma_start(gs[:, 1, :], in_chunks(shift), allow_slow_non_contiguous=True).then_inc(gain_in, 16)

        @block.vector
        def _(dve):
            with dve.Fori(0, TILES // SLOTS) as i:
                for j in range(SLOTS):
                    dve.bn_stats(raw[:, SLOTS * i + j, :], src[:, SLOTS * i + j, :]).then_inc(stats, 1)
            dve.wait_ge(stats, TILES)
            do = Steps(dve, dve_step)
            small_stats(do, dve, raw, mean, var, eps, rms)
            dve.wait_ge(rstd_ready, 1)
            with dve.Fori(0, TILES // SLOTS) as i:
                for j in range(SLOTS):
                    t = SLOTS * i + j
                    dve.wait_ge(rows_free, t + 1)
                    if rms:
                        dve.tensor_scalar(row[:, j, :], src[:, t, :], rstd[:, bass.ds(t, 1)], None,
                                          ALU.mult).then_inc(rows_ready, 1)
                    else:
                        dve.tensor_scalar(row[:, j, :], src[:, t, :], mean[:, bass.ds(t, 1)],
                                          rstd[:, bass.ds(t, 1)], ALU.subtract,
                                          ALU.mult).then_inc(rows_ready, 1)

        @block.gpsimd
        def _(pool):
            pool.wait_ge(dve_step, 9 if rms else 7)
            pool.tensor_tensor(rstd[:], var[:], core.consts[:, C_HALF:C_HALF + TILES],
                               ALU.pow).then_inc(rstd_ready, 1)

        @block.tensor
        def _(pe):
            with pe.Fori(0, TILES // SLOTS) as i:
                for j in range(SLOTS):
                    pe.wait_ge(rows_ready, SLOTS * i + j + 1)
                    for c in range(DC):
                        ins = pe.transpose(turned[:, j, c * P:(c + 1) * P], row[:, j, c * P:(c + 1) * P],
                                           core.ident)
                    ins.then_inc(rows_turned, 1)

        @block.scalar
        def _(act):
            act.preload_act_table(ACT.Identity)
            act.sem_inc(rows_free, SLOTS)
            if n_gain:
                act.wait_ge(gain_in, 16 * n_gain)
            with act.Fori(0, TILES // SLOTS) as i:
                for j in range(SLOTS):
                    act.wait_ge(rows_turned, SLOTS * i + j + 1)
                    if tok_out is not None:
                        act.activation(tok_out[:, SLOTS * i + j, :], row[:, j, :], ACT.Copy)
                    out = col_group(out_T, SLOTS // 2 * i + j // 2, j % 2)
                    if not n_gain:
                        act.activation(out, turned[:, j, 0:D].rearrange("p (c q) -> p c q", c=DC),
                                       ACT.Copy).then_inc(rows_free, 1)
                        continue
                    for c in range(DC):
                        ins = act.activation(out[:, c, :], turned[:, j, c * P:(c + 1) * P], ACT.Identity,
                                             bias=gs[:, 1, c:c + 1] if shift is not None else 0.0,
                                             scale=gs[:, 0, c:c + 1])
                    ins.then_inc(rows_free, 1)



def layer0_mix(nc, st, core, dram, gsT, gateT, last_rows):
    sem = st.sem
    H = 1024
    HC = H // P
    KS = 4
    w_c, w_d, w_g = (st.sb(n, [P, DC, D]) for n in ("w_c", "w_d", "w_g"))
    w_agg, w_bc = st.sb("w_agg", [P, DC, D]), st.sb("w_bc", [P, DC, D])
    w1, w2 = st.sb("w1", [P, DC, H]), st.sb("w2", [P, HC, D])
    cols = st.sb("cols", [P, 5, DC])
    b1 = st.sb("b1", [P, HC])
    rows = st.sb("rows", [B, 6, D])
    ab = st.sb("ab", [P, 2, DC, 64])
    ab_sum = core.ab_sum
    decay_col, decay = st.sb("decay_col", [P, DC]), st.sb("decay", [P, DC, T])
    sig = st.sb("sig", [P, 2, T])
    drive = st.sb("drive", [P, 2, T])
    thought, tnorm = st.sb("thought", [B, D]), st.sb("tnorm", [B, D])
    tT, hT = st.sb("tT", [P, DC, B]), st.sb("hT", [P, HC, B])
    raw, mean, var, rstd = st.sb("traw", [B, 6]), st.sb("tmean", [B, 1]), st.sb("tvar", [B, 1]), st.sb("trstd", [B, 1])
    pC, pD, pG = (st.ps(n, [P, 2, T]) for n in ("pC", "pD", "pG"))
    pS = st.ps("pS", [P, 512])
    pR = st.ps("pR", [P, 512])

    names = ("proj_w_in small_in agg_w_in mlp_w_in last_in c_ready d_ready g_ready sig_ready gate_ready "
             "proj_free sig_used scanned decay_ready setup_step dve_step t_turned t_copied h_ready h_biased h_act "
             "rows_done rstd_ready bc_ready bc_done out_step").split()
    s = {n: sem(n) for n in names}
    TSTEPS = 11

    with nc.Block() as block:
        @block.sync
        def _(sp):
            sp.dma_start(last_rows[:], core.xn[P - 1:P, 3::4, :]
                         ).then_inc(s["last_in"], 16)
            for w, n in ((w_c, "C_wT"), (w_d, "D_wT"), (w_g, "L0_ffn_gate_w")):
                sp.dma_start(w[:], in_chunks(dram[n])).then_inc(s["proj_w_in"], 16)
            for k, n in enumerate(("L0_attn_C_b", "L0_attn_D_b", "L0_ffn_gate_b", "L0_ffn_bc_b",
                                   "L0_attn_log_delta")):
                sp.dma_start(cols[:, k, :], in_chunks(dram[n]),
                             allow_slow_non_contiguous=True).then_inc(s["small_in"], 16)
            sp.dma_start(b1[:], in_chunks(dram["L0_ffn_d1_b"]),
                         allow_slow_non_contiguous=True).then_inc(s["small_in"], 16)
            for k, n in enumerate(("in_gamma", "in_beta", "agg_b", "pn_gamma", "pn_beta", "d2_b")):
                sp.dma_start(rows[:, k, :], on_all_partitions(dram["L0_ffn_" + n], B)).then_inc(s["small_in"], 16)
            for k, n in enumerate("AB"):
                sp.dma_start(ab[:, k, :, :], in_chunks(dram["L0_attn_" + n])).then_inc(s["small_in"], 16)
            for w, n in ((w_agg, "agg_w"), (w_bc, "bc_w")):
                sp.dma_start(w[:], in_chunks(dram["L0_ffn_" + n])).then_inc(s["agg_w_in"], 16)
            for w, n in ((w1, "d1_w"), (w2, "d2_w")):
                sp.dma_start(w[:], in_chunks(dram["L0_ffn_" + n])).then_inc(s["mlp_w_in"], 16)

        SMALL = 16 * 14

        @block.tensor
        def _(pe):
            def turn_rows(n):
                pe.wait_ge(s["dve_step"], (n + 1) * TSTEPS)
                for c in range(DC):
                    ins = pe.transpose(pS[:, B * c:B * c + B], tnorm[:, c * P:(c + 1) * P],
                                       core.ident[0:B, 0:B])
                ins.then_inc(s["t_turned"], 1)
                pe.wait_ge(s["t_copied"], n + 1)

            def add_rows(w, lhs, n_c):
                for c in range(n_c):
                    ins = pe.matmul(pR[0:B, 0:D], lhs[:, c, :], w[:, c, :], start=(c == 0), stop=(c == n_c - 1))
                ins.then_inc(s["rows_done"], 1)

            pe.wait_ge(s["agg_w_in"], 32)
            turn_rows(0)
            add_rows(w_agg, tT, DC)
            pe.wait_ge(s["proj_w_in"], 48)
            pe.wait_ge(s["mlp_w_in"], 32)
            with pe.Fori(0, B) as b:
                for o in range(DC):
                    pe.wait_ge(s["proj_free"], 2 * b + o + 1)
                    for ps, w, name in ((pD, w_d, "d_ready"), (pC, w_c, "c_ready"), (pG, w_g, "g_ready")):
                        for c in range(DC):
                            ins = pe.matmul(ps[:, o, :], w[:, c, o * P:(o + 1) * P],
                                            core.xnT[:, c, bass.ds(b * T, T)], start=(c == 0), stop=(c == DC - 1))
                        ins.then_inc(s[name], 1)
                pe.wait_ge(s["dve_step"], (b + 2) * TSTEPS)
                for c in range(DC):
                    ins = pe.matmul(pS[:, B * c:B * c + B], tnorm[:, c * P:(c + 1) * P],
                                    core.ident[0:B, 0:B], start=True, stop=True)
                ins.then_inc(s["t_turned"], 1)
                pe.wait_ge(s["t_copied"], b + 2)
                for h in range(HC):
                    for c in range(DC):
                        ins = pe.matmul(pS[:, 64 + B * h:64 + B * h + B], w1[:, c, h * P:(h + 1) * P], tT[:, c, :],
                                        start=(c == 0), stop=(c == DC - 1))
                ins.then_inc(s["h_ready"], 1)
                pe.wait_ge(s["h_act"], b + 1)
                add_rows(w2, hT, HC)
            pe.wait_ge(s["out_step"], 1 + 2 * KS)
            for c in range(DC):
                ins = pe.transpose(pS[:, B * c:B * c + B], thought[:, c * P:(c + 1) * P], core.ident[0:B, 0:B])
            ins.then_inc(s["t_turned"], 1)
            pe.wait_ge(s["t_copied"], KS + 2)
            for o in range(DC):
                for c in range(DC):
                    ins = pe.matmul(pR[:, 256 + B * o:256 + B * o + B], w_bc[:, c, o * P:(o + 1) * P], tT[:, c, :],
                                    start=(c == 0), stop=(c == DC - 1))
            ins.then_inc(s["bc_ready"], 1)

        @block.scalar
        def _(act):
            act.wait_ge(s["small_in"], SMALL)
            act.activation(decay_col[:], cols[:, 4, :], ACT.Sigmoid, scale=-1.0).then_inc(s["decay_ready"], 1)
            act.sem_inc(s["sig_used"], 2)
            with act.Fori(0, B) as b:
                for o in range(DC):
                    act.wait_ge(s["d_ready"], 2 * b + o + 1)
                    act.wait_ge(s["sig_used"], 2 * b + o + 3)
                    act.activation(sig[:, o, :], pD[:, o, :], ACT.Sigmoid,
                                   bias=cols[:, 1, o:o + 1]).then_inc(s["sig_ready"], 1)
                    act.wait_ge(s["g_ready"], 2 * b + o + 1)
                    act.activation(gateT[:, o, bass.ds(b * T, T)], pG[:, o, :], ACT.Sigmoid,
                                   bias=cols[:, 2, o:o + 1]).then_inc(s["gate_ready"], 1)
                act.wait_ge(s["h_biased"], b + 1)
                act.activation(hT[:], hT[:], ACT.Gelu).then_inc(s["h_act"], 1)

        @block.gpsimd
        def _(pool):
            for n in range(KS + 1):
                pool.wait_ge(s["dve_step"], n * TSTEPS + 8)
                pool.tensor_tensor(rstd[:], var[:], core.consts[0:B, C_HALF:C_HALF + 1],
                                   ALU.pow).then_inc(s["rstd_ready"], 1)

        @block.vector
        def _(dve):
            dve.sem_inc(s["proj_free"], 2)
            dve.sem_inc(s["sig_used"], 2)
            dve.wait_ge(s["small_in"], SMALL)
            setup_do = Steps(dve, s["setup_step"])
            setup_do(dve.tensor_tensor(ab[:, 0, :, :], ab[:, 0, :, :], ab[:, 1, :, :], ALU.mult))
            setup_do(dve.reduce_sum(ab_sum[:], ab[:, 0, :, :], AX.X))
            setup_do(dve.memset(decay[:], 1.0))
            dve.wait_ge(s["decay_ready"], 1)
            for c in range(DC):
                setup_do(dve.tensor_scalar(decay[:, c, :], decay[:, c, :], decay_col[:, c:c + 1], None, ALU.mult))

            def thought_norm(src, n, gamma, beta, after_stats=None):
                do = Steps(dve, s["dve_step"], n * TSTEPS, TSTEPS)
                do(dve.bn_stats(raw[:], src))
                do(dve.tensor_tensor(mean[:], raw[:, 1:2], raw[:, 4:5], ALU.add))
                do(dve.tensor_tensor(var[:], raw[:, 1:2], raw[:, 4:5], ALU.subtract))
                do(dve.tensor_tensor(var[:], var[:], var[:], ALU.mult))
                do(dve.scalar_tensor_tensor(out=var[:], in0=raw[:, 2:3], scalar=4.0 / D, in1=var[:],
                                            op0=ALU.mult, op1=ALU.add))
                do(dve.scalar_tensor_tensor(out=var[:], in0=raw[:, 5:6], scalar=4.0 / D, in1=var[:],
                                            op0=ALU.mult, op1=ALU.add))
                do(dve.tensor_scalar(mean[:], mean[:], 0.5, None, ALU.mult))
                do(dve.tensor_scalar(var[:], var[:], 0.25, 1e-6, ALU.mult, ALU.add))
                dve.wait_ge(s["rstd_ready"], n + 1)
                do(dve.tensor_scalar(tnorm[:], src, mean[:, 0:1], rstd[:, 0:1], ALU.subtract, ALU.mult))
                do(dve.tensor_tensor(tnorm[:], tnorm[:], rows[:, gamma, :], ALU.mult))
                do(dve.tensor_tensor(tnorm[:], tnorm[:], rows[:, beta, :], ALU.add))
                do.close()

            dve.wait_ge(s["last_in"], 16)
            thought_norm(last_rows[:], 0, 0, 1)
            dve.wait_ge(s["t_turned"], 1)
            dve.tensor_copy(tT[:], pS[:, 0:DC * B].rearrange("p (c b) -> p c b", b=B)).then_inc(s["t_copied"], 1)
            dve.wait_ge(s["rows_done"], 1)
            out_do = Steps(dve, s["out_step"], 0, 1)
            out_do(dve.tensor_tensor(thought[:], pR[0:B, 0:D], rows[:, 2, :], ALU.add))
            with dve.Fori(0, B) as b:
                thought_norm(thought[:], b + 1, 3, 4)
                for o in range(DC):
                    dve.wait_ge(s["c_ready"], 2 * b + o + 1)
                    dve.wait_ge(s["sig_ready"], 2 * b + o + 1)
                    dve.scalar_tensor_tensor(out=drive[:, o, :], in0=pC[:, o, :], scalar=cols[:, 0, o:o + 1],
                                             in1=sig[:, o, :], op0=ALU.add, op1=ALU.mult).then_inc(s["sig_used"], 1)
                    dve.wait_ge(s["sig_used"], 2 * b + o + 5)
                    dve.wait_ge(s["gate_ready"], 2 * b + o + 1)
                    dve.tensor_tensor_scan(gsT[:, o, bass.ds(b * T, T)], decay[:, o, :], drive[:, o, :], 0.0,
                                           ALU.mult, ALU.add).then_inc(s["proj_free"], 1)
                dve.wait_ge(s["t_turned"], b + 2)
                dve.tensor_copy(tT[:], pS[:, 0:DC * B].rearrange("p (c b) -> p c b", b=B)).then_inc(s["t_copied"], 1)
                dve.wait_ge(s["h_ready"], b + 1)
                dve.tensor_tensor(hT[:], pS[:, 64:64 + HC * B].rearrange("p (h b) -> p h b", b=B),
                                  b1[:].unsqueeze(2).to_broadcast([P, HC, B]), ALU.add).then_inc(s["h_biased"], 1)
                dve.wait_ge(s["rows_done"], b + 2)
                out_b = Steps(dve, s["out_step"], 1 + 2 * b, 2)
                out_b(dve.tensor_tensor(thought[:], pR[0:B, 0:D], thought[:], ALU.add))
                out_b(dve.tensor_tensor(thought[:], thought[:], rows[:, 5, :], ALU.add))
                out_b.close()
            dve.wait_ge(s["t_turned"], KS + 2)
            dve.tensor_copy(tT[:], pS[:, 0:DC * B].rearrange("p (c b) -> p c b", b=B)).then_inc(s["t_copied"], 1)
            dve.wait_ge(s["bc_ready"], 1)
            dve.tensor_tensor(core.bcT[:], pR[:, 256:256 + DC * B].rearrange("p (c b) -> p c b", b=B),
                              cols[:, 3, :].unsqueeze(2).to_broadcast([P, DC, B]), ALU.add
                              ).then_inc(s["bc_done"], 1)
            dve.wait_ge(s["bc_done"], 1)
            for c in range(DC):
                for b in range(B):
                    dve.scalar_tensor_tensor(out=gateT[:, c, b * T:(b + 1) * T], in0=gateT[:, c, b * T:(b + 1) * T],
                                             scalar=core.bcT[:, c, b:b + 1], in1=core.xnT[:, c, b * T:(b + 1) * T],
                                             op0=ALU.mult, op1=ALU.add)


def layer0_join(nc, st, core, dram, gsT, ffT):
    sem = st.sem
    y = core.xn
    SLOTS = 4
    slot = st.sb("slot", [P, SLOTS, 2 * DC, P])
    gb = st.sb("gb", [P, 2, D])
    raw = st.sb("raw", [P, TILES, 6])
    mean, var, rstd = (st.sb(n, [P, TILES]) for n in ("mean", "var", "rstd"))
    back = st.ps("back", [P, SLOTS, 512])
    gb_in, slot_ready, slot_free, turned = (sem(n) for n in ("gb_in", "slot_ready", "slot_free", "turned"))
    dve_step, rstd_ready = sem("dve_step"), sem("rstd_ready")
    scaled, gained, shifted, act_waited, pool_waited = (sem(n) for n in (
        "scaled", "gained", "shifted", "act_waited", "pool_waited"))
    with nc.Block() as block:
        @block.sync
        def _(sp):
            for k, n in enumerate(("L0_ffn_out_gamma", "L0_ffn_out_beta")):
                sp.dma_start(gb[:, k, :], on_all_partitions(dram[n], P)).then_inc(gb_in, 16)

        @block.gpsimd
        def _(pool):
            pool.wait_ge(dve_step, 7)
            pool.tensor_tensor(rstd[:], var[:], core.consts[:, C_HALF:C_HALF + TILES],
                               ALU.pow).then_inc(rstd_ready, 1)
            with pool.Fori(0, GROUPS) as g:
                wait_apart(pool, shifted, g + 1, pool_waited)
                x = core.x[:, bass.ds(2 * g, 2), :]
                pool.tensor_tensor(x, y[:, bass.ds(2 * g, 2), :], x, ALU.add)

        @block.scalar
        def _(act):
            act.preload_act_table(ACT.Copy)
            with act.Fori(0, TILES // SLOTS) as i:
                for j in range(SLOTS):
                    g, p = SLOTS // 2 * i + j // 2, j % 2
                    wait_apart(act, slot_free, SLOTS * i + j + 1, act_waited)
                    for c in range(DC):
                        act.activation(slot[:, j, c, :], col_group(gsT, g, p)[:, c, :], ACT.Copy,
                                       scale=core.ab_sum[:, c:c + 1])
                    act.activation(slot[:, j, DC:2 * DC, :], col_group(ffT, g, p), ACT.Copy).then_inc(slot_ready, 1)

        @block.tensor
        def _(pe):
            with pe.Fori(0, TILES // SLOTS) as i:
                for j in range(SLOTS):
                    pe.wait_ge(slot_ready, SLOTS * i + j + 1)
                    for k in range(2 * DC):
                        ins = pe.transpose(back[:, j, k * P:(k + 1) * P], slot[:, j, k, :], core.ident)
                    ins.then_inc(turned, 1)

        @block.vector
        def _(dve):
            dve.sem_inc(slot_free, SLOTS)
            with dve.Fori(0, TILES // SLOTS) as i:
                for j in range(SLOTS):
                    t = SLOTS * i + j
                    dve.wait_ge(turned, t + 1)
                    dve.tensor_tensor(core.x[:, t, :], back[:, j, 0:D], core.x[:, t, :], ALU.add)
                    dve.bn_stats(raw[:, t, :], back[:, j, D:2 * D])
                    dve.tensor_copy(y[:, t, :], back[:, j, D:2 * D]).then_inc(slot_free, 1)
            dve.wait_ge(slot_free, TILES + SLOTS)
            do = Steps(dve, dve_step)
            small_stats(do, dve, raw, mean, var, 1e-6, False)
            dve.wait_ge(rstd_ready, 1)
            dve.wait_ge(gb_in, 32)
            with dve.Fori(0, GROUPS) as g:
                for p in range(2):
                    t = 2 * g + p
                    dve.tensor_scalar(y[:, t, :], y[:, t, :], mean[:, bass.ds(t, 1)], rstd[:, bass.ds(t, 1)],
                                      ALU.subtract, ALU.mult).then_inc(scaled, 1)
                pair = y[:, bass.ds(2 * g, 2), :]
                dve.wait_ge(scaled, 2 * g + 2)
                dve.tensor_tensor(pair, pair, gb[:, 0, :].unsqueeze(1).to_broadcast([P, 2, D]),
                                  ALU.mult).then_inc(gained, 1)
                dve.wait_ge(gained, g + 1)
                dve.tensor_tensor(pair, pair, gb[:, 1, :].unsqueeze(1).to_broadcast([P, 2, D]),
                                  ALU.add).then_inc(shifted, 1)


def layer1_attention(nc, st, core):
    sem = st.sem
    HD, H2 = 16, 8
    keys = st.sb("keys", [P, 2, DC, P])
    vals = st.sb("vals", [P, 2, H2, HD + 1])
    e = st.sb("e", [P, 2, H2, P])
    inv, part = st.sb("inv", [P, 2, H2]), st.sb("part", [P, 2, H2, HD])
    ps = st.ps("scores", [P, 4, 2, DC, P])
    po = st.ps("out", [P, 2, 512])
    ones, keys_ready, vals_ready, scores_ready = (sem(n) for n in ("ones", "keys_ready", "vals_ready", "scores_ready"))
    exp_ready, masked, out_ready, inv_ready, scaled, tile_done = (sem(n) for n in (
        "exp_ready", "masked", "out_ready", "inv_ready", "scaled", "tile_done"))
    heads = [(c, j) for c in range(DC) for j in range(4)]

    def own(t, p):
        return t.rearrange("q (h two d) -> q h two d", two=2, d=HD)[:, :, p, :]

    with nc.Block() as block:
        @block.gpsimd
        def _(pool):
            pool.memset(vals[:], 1.0).then_inc(ones, 1)
            pool.wait_ge(ones, 1)
            with pool.Fori(0, GROUPS) as g:
                for p in range(2):
                    pool.wait_ge(scores_ready, 2 * g + p + 1)
                    pool.tensor_tensor(keys[:, p, :, :], col_group(core.xnT, g, p),
                                       core.consts[:, C_EVEN + p:C_EVEN + p + 1].unsqueeze(2).to_broadcast([P, DC, P]),
                                       ALU.mult).then_inc(keys_ready, 1)
                    pool.wait_ge(out_ready, 2 * g + p + 1)
                    pool.tensor_copy(vals[:, p, :, 0:HD],
                                     own(core.xn[:, bass.ds(2 * g + p, 1), :].rearrange("q t d -> q (t d)"), p)
                                     ).then_inc(vals_ready, 1)

        @block.tensor
        def _(pe):
            pe.sem_inc(scores_ready, 2)
            pe.sem_inc(out_ready, 2)

            def scores(g, p, first=False):
                pe.wait_ge(keys_ready, 2 * g + p + 1)
                if not first:
                    pe.wait_ge(exp_ready, 2 * g + p)
                for h, (c, j) in enumerate(heads):
                    rows = keys[32 * j:32 * j + 32, p, c, :]
                    ins = pe.matmul(ps[:, j, p, c, :], rows, rows, start=True, stop=True)
                ins.then_inc(scores_ready, 1)

            def values(g, p):
                pe.wait_ge(masked, 2 * g + p + 1)
                pe.wait_ge(vals_ready, 2 * g + p + 1)
                for h in range(H2):
                    ins = pe.matmul(po[:, p, h * (HD + 1):(h + 1) * (HD + 1)], e[:, p, h, :], vals[:, p, h, :],
                                    start=True, stop=True)
                ins.then_inc(out_ready, 1)

            scores(0, 0, first=True)
            with pe.Fori(0, GROUPS - 1) as g:
                scores(g, 1)
                values(g, 0)
                scores(g + 1, 0)
                values(g, 1)
            scores(GROUPS - 1, 1)
            values(GROUPS - 1, 0)
            values(GROUPS - 1, 1)

        @block.scalar
        def _(act):
            act.preload_act_table(ACT.Exp)
            with act.Fori(0, GROUPS) as g:
                for p in range(2):
                    act.wait_ge(scores_ready, 2 * g + p + 3)
                    act.activation(e[:, p, :, :].rearrange("q (c j) k -> q j c k", c=DC), ps[:, :, p, :, :], ACT.Exp,
                                   scale=HD ** -0.5).then_inc(exp_ready, 1)

        @block.vector
        def _(dve):
            def mask(g, p):
                dve.wait_ge(exp_ready, 2 * g + p + 1)
                dve.tensor_tensor(e[:, p, :, :], e[:, p, :, :], core.blk.unsqueeze(1).to_broadcast([P, H2, P]),
                                  ALU.mult).then_inc(masked, 1)

            def finish(g, p):
                n = 2 * g + p
                dve.wait_ge(out_ready, n + 3)
                o = po[:, p, 0:H2 * (HD + 1)].rearrange("q (h d) -> q h d", h=H2)
                dve.reciprocal(inv[:, p, :], o[:, :, HD]).then_inc(inv_ready, 1)
                dve.wait_ge(inv_ready, n + 1)
                dve.tensor_tensor(part[:, p, :, :], o[:, :, 0:HD],
                                  inv[:, p, :].unsqueeze(2).to_broadcast([P, H2, HD]), ALU.mult
                                  ).then_inc(scaled, 1)
                dve.wait_ge(scaled, n + 1)
                x = own(core.x[:, bass.ds(n, 1), :].rearrange("q t d -> q (t d)"), p)
                dve.tensor_tensor(x, x, part[:, p, :, :], ALU.add).then_inc(tile_done, 1)
                dve.wait_ge(tile_done, n + 1)

            mask(0, 0)
            with dve.Fori(0, GROUPS - 1) as g:
                mask(g, 1)
                finish(g, 0)
                mask(g + 1, 0)
                finish(g, 1)
            mask(GROUPS - 1, 1)
            finish(GROUPS - 1, 0)
            finish(GROUPS - 1, 1)


def split(nc, st, src, dst):
    hi_ready = st.sem("hi_ready")
    with nc.Block() as block:
        @block.scalar
        def _(act):
            for b in range(B):
                cols = slice(b * T, (b + 1) * T)
                act.activation(dst.hi[:, :, cols], src[:, :, cols], ACT.Copy).then_inc(hi_ready, 1)

        @block.vector
        def _(dve):
            for b in range(B):
                cols = slice(b * T, (b + 1) * T)
                dve.wait_ge(hi_ready, b + 1)
                dve.tensor_tensor(dst.lo[:, :, cols], src[:, :, cols], dst.hi[:, :, cols].bitcast(F32), ALU.subtract)


def layer2_abc(nc, st, core, dram, a):
    sem = st.sem
    HP, DK, DV, NCH = 8, 64, 128, TB
    PV = 2 * DV
    PER = 2 * B
    ROUNDS = HP // 2
    ones = st.sb("ones", [P, T])
    WQ, WC = 3 * DC * P, 3 * DC * P + 2 * DC * PV
    w_raw, w_in_parts = st.sb("w_raw", [P, 2, WC]), st.sb_parts("w", [P, 2, WC])
    w_o = st.sb("w_o", [P, 2, 2, D])
    gnorm = st.sb("gnorm", [P, 1])
    qT, kT, eT = (st.sb(n, [P, 2, T]) for n in ("qT", "kT", "eT"))
    rT = st.sb("rT", [P, T])
    k_tok, e_tok, r_tok = (st.sb(n, [P, 2, NCH, P]) for n in ("k_tok", "e_tok", "r_tok"))
    v, gate = (st.sb(n, [P, 2, NCH, PV]) for n in ("v", "gate"))
    th = st.sb("th", [P, NCH, PV])
    sm, am = st.sb("sm", [P, 2, NCH, P]), st.sb("am", [P, 2, NCH, P])
    hk, hv = st.sb("hk", [P, 3, P]), st.sb("hv", [P, 3, DV])
    lg, ex, wt = (st.sb(n, [P, NCH, P]) for n in ("lg", "ex", "wt"))
    wT = st.sb("wT", [P, T])
    mx, den = st.sb("mx", [P, 8]), st.sb("den", [P, 8])
    on, gr = (st.sb(n, [P, 2, NCH, DV]) for n in ("on", "gr"))
    sq = on
    ms, rstd = st.sb("ms", [P, 8]), st.sb("rstd", [P, 8])
    oT = st.sb("oT", [P, 2, T])
    ring = [st.ps(f"ring{k}", [P, T]) for k in range(3)]
    pab = st.ps("pab", [P, 2, T])
    pc = st.ps("pc", [P, T])
    pde = st.ps("pde", [P, 2, T])
    names = ("once_in q_ready k_ready s_ready v_ready g_ready q_copied k_copied s_clipped e_ready "
             "c_ready r_ready v_copied tanh_ready gate_ready k_turned e_turned r_turned k_tok_ready e_tok_ready "
             "r_tok_ready scores_ready sm_ready hk_sums hk_step ok_ready hv_sums hv_step zeros logit_step ex_ready "
             "er_ready den_step wt_ready w_turned wT_ready am_sums am_ready ov_ready sq_ready ms_step rstd_ready "
             "gr_ready on_ready o_turned oT_ready y_ready y_added").split()
    s = {n: sem(n) for n in names}
    w_in, w_hi, w_split = [sem("w0_in"), sem("w1_in")], sem("w_hi"), sem("w_split")
    FILL = {n: k for k, n in enumerate("s q k v0 v1 g0 g1 kt et rt hv".split())}
    taken_by = ("s_clipped", "q_copied", "k_copied", "v_copied", "v_copied", "gate_ready", "gate_ready",
                "k_tok_ready", "e_tok_ready", "r_tok_ready", "hv_step")
    per_unit = {"v_copied": 2, "gate_ready": 2, "hv_step": 3, "v_ready": 2, "g_ready": 2, "tanh_ready": 2}

    def bank(name):
        return ring[FILL[name] % 3]

    def chunks(a):
        return a.rearrange("t (c m) -> t c m", c=NCH)

    pst = pab[:].rearrange("j h (c t) -> j h c t", c=NCH)
    pov = pde[:].rearrange("t h (c v) -> t h c v", c=NCH)
    pyy = pab[:].rearrange("t b (c v) -> t (b c) v", v=PV)
    heads8 = lambda a: a.rearrange("t c (h m) -> t (c h) m", h=2)

    def w_qks(t, slot):
        return t[:, slot, 0:WQ].rearrange("p (k c n) -> p k c n", k=3, c=DC)

    def w_vg(t, slot):
        return t[:, slot, WQ:WC].rearrange("p (k c n) -> p k c n", k=2, c=DC)

    def load(sp, slot, hp):
        for k, n in enumerate(("Ws", "Wq", "Wk")):
            sp.dma_start(w_qks(w_raw, slot)[:, k, :, :], in_chunks(dram["L2_attn_" + n])[:, :, bass.ds(hp * P, P)]
                         ).then_inc(w_in[slot], 16)
        for k, n in enumerate(("Wv", "Wg")):
            sp.dma_start(w_vg(w_raw, slot)[:, k, :, :], in_chunks(dram["L2_attn_" + n])[:, :, bass.ds(hp * PV, PV)]
                         ).then_inc(w_in[slot], 16)
        sp.dma_start(w_o[:, slot, :, :], in_chunks(dram["L2_attn_Wo"])[:, bass.ds(hp * 2, 2), :]
                     ).then_inc(w_in[slot], 16)

    def split_in(u, k):
        return {2: (1, (u - k) * (96 // PER) + 96), 6: (0, (u - k) * (96 // PER) + 192)}.get(k)

    def last_round(u):
        return isinstance(u, int) and u >= PER * (ROUNDS - 1)

    def rounds(eng, unit):
        for k in range(PER):
            unit(k, k, k == 0, False)
        with eng.Fori(1, ROUNDS - 1) as i:
            for k in range(PER):
                unit(i * PER + k, k, False, False)
        for k in range(PER):
            unit((ROUNDS - 1) * PER + k, k, False, k == PER - 1)

    with nc.Block() as block:
        @block.sync
        def _(sp):
            sp.dma_start(gnorm[:], dram["L2_attn_g_norm_weight"].unsqueeze(1),
                         allow_slow_non_contiguous=True).then_inc(s["once_in"], 16)
            for slot in range(2):
                load(sp, slot, slot)
            with sp.Fori(1, ROUNDS) as i:
                for slot in range(2):
                    sp.wait_ge(s["y_ready"], (i - 1) * PER + (slot + 1) * B)
                    load(sp, slot, i * 2 + slot)

        @block.gpsimd
        def _(pool):
            pool.memset(ones[:], 1.0).then_inc(s["zeros"], 1)
            pool.memset(hk[:], 0.0).then_inc(s["zeros"], 1)

            def rest_of_weights(slot, n):
                pool.wait_ge(w_hi, n)
                pool.tensor_tensor(w_in_parts.lo[:, slot, :], w_raw[:, slot, :],
                                   w_in_parts.hi[:, slot, :].bitcast(F32), ALU.subtract).then_inc(w_split, B)

            def unit(u, k, first, last):
                pool.wait_ge(s["ex_ready"], u + 1)
                pool.wait_ge(s["r_tok_ready"], u + 1)
                pool.tensor_tensor(wt[:], ex[:], r_tok[:, k % 2], ALU.mult).then_inc(s["er_ready"], 1)
                pool.wait_ge(s["ms_step"], 2 * (u + 1))
                pool.tensor_tensor(rstd[:], ms[:], core.consts[:, C_HALF:C_HALF + 8], ALU.pow
                                   ).then_inc(s["rstd_ready"], 1)
                pool.wait_ge(s["rstd_ready"], u + 1)
                pool.wait_ge(s["gate_ready"], 2 * (u + 1))
                pool.tensor_tensor(gr[:].rearrange("t h c v -> t c h v"),
                                   gate[:, k % 2].rearrange("t c (h v) -> t c h v", h=2),
                                   rstd[:].rearrange("t (h c) -> t c h", h=2).unsqueeze(3).to_broadcast(
                                       [P, NCH, 2, DV]), ALU.mult).then_inc(s["gr_ready"], 1)
                if split_in(0, k) and not (k == 6 and last_round(u)):
                    rest_of_weights(split_in(0, k)[0], u + 2 * B - k % B)

            rest_of_weights(0, B)
            rounds(pool, unit)

        @block.tensor
        def _(pe):
            pe.wait_ge(s["zeros"], 2)

            def ring_free(name, u):
                n = FILL[name]
                if n >= 3:
                    by = taken_by[n - 3]
                    per = per_unit.get(by, 1)
                    step = 1 if n - 3 in (FILL["v0"], FILL["g0"]) else per
                    pe.wait_ge(s[by], per * u + step)
                else:
                    if isinstance(u, int) and u == 0:
                        return
                    by = {0: "r_tok_ready", 1: "hv_step", 2: "e_tok_ready"}[n]
                    per = per_unit.get(by, 1)
                    pe.wait_ge(s[by], per * u)

            def project_rows(name, u, k):
                b, slot = k % B, (k // B) % 2
                if name == "s" and b == 0:
                    pe.wait_ge(w_split, u + B)
                ring_free(name, u)
                for c in range(DC):
                    ins = split_matmul(pe, bank(name)[:],
                                       w_in_parts.view(lambda t: w_qks(t, slot)[:, FILL[name], c, :]),
                                       a.view(lambda t: t[:, c, b * T:(b + 1) * T]),
                                       start=(c == 0), stop=(c == DC - 1))
                ins.then_inc(s[name + "_ready"], 1)

            def project_tokens(name, half, u, k):
                b, slot = k % B, (k // B) % 2
                fill = name + str(half)
                ring_free(fill, u)
                for t in range(2):
                    at = b * T + (2 * half + t) * P
                    for c in range(DC):
                        ins = split_matmul(pe, bank(fill)[:, t * PV:(t + 1) * PV],
                                           a.view(lambda x: x[:, c, at:at + P]),
                                           w_in_parts.view(lambda x: w_vg(x, slot)[:, "vg".index(name), c, :]),
                                           start=(c == 0), stop=(c == DC - 1))
                ins.then_inc(s[name + "_ready"], 1)

            def turn(fill, src, need, done, u):
                ring_free(fill, u)
                pe.wait_ge(s[need], u + 1)
                for t in range(NCH):
                    ins = pe.transpose(bank(fill)[:, t * P:(t + 1) * P], src[:, t * P:(t + 1) * P], core.ident)
                ins.then_inc(s[done], 1)

            def scores(u, k):
                pe.wait_ge(s["k_copied"], u + 1)
                pe.wait_ge(s["q_copied"], u + 1)
                if not (isinstance(u, int) and u == 0):
                    pe.wait_ge(s["am_ready"], 2 * u)
                for c in range(NCH):
                    for h in range(2):
                        rows, cols = slice(DK * h, DK * h + DK), slice(c * P, (c + 1) * P)
                        ins = pe.matmul(pst[:, h, c, :], kT[rows, k % 2, cols], qT[rows, k % 2, cols],
                                        start=True, stop=True)
                ins.then_inc(s["scores_ready"], 1)

            def chunk_sums(u, k):
                pe.wait_ge(s["k_tok_ready"], u + 1)
                pe.wait_ge(s["e_tok_ready"], u + 1)
                if not (isinstance(u, int) and u == 0):
                    pe.wait_ge(s["wT_ready"], u)
                for c in range(3):
                    ins = pe.matmul(pc[:, c * P:(c + 1) * P], k_tok[:, k % 2, c, :], e_tok[:, k % 2, c, :],
                                    start=True, stop=True)
                ins.then_inc(s["hk_sums"], 1)
                pe.wait_ge(s["v_copied"], 2 * (u + 1))
                for c in range(3):
                    for h in range(2):
                        ins = pe.matmul(bank("hv")[DK * h:DK * h + DK, c * DV:(c + 1) * DV],
                                        e_tok[:, k % 2, c, DK * h:DK * h + DK],
                                        v[:, k % 2, c, DV * h:DV * h + DV], start=True, stop=True)
                ins.then_inc(s["hv_sums"], 1)

            def turn_out(u):
                pe.wait_ge(s["on_ready"], u + 1)
                for h in range(2):
                    for c in range(NCH):
                        ins = pe.transpose(pde[:, h, c * P:(c + 1) * P], on[:, h, c, :], core.ident)
                ins.then_inc(s["o_turned"], 1)

            def emit(u, k):
                slot = (k // B) % 2
                pe.wait_ge(s["oT_ready"], u + 1)
                for t in range(NCH):
                    for h in range(2):
                        cols = oT[:, h, :].rearrange("d (g q p) -> d g p q", q=P, p=2)[:, t // 2, t % 2, :]
                        ins = pe.matmul(pyy[:, t, :], cols, w_o[:, slot, h, :], start=(h == 0), stop=(h == 1))
                ins.then_inc(s["y_ready"], 1)

            def ok(u, k):
                pe.wait_ge(s["sm_ready"], 2 * (u + 1))
                pe.wait_ge(s["hk_step"], 6 * (u + 1))
                tok4 = chunks(pc[:])
                for c in range(NCH):
                    if c:
                        pe.matmul(tok4[:, c, :], qT[:, k % 2, c * P:(c + 1) * P], hk[:, c - 1, :], start=True,
                                  stop=False, skip_group_check=True)
                    for h in range(2):
                        m = slice(DK * h, DK * h + DK)
                        ins = pe.matmul(tok4[:, c, m], sm[:, h, c, :], e_tok[:, k % 2, c, m], start=(c == 0),
                                        stop=True, skip_group_check=True)
                ins.then_inc(s["ok_ready"], 1)

            def turn_w(u):
                pe.wait_ge(s["wt_ready"], u + 1)
                for t in range(NCH):
                    ins = pe.transpose(pc[:, t * P:(t + 1) * P], wt[:, t, :], core.ident)
                ins.then_inc(s["w_turned"], 1)

            def weights(u, k):
                pe.wait_ge(s["wT_ready"], u + 1)
                if not (isinstance(u, int) and u == 0):
                    pe.wait_ge(s["y_added"], u)
                for c in range(NCH):
                    for h in range(2):
                        rows, cols = slice(DK * h, DK * h + DK), slice(c * P, (c + 1) * P)
                        ins = pe.matmul(pst[:, h, c, :], eT[rows, k % 2, cols], wT[rows, cols], start=True, stop=True)
                ins.then_inc(s["am_sums"], 1)

            def ov(u, k):
                pe.wait_ge(s["hv_step"], 3 * (u + 1))
                for h in range(2):
                    pe.wait_ge(s["am_ready"], 2 * u + h + 1)
                    for c in range(NCH):
                        rows = slice(DK * h, DK * h + DK)
                        if c:
                            pe.matmul(pov[:, h, c, :], wT[rows, c * P:(c + 1) * P], hv[rows, c - 1, :],
                                      start=True, stop=False)
                        ins = pe.matmul(pov[:, h, c, :], am[:, h, c, :], v[:, k % 2, c, DV * h:DV * h + DV],
                                        start=(c == 0), stop=True)
                ins.then_inc(s["ov_ready"], 1)

            def part(steps, u, k):
                for x in steps.split():
                    if x in ("q", "k", "s"):
                        project_rows(x, u, k)
                    elif x[0] in "vg":
                        project_tokens(x[0], int(x[1]), u, k)
                    elif x == "kt":
                        turn("kt", kT[:, k % 2], "k_copied", "k_turned", u)
                    elif x == "et":
                        turn("et", eT[:, k % 2], "e_ready", "e_turned", u)
                    else:
                        turn("rt", rT[:], "r_ready", "r_turned", u)

            def unit(u, k, first, last):
                kn = (k + 1) % PER

                def project(steps):
                    if not last:
                        part(steps, u + 1, kn)

                scores(u, k)
                chunk_sums(u, k)
                project("s q k")
                ok(u, k)
                project("v0")
                if not first:
                    turn_out(u - 1)
                project("v1")
                if not first:
                    emit(u - 1, (k - 1) % PER)
                project("g0")
                turn_w(u)
                project("g1")
                weights(u, k)
                project("kt et rt")
                ov(u, k)

            part("s q k v0 v1 g0 g1 kt et rt", 0, 0)
            rounds(pe, unit)
            turn_out(HP * B - 1)
            emit(HP * B - 1, PER - 1)

        @block.scalar
        def _(act):
            act.preload_act_table(ACT.Exp)
            act.wait_ge(s["once_in"], 16)

            def split_weights(slot, loads):
                act.wait_ge(w_in[slot], loads)
                act.activation(w_in_parts.hi[:, slot, :], w_raw[:, slot, :], ACT.Copy).then_inc(w_hi, B)

            def copy(ready, n, out, in_, done, **kw):
                act.wait_ge(s[ready], n)
                act.activation(out, in_, ACT.Copy, **kw).then_inc(s[done], 1)

            def project_q(u, k):
                copy("q_ready", u + 1, qT[:, k % 2], bank("q")[:], "q_copied", scale=DK ** -0.5)

            def project_e(u, k):
                act.wait_ge(s["s_clipped"], u + 1)
                act.activation(eT[:, k % 2], eT[:, k % 2], ACT.Exp).then_inc(s["e_ready"], 1)

            def project_v(u, k, half):
                copy("v_ready", 2 * u + half + 1, v[:, k % 2, 2 * half:2 * half + 2],
                     bank(f"v{half}")[:].rearrange("t (c v) -> t c v", v=PV), "v_copied")

            def project_g(u, k, half):
                act.wait_ge(s["g_ready"], 2 * u + half + 1)
                act.activation(th[:, 2 * half:2 * half + 2], bank(f"g{half}")[:].rearrange("t (c v) -> t c v", v=PV),
                               ACT.Tanh, scale=0.5).then_inc(s["tanh_ready"], 1)

            def project_turned(u, k, names):
                for x, dst, n in (("kt", k_tok, "k"), ("et", e_tok, "e"), ("rt", r_tok, "r")):
                    if x in names:
                        copy(n + "_turned", u + 1, dst[:, k % 2], chunks(bank(x)[:]), n + "_tok_ready")

            def emit(u):
                act.wait_ge(s["o_turned"], u + 1)
                act.activation(oT[:], pde[:], ACT.Copy, scale=gnorm[:, 0:1]).then_inc(s["oT_ready"], 1)

            def unit(u, k, first, last):
                n, kn = u + 1, (k + 1) % PER
                if not last:
                    project_e(n, kn)
                    project_q(n, kn)
                    project_v(n, kn, 0)
                if not first:
                    emit(u - 1)
                if not last:
                    project_v(n, kn, 1)
                act.wait_ge(s["logit_step"], 3 * (u + 1))
                act.activation(ex[:], lg[:], ACT.Exp).then_inc(s["ex_ready"], 1)
                if not last:
                    project_g(n, kn, 0)
                copy("w_turned", u + 1, wT[:], pc[:], "wT_ready")
                if not last:
                    project_g(n, kn, 1)
                    project_turned(n, kn, ("kt", "et", "rt"))
                act.wait_ge(s["ov_ready"], u + 1)
                act.activation(sq[:], pov, ACT.Square).then_inc(s["sq_ready"], 1)
                if split_in(u, k) and not (k == 6 and last_round(u)):
                    split_weights(*split_in(u, k))

            split_weights(0, 96)
            project_e(0, 0)
            project_q(0, 0)
            project_v(0, 0, 0)
            project_v(0, 0, 1)
            project_g(0, 0, 0)
            project_g(0, 0, 1)
            project_turned(0, 0, ("kt", "et", "rt"))
            rounds(act, unit)
            emit(HP * B - 1)

        @block.vector
        def _(dve):
            dve.wait_ge(s["zeros"], 2)
            tri8 = core.tri.unsqueeze(1).to_broadcast([P, NCH, P])

            def project_s(u, k):
                dve.wait_ge(s["s_ready"], u + 1)
                dve.tensor_scalar(eT[:, k % 2], bank("s")[:], 32.0, -32.0, ALU.min, ALU.max
                                  ).then_inc(s["s_clipped"], 1)

            def project_k(u, k):
                dve.wait_ge(s["k_ready"], u + 1)
                dve.tensor_copy(kT[:, k % 2], bank("k")[:]).then_inc(s["k_copied"], 1)

            def project_c(u, k):
                dve.wait_ge(s["e_ready"], u + 1)
                dve.tensor_tensor_scan(rT[:], ones[:], eT[:, k % 2], 0.0, ALU.mult, ALU.add).then_inc(s["c_ready"], 1)
                dve.wait_ge(s["c_ready"], u + 1)
                dve.reciprocal(rT[:], rT[:]).then_inc(s["r_ready"], 1)

            def project_g(u, k, half):
                c = slice(2 * half, 2 * half + 2)
                dve.wait_ge(s["tanh_ready"], 2 * u + half + 1)
                dve.scalar_tensor_tensor(out=gate[:, k % 2, c], in0=th[:, c], scalar=1.0,
                                         in1=bank(f"g{half}")[:].rearrange("t (c v) -> t c v", v=PV),
                                         op0=ALU.add, op1=ALU.mult).then_inc(s["gate_ready"], 1)

            def mask(ready, dst, done, u):
                dve.wait_ge(s[ready], u + 1)
                for h in range(2):
                    dve.tensor_tensor(dst[:, h], pst[:, h], tri8, ALU.mult).then_inc(s[done], 1)

            def prefix_v(u):
                dve.wait_ge(s["hv_sums"], u + 1)
                do = Steps(dve, s["hv_step"], 3 * u, 3)
                for c in range(3):
                    new = bank("hv")[:, c * DV:(c + 1) * DV]
                    if c:
                        do(dve.tensor_tensor(hv[:, c, :], new, hv[:, c - 1, :], ALU.add))
                    else:
                        do(dve.tensor_copy(hv[:, c, :], new))
                do.close()

            def prefix_k(u):
                dve.wait_ge(s["hk_sums"], u + 1)
                do = Steps(dve, s["hk_step"], 6 * u, 6)
                for c in range(3):
                    for h in range(2):
                        r = slice(DK * h, DK * h + DK)
                        new = pc[r, c * P + DK * h:c * P + DK * h + DK]
                        if c:
                            do(dve.tensor_tensor(hk[r, c, r], new, hk[r, c - 1, r], ALU.add))
                        else:
                            do(dve.tensor_copy(hk[r, c, r], new))
                do.close()

            def mean_square(u):
                dve.wait_ge(s["sq_ready"], u + 1)
                do = Steps(dve, s["ms_step"], 2 * u, 2)
                do(dve.reduce_sum(ms[:], sq[:].rearrange("t h c v -> t (h c) v"), AX.X))
                do(dve.tensor_scalar(ms[:], ms[:], 4.0 / DV, 4e-5, ALU.mult, ALU.add))
                do.close()

            def gated(u):
                dve.wait_ge(s["gr_ready"], u + 1)
                dve.tensor_tensor(on[:], pov, gr[:], ALU.mult).then_inc(s["on_ready"], 1)

            def emit(u, k):
                dve.wait_ge(s["y_ready"], u + 1)
                b = k % B
                x = core.x[:, 4 * b:4 * b + 4, :]
                dve.tensor_tensor(x, pyy, x, ALU.add).then_inc(s["y_added"], 1)

            def unit(u, k, first, last):
                n, kn = u + 1, (k + 1) % PER
                mask("scores_ready", sm, "sm_ready", u)
                prefix_v(u)
                if not last:
                    project_s(n, kn)
                prefix_k(u)
                if not first:
                    gated(u - 1)
                if not last:
                    project_k(n, kn)
                    project_c(n, kn)
                dve.wait_ge(s["ok_ready"], u + 1)
                dve.wait_ge(s["r_tok_ready"], u + 1)
                do = Steps(dve, s["logit_step"], 3 * u, 3)
                do(dve.tensor_tensor(lg[:], chunks(pc[:]), r_tok[:, k % 2], ALU.mult))
                do(dve.tensor_reduce(mx[:], heads8(lg[:]), AX.X, ALU.max))
                do(dve.tensor_tensor(heads8(lg[:]), heads8(lg[:]), mx[:].unsqueeze(2).to_broadcast([P, 8, DK]),
                                     ALU.subtract))
                do.close()
                dve.wait_ge(s["ex_ready"], u + 1)
                do = Steps(dve, s["den_step"], 2 * u, 2)
                do(dve.reduce_sum(den[:], heads8(ex[:]), AX.X))
                do(dve.reciprocal(den[:], den[:]))
                do.close()
                dve.wait_ge(s["er_ready"], u + 1)
                dve.tensor_tensor(heads8(wt[:]), heads8(wt[:]), den[:].unsqueeze(2).to_broadcast([P, 8, DK]),
                                  ALU.mult).then_inc(s["wt_ready"], 1)
                if not first:
                    emit(u - 1, (k - 1) % PER)
                if not last:
                    project_g(n, kn, 0)
                    project_g(n, kn, 1)
                mask("am_sums", am, "am_ready", u)
                mean_square(u)

            project_s(0, 0)
            project_k(0, 0)
            project_c(0, 0)
            project_g(0, 0, 0)
            project_g(0, 0, 1)
            rounds(dve, unit)
            gated(HP * B - 1)
            emit(HP * B - 1, PER - 1)


def layer2_attention(nc, st, core, dram, aT):
    sem = st.sem
    H, LAT = 16, 64
    w_kvq = st.sb("w_kvq", [P, DC, P])
    w_low = st.sb("w_low", [P, 2, D])
    w_kr, w_kt = st.sb("w_kr", [P, DC, D]), st.sb("w_kt", [P, DC, D])
    w_o = st.sb("w_o", [P, DC, D])
    rope = st.sb("rope", [P, 2, T])
    low = st.sb("low", [P, T])
    turn = st.sb("turn", [P, 2, T])
    qT, kT = st.sb("qT", [P, DC, T]), st.sb("kT", [P, DC, T])
    keys = st.sb("keys", [P, 2, DC, T])
    v = st.sb("v", [P, 2, TB, D])
    r32 = mybir.dt.float32r
    mask = st.scope.enter_context(nc.sbuf_tensor(st.name + "_mask", [P, 2, P], r32))
    pr, prT = st.sb("pr", [P, 2, TB, T]), st.sb("prT", [P, 2, TB, T])
    nmax = st.sb("nmax", [P, 2, TB])
    total = st.sb("total", [P, H, TB])
    sums, o, oT = st.sb("sums", [P, DC, T]), st.sb("o", [P, TB, D]), st.sb("oT", [P, DC, T])
    pa, pw, po = st.ps("pa", [P, 4, T]), st.ps("pw", [P, 2, T]), st.ps("po", [P, DC, T])
    (w_in, low_ready, low_copied, rot_ready, rot_step, rot_done, keys_ready, v_ready, v_copied, scores_ready,
     max_ready, exp_ready, turned, even_copied, odd_copied, heads_out, zeros, mask_ready, sums_copied, sums_turned,
     norm_step, o_turned, o_copied, y_ready, y_added, pool_waited) = (
        sem(n) for n in ("w_in low_ready low_copied rot_ready rot_step rot_done keys_ready v_ready v_copied "
                         "scores_ready max_ready exp_ready turned even_copied odd_copied heads_out zeros mask_ready "
                         "sums_copied sums_turned norm_step "
                         "o_turned o_copied y_ready y_added pool_waited").split())
    loads = [(w_kvq[:], in_chunks(dram["L2_kvq_d"])), (w_low[0:LAT, 0, :], dram["L2_k_plain"]),
             (w_low[0:LAT, 1, :], dram["L2_ffn_v_u_w"]), (w_low[LAT:P, 0, :], dram["L2_q_both"]),
             (w_low[LAT:P, 1, :], dram["L2_q_turned"]), (w_kr[:], in_chunks(dram["L2_k_rope"])),
             (w_kt[:], in_chunks(dram["L2_k_turned"])), (w_o[:], in_chunks(dram["L2_ffn_o_w"])),
             (rope[:], dram["rope"].rearrange("k p t -> p k t"))]
    p_low, po_T = pa[:, 3, :], pw
    po_v = po[:].rearrange("q a (t d) -> q (a t) d", d=D)
    pw_tok = pw[:].rearrange("q a (t d) -> q (a t) d", d=D)
    py = pw_tok
    copied = (even_copied, odd_copied)

    def sequences(eng, change, heads):
        change(None, 0)
        with eng.Fori(0, B - 1) as b:
            heads(b)
            change(b, b + 1)
        heads(B - 1)
        change(B - 1, None)

    def own(t, p):
        return t.rearrange("q t (h two d) -> q t h two d", two=2, d=16)[:, :, :, p, :]
    with nc.Block() as block:
        @block.sync
        def _(sp):
            for dst, src in loads:
                sp.dma_start(dst, src).then_inc(w_in, 16)

        @block.tensor
        def _(pe):
            pe.wait_ge(w_in, 16 * len(loads))

            def scores(b, h, k):
                q = QB_ORDER[k]
                c, j, other = h // 8, (h % 8) // 2, h % 2
                rows = slice(32 * j, 32 * j + 32)
                n = (q + 1) * P
                if h:
                    pe.wait_ge(exp_ready, TB * H * b + TB * (h - 1) + k + 1)
                pe.matmul(pa[:, q, 0:n], qT[rows, c, q * P:(q + 1) * P], keys[rows, other, c, 0:n],
                          start=True, stop=False, skip_group_check=True)
                pe.matmul(pa[:, q, n - P:n], mask[:, 0, :], mask[:, 1, :], start=False, stop=True,
                          skip_group_check=True).then_inc(scores_ready, 1)

            def turn(b, h, k):
                n = H * b + h
                pe.wait_ge(exp_ready, TB * (n + 1))
                pe.wait_ge(copied[k % 2], 2 * n + k // 2 + 1)
                if h == 0 and k < 2:
                    pe.wait_ge(y_added, b + 1)
                for q in range(k, TB):
                    ins = pe.transpose(pw[:, k % 2, q * P:(q + 1) * P], pr[:, h % 2, q, k * P:(k + 1) * P], core.ident)
                ins.then_inc(turned, 1)

            def values(b, h, k):
                n = H * b + h
                pe.wait_ge(copied[k % 2], 2 * n + k // 2 + 2)
                pair = h // 2
                ins = pe.matmul(po[32 * (pair % 4):32 * (pair % 4) + 32, pair // 4, k * P:T],
                                v[:, h % 2, k, 32 * pair:32 * pair + 32], prT[:, h % 2, k, k * P:T],
                                start=(h % 2 == 0 and k == 0), stop=(h % 2 == 1 and k == TB - 1),
                                skip_group_check=True)
                if k == TB - 1:
                    ins.then_inc(heads_out, 1)

            def low_rank(b):
                for c in range(DC):
                    ins = pe.matmul(p_low, w_kvq[:, c, :], aT[:, c, bass.ds(b * T, T)], start=(c == 0),
                                    stop=(c == DC - 1))
                ins.then_inc(low_ready, 1)

            def key_products(b, o_):
                cols = slice(o_ * P, (o_ + 1) * P)
                x = [aT[:, c, bass.ds(b * T, T)] for c in range(DC)]
                pe.wait_ge(low_copied, b + 1)
                pe.matmul(pa[:, 2 * o_, :], w_low[0:LAT, 0, cols], low[0:LAT, :], start=True, stop=False)
                for c in range(DC):
                    pe.matmul(pa[:, 2 * o_, :], w_kr[:, c, cols], x[c], start=False, stop=(c == DC - 1))
                for c in range(DC):
                    ins = pe.matmul(pa[:, 2 * o_ + 1, :], w_kt[:, c, cols], x[c], start=(c == 0), stop=(c == DC - 1))
                ins.then_inc(rot_ready, 1)

            def value_products(b):
                for t in range(TB):
                    ins = pe.matmul(po_v[:, t, :], low[0:LAT, t * P:(t + 1) * P], w_low[0:LAT, 1, :],
                                    start=True, stop=True)
                ins.then_inc(v_ready, 1)

            def query_products(b, o_):
                cols = slice(o_ * P, (o_ + 1) * P)
                pe.wait_ge(rot_done, 4 * b + o_ + 1)
                for k in range(2):
                    ins = pe.matmul(pa[:, 2 * o_ + k, :], w_low[LAT:P, k, cols], low[LAT:P, :], start=True, stop=True)
                ins.then_inc(rot_ready, 1)

            def turn_back(b):
                pe.wait_ge(sums_copied, b + 1)
                for t in range(TB):
                    for c in range(DC):
                        ins = pe.transpose(pw_tok[:, t, c * P:(c + 1) * P], sums[:, c, t * P:(t + 1) * P], core.ident)
                ins.then_inc(sums_turned, 1)

            def turn_o(b):
                pe.wait_ge(norm_step, 2 * (b + 1))
                for t in range(TB):
                    for c in range(DC):
                        ins = pe.transpose(po_T[:, c, t * P:(t + 1) * P], o[:, t, c * P:(c + 1) * P], core.ident)
                ins.then_inc(o_turned, 1)

            def output(b):
                pe.wait_ge(o_copied, b + 1)
                for t in range(TB):
                    for c in range(DC):
                        cols = oT[:, c, :].rearrange("d (g q p) -> d g p q", q=P, p=2)[:, t // 2, t % 2, :]
                        ins = pe.matmul(py[:, t, :], cols, w_o[:, c, :], start=(c == 0), stop=(c == DC - 1))
                ins.then_inc(y_ready, 1)

            def change(e, n):
                if n is not None:
                    low_rank(n)
                if e is not None:
                    turn_back(e)
                if n is not None:
                    key_products(n, 0)
                if e is not None:
                    turn_o(e)
                if n is not None:
                    key_products(n, 1)
                    value_products(n)
                if e is not None:
                    output(e)
                if n is not None:
                    query_products(n, 0)
                    query_products(n, 1)

            def heads(b):
                pe.wait_ge(keys_ready, 2 * (b + 1))
                pe.wait_ge(rot_done, 4 * (b + 1))
                pe.wait_ge(v_copied, b + 1)
                pe.wait_ge(mask_ready, 2)
                for h in range(H + 2):
                    if 1 <= h <= H:
                        turn(b, h - 1, 0)
                        turn(b, h - 1, 1)
                    if h < H:
                        for k in range(TB):
                            scores(b, h, k)
                    if 1 <= h <= H:
                        turn(b, h - 1, 2)
                        turn(b, h - 1, 3)
                    if h >= 2:
                        for k in range(TB):
                            values(b, h - 2, k)

            sequences(pe, change, heads)

        @block.gpsimd
        def _(pool):
            pool.memset(v[:], 0.0).then_inc(zeros, 1)

            def change(e, n):
                if n is not None:
                    pool.wait_ge(rot_done, 4 * n + 2)
                    for k in range(2):
                        pool.tensor_tensor(keys[:, k, :, :], kT[:], core.consts[:, C_KEYS + k:C_KEYS + k + 1].unsqueeze(
                            2).to_broadcast([P, DC, T]), ALU.mult).then_inc(keys_ready, 1)
                if e is not None:
                    wait_apart(pool, y_added, e + 2, pool_waited)
                    x = core.x[:, bass.ds(4 * e, 4), :]
                    pool.tensor_tensor(x, x, core.xn[:, bass.ds(4 * e, 4), :], ALU.add)

            sequences(pool, change, lambda b: None)

        @block.scalar
        def _(act):
            act.preload_act_table(ACT.Exp)
            act.activation(mask[:, 0, :], core.ident, ACT.Copy).then_inc(mask_ready, 1)
            act.activation(mask[:, 1, :], core.neg, ACT.Copy).then_inc(mask_ready, 1)
            act.sem_inc(odd_copied, 1)
            act.wait_ge(zeros, 1)

            def copy(b, h, k):
                act.wait_ge(turned, TB * (H * b + h) + k + 1)
                if h >= 2:
                    act.wait_ge(heads_out, H * b + h - 1)
                act.activation(prT[:, h % 2, k, k * P:T], pw[:, k % 2, k * P:T], ACT.Copy).then_inc(odd_copied, 1)

            def change(e, n):
                if e is not None:
                    act.wait_ge(heads_out, H * (e + 1))
                    act.activation(sums[:], po[:], ACT.Copy).then_inc(sums_copied, 1)
                if n is not None:
                    act.wait_ge(low_ready, n + 1)
                    act.activation(low[:], p_low, ACT.Copy).then_inc(low_copied, 1)
                if e is not None:
                    act.wait_ge(o_turned, e + 1)
                    act.activation(oT[:], po_T[:], ACT.Copy).then_inc(o_copied, 1)
                if n is not None:
                    act.wait_ge(v_ready, n + 1)
                    for p in range(2):
                        ins = act.activation(own(v[:, p], p), own(po_v, p), ACT.Copy)
                    ins.then_inc(v_copied, 1)

            def heads(b):
                for h in range(H + 1):
                    if h:
                        copy(b, h - 1, 1)
                    if h < H:
                        for k, q in enumerate(QB_ORDER):
                            n = (q + 1) * P
                            act.wait_ge(max_ready, TB * H * b + TB * h + k + 1)
                            act.activation(pr[:, h % 2, q, 0:n], pa[:, q, 0:n], ACT.Exp,
                                           bias=nmax[:, h % 2, q:q + 1],
                                           accum_out=total[:, h, q:q + 1]).then_inc(exp_ready, 1)
                    if h:
                        copy(b, h - 1, 3)

            sequences(act, change, heads)

        @block.vector
        def _(dve):
            dve.sem_inc(y_added, 1)
            dve.sem_inc(even_copied, 1)
            dve.wait_ge(w_in, 16 * len(loads))

            def rotate(b, which, o_):
                n, dst = 4 * b + 2 * which + o_, (kT, qT)[which]
                dve.wait_ge(rot_ready, n + 1)
                dve.tensor_tensor(turn[:, 0, :], pa[:, 2 * o_, :], rope[:, 0, :], ALU.mult)
                dve.tensor_tensor(turn[:, 1, :], pa[:, 2 * o_ + 1, :], rope[:, 1, :], ALU.mult).then_inc(rot_step, 1)
                dve.wait_ge(rot_step, n + 1)
                dve.tensor_tensor(dst[:, o_, :], turn[:, 0, :], turn[:, 1, :], ALU.add).then_inc(rot_done, 1)
                dve.wait_ge(rot_done, n + 1)

            def normalise_heads(b):
                dve.wait_ge(sums_turned, b + 1)
                inv = Steps(dve, norm_step, 2 * b, 2)
                inv(dve.reciprocal(total[:], total[:]))
                inv(dve.tensor_tensor(o[:].rearrange("q t (h d) -> q t h d", d=16),
                                      pw_tok.rearrange("q t (h d) -> q t h d", d=16),
                                      total[:].rearrange("q h t -> q t h").unsqueeze(3).to_broadcast([P, TB, H, 16]),
                                      ALU.mult))
                inv.close()

            def change(e, n):
                if e is not None:
                    normalise_heads(e)
                if n is not None:
                    rotate(n, 0, 0)
                    rotate(n, 0, 1)
                if e is not None:
                    xn = core.xn[:, bass.ds(4 * e, 4), :]
                    dve.wait_ge(y_ready, e + 1)
                    dve.tensor_tensor(xn, py, xn, ALU.add).then_inc(y_added, 1)
                if n is not None:
                    rotate(n, 1, 0)
                    rotate(n, 1, 1)

            def copy(b, h, k):
                dve.wait_ge(turned, TB * (H * b + h) + k + 1)
                if h >= 2:
                    dve.wait_ge(heads_out, H * b + h - 1)
                dve.tensor_copy(prT[:, h % 2, k, k * P:T], pw[:, k % 2, k * P:T]).then_inc(even_copied, 1)

            def heads(b):
                for h in range(H + 1):
                    if h:
                        copy(b, h - 1, 0)
                    if h < H:
                        for k, q in enumerate(QB_ORDER):
                            dve.wait_ge(scores_ready, TB * (H * b + h) + k + 1)
                            dve.tensor_reduce(nmax[:, h % 2, q:q + 1], pa[:, q, 0:(q + 1) * P], AX.X, ALU.max,
                                              negate=True).then_inc(max_ready, 1)
                    if h:
                        copy(b, h - 1, 2)

            sequences(dve, change, heads)


class Spec:
    pass


def layer1_spec(dram):
    s = Spec()
    s.router, s.router_bias = dram["L1_gate_wT"], dram["L1_ffn_gate_b"]
    s.gate, s.up, s.down = dram["L1_ffn_w_gate"], dram["L1_ffn_w_up"], dram["L1_ffn_w_down"]
    s.gate_bT, s.up_bT, s.down_b = dram["L1_b_gateT"], dram["L1_b_upT"], dram["L1_ffn_b_down"]
    s.routed, s.experts, s.top, s.kind, s.weigh = 32, 32, 4, "swiglu", "softmax"
    s.alpha, s.limit = 1.702, 7.0
    s.factor = 1.0 / s.alpha
    return s


def layer2_spec(dram):
    s = Spec()
    s.router, s.router_bias = dram["L2_ffn_router_w"], dram["L2_ffn_router_b"]
    s.gate, s.up, s.down, s.down_b = dram["L2_gate"], dram["L2_up"], dram["L2_down"], None
    s.routed, s.experts, s.top, s.kind, s.weigh = 7, 8, 2, "silu", "sigmoid"
    s.factor = 1.0 / 8.0
    return s


def layer3_spec(dram):
    s = Spec()
    s.router, s.router_bias = dram["L3_ffn_gate_w"], None
    s.gate, s.up, s.down, s.down_b = dram["L3_ffn_w0"], dram["L3_ffn_w1"], dram["L3_ffn_wo"], None
    s.routed, s.experts, s.top, s.kind, s.weigh = 8, 8, 2, "silu", "softmax"
    s.factor = 1.0
    return s


def route(nc, st, core, spec, aT, cw, a, first_loads, first_hi, first_lo):
    sem = st.sem
    a_hi = sem("a_hi")
    R, K = spec.routed, spec.top
    E8 = max(R, 8)
    w, bias = st.sb("w", [P, DC, R]), st.sb("bias", [P, R])
    scores = st.sb("scores", [P, TILES, E8])
    top = st.sb("top", [P, TILES, 8])
    which = st.scope.enter_context(nc.sbuf_tensor(st.name + "_which", [P, TILES, 8], mybir.dt.uint32))
    weight, hit = st.sb("weight", [P, TILES, K]), st.sb("hit", [P, TILES, R])
    total = st.sb("total", [P, TILES])
    logits = st.ps("logits", [P, TILES, 32])
    w_in, products, step, act_done = sem("w_in"), sem("products"), sem("step"), sem("act_done")
    picked, at_score = sem("picked"), sem("at_score")
    n_in = 16 * (1 + (spec.router_bias is not None))
    if spec.down_b is not None:
        db, cwT = st.sb("down_b", [R, D]), st.sb("cwT", [R, TILES, P])
        pT, pb = st.ps("cwT_p", [P, 2, 4, P]), st.ps("bias_p", [P, 2, 4, D])
        cw_turned, cwT_ready, bias_ready, bias_added = (sem(n) for n in (
            "cw_turned", "cwT_ready", "bias_ready", "bias_added"))
        n_in += 16
    with nc.Block() as block:
        @block.sync
        def _(sp):
            sp.dma_start(w[:], in_chunks(spec.router)).then_inc(w_in, 16)
            if spec.router_bias is not None:
                sp.dma_start(bias[:], on_all_partitions(spec.router_bias, P)).then_inc(w_in, 16)
            if spec.down_b is not None:
                sp.dma_start(db[:], spec.down_b).then_inc(w_in, 16)
            first_loads(sp)

        @block.tensor
        def _(pe):
            pe.wait_ge(w_in, n_in)
            for t in range(TILES):
                for c in range(DC):
                    ins = pe.matmul(logits[:, t, 0:R], col_group(aT, t // 2, t % 2)[:, c, :], w[:, c, :],
                                    start=(c == 0), stop=(c == DC - 1))
            ins.then_inc(products, 1)
            if spec.down_b is not None:
                pe.wait_ge(at_score, 1)
                for t in range(TILES):
                    if t % 4 == 0 and t >= 8:
                        pe.wait_ge(cwT_ready, t // 4 - 1)
                    ins = pe.transpose(pT[0:R, t // 4 % 2, t % 4, :], cw[:, t, 0:R], core.ident)
                    if t % 4 == 3:
                        ins.then_inc(cw_turned, 1)
                for t in range(TILES):
                    if t % 4 == 0:
                        pe.wait_ge(cwT_ready, t // 4 + 1)
                    if t % 4 == 0 and t >= 8:
                        pe.wait_ge(bias_added, t // 4 - 1)
                    ins = pe.matmul(pb[:, t // 4 % 2, t % 4, :], cwT[:, t, :], db[:], start=True, stop=True)
                    if t % 4 == 3:
                        ins.then_inc(bias_ready, 1)

        @block.gpsimd
        def _(pool):
            pool.wait_ge(a_hi, 1)
            pool.tensor_tensor(a.lo[:], aT[:], a.hi[:].bitcast(F32), ALU.subtract)
            first_lo(pool)

        @block.scalar
        def _(act):
            act.activation(a.hi[:], aT[:], ACT.Copy).then_inc(a_hi, 1)
            if spec.weigh == "sigmoid":
                act.wait_ge(step, 2)
                act.activation(scores[:, :, 0:R], scores[:, :, 0:R], ACT.Sigmoid).then_inc(act_done, 1)
            else:
                act.wait_ge(step, 2)
                act.activation(weight[:], weight[:], ACT.Exp).then_inc(act_done, 1)
            first_hi(act)

        @block.vector
        def _(dve):
            do = Steps(dve, step)
            dve.wait_ge(w_in, n_in)
            dve.wait_ge(products, 1)
            if spec.weigh == "sigmoid":
                do(dve.memset(scores[:, :, R:E8], -1.0))
            if spec.router_bias is not None:
                ins = dve.tensor_tensor(scores[:, :, 0:R], logits[:, :, 0:R],
                                        bias[:].unsqueeze(1).to_broadcast([P, TILES, R]), ALU.add)
            else:
                ins = dve.tensor_copy(scores[:, :, 0:R], logits[:, :, 0:R])
            do(ins)
            if spec.weigh == "sigmoid":
                dve.wait_ge(act_done, 1)
            for t in range(TILES):
                dve.max(top[:, t, :], scores[:, t, :]).then_inc(picked, 1)
            for t in range(TILES):
                dve.wait_ge(picked, t + 1)
                ins = dve.max_index(which[:, t, :], top[:, t, :], scores[:, t, :])
                ins.then_inc(picked, 1)
            dve.wait_ge(picked, 2 * TILES)
            if spec.weigh == "softmax":
                do(dve.tensor_tensor(weight[:], top[:, :, 0:K], top[:, :, 0:1].to_broadcast([P, TILES, K]),
                                     ALU.subtract))
                dve.wait_ge(act_done, 1)
            else:
                do(dve.tensor_copy(weight[:], top[:, :, 0:K]))
            do(dve.reduce_sum(total[:], weight[:], AX.X))
            do(dve.reciprocal(total[:], total[:]))
            do(dve.tensor_scalar(total[:], total[:], spec.factor, None, ALU.mult))
            do(dve.tensor_tensor(weight[:], weight[:], total[:].unsqueeze(2).to_broadcast([P, TILES, K]),
                                 ALU.mult))
            numbers = core.consts[:, C_COUNT:C_COUNT + R].unsqueeze(1).to_broadcast([P, TILES, R])
            if spec.experts > R:
                do(dve.memset(cw[:, :, R:spec.experts], spec.factor))
            for k in range(K):
                to = cw[:, :, 0:R] if k == 0 else hit[:]
                do(dve.tensor_tensor(to, numbers, which[:, :, k:k + 1].to_broadcast([P, TILES, R]), ALU.is_equal))
                do(dve.tensor_tensor(to, to, weight[:, :, k:k + 1].to_broadcast([P, TILES, R]), ALU.mult))
                if k:
                    do(dve.tensor_tensor(cw[:, :, 0:R], cw[:, :, 0:R], hit[:], ALU.add))
            if spec.down_b is not None:
                assert spec.factor != 1.0
                dve.sem_inc(at_score, 1)
                for k in range(TILES // 4):
                    dve.wait_ge(cw_turned, k + 1)
                    dve.tensor_scalar(cwT[:, 4 * k:4 * k + 4, :], pT[0:R, k % 2, :, :], 1.0 / spec.factor, None,
                                      ALU.mult).then_inc(cwT_ready, 1)
                for k in range(TILES // 4):
                    dve.wait_ge(bias_ready, k + 1)
                    x = core.x[:, 4 * k:4 * k + 4, :]
                    dve.tensor_tensor(x, pb[:, k % 2], x, ALU.add).then_inc(bias_added, 1)


def experts(nc, st, core, spec, aT):
    sem = st.sem
    E = spec.experts
    I = spec.gate.shape[2]
    MC = I // P
    U = 4 if MC == 1 else 2
    ROUNDS = E // U
    BLOCKS = TB
    assert TOK == BLOCKS * 512 and ROUNDS > 1 and E % U == 0
    PER = BLOCKS * MC
    STEPS = U * PER
    LAG = 3 if spec.kind == "swiglu" else 2
    RING = 4
    GI, WC = DC * I, 2 * DC * I + MC * D
    PIECE = 768
    PIECES = WC // PIECE
    assert STEPS % RING == 0 and WC % PIECE == 0 and (PIECES == 1 or 3 * PIECES + LAG <= PER)
    cw = st.sb("cw", [P, TILES, max(E, 8)])
    a = st.sb_parts("a", [P, DC, TOK])
    swiglu = spec.kind == "swiglu"
    w_raw, w = st.sb("w_raw", [P, U, WC]), st.sb_parts("w", [P, U, WC])
    raw, hidden = st.sb("raw", [P, 2, 512]), st.sb_parts("hidden", [P, RING, 512])
    silu = st.sb("silu", [P, 2, 512])
    if swiglu:
        bg, bu = st.sb("bg", [P, E]), st.sb("bu", [P, E])
        gate, up = st.sb("gate", [P, 2, 512]), st.sb("up", [P, 2, 512])
    w_in = [sem(f"w{u}_in") for u in range(U)]
    bias_in, w_hi, w_split = sem("bias_in"), sem("w_hi"), sem("w_split")

    def gate_w(t, u):
        return t[:, u, 0:GI].rearrange("p (c i) -> p c i", c=DC)

    def up_w(t, u):
        return t[:, u, GI:2 * GI].rearrange("p (c i) -> p c i", c=DC)

    def down_w(t, u):
        return t[:, u, 2 * GI:WC].rearrange("p (m d) -> p m d", m=MC)

    def load(sp, u, e):
        for view, src, pattern in ((gate_w, spec.gate, "e (c p) i -> p (e c) i"),
                                   (up_w, spec.up, "e (c p) i -> p (e c) i"),
                                   (down_w, spec.down, "e (m p) d -> p (e m) d")):
            sp.dma_start(view(w_raw, u), src[bass.ds(e, 1)].rearrange(pattern, p=P)).then_inc(w_in[u], 16)

    def first_loads(sp):
        for u in range(U):
            load(sp, u, u)
        if swiglu:
            sp.dma_start(bg[:], spec.gate_bT).then_inc(bias_in, 16)
            sp.dma_start(bu[:], spec.up_bT).then_inc(bias_in, 16)

    def first_hi(act):
        act.wait_ge(w_in[0], 48)
        for p in range(PIECES):
            cols = slice(p * PIECE, (p + 1) * PIECE)
            act.activation(w.hi[:, 0, cols], w_raw[:, 0, cols], ACT.Copy).then_inc(w_hi, 1)

    def rest_of_weights(pool, slot, p, n):
        cols = slice(p * PIECE, (p + 1) * PIECE)
        pool.wait_ge(w_hi, n)
        pool.tensor_tensor(w.lo[:, slot, cols], w_raw[:, slot, cols], w.hi[:, slot, cols].bitcast(F32),
                           ALU.subtract).then_inc(w_split, 1)

    def first_lo(pool):
        for p in range(PIECES):
            rest_of_weights(pool, 0, p, p + 1)

    with ExitStack() as scope:
        route(nc, Stage(nc, st.keep, scope, st.name + "r"), core, spec, aT, cw, a, first_loads, first_hi, first_lo)

    pg, pu = st.ps("pg", [P, 2, 512]), st.ps("pu", [P, 2, 512])
    py = st.ps("py", [P, 2, 4, D])
    g_ready, u_ready, g_taken, u_taken = (sem(n) for n in ("g_ready", "u_ready", "g_taken", "u_taken"))
    silu_ready, up_clipped = sem("silu_ready"), sem("up_clipped")
    raw_ready, hi_ready, hidden_ready = sem("raw_ready"), sem("hi_ready"), sem("hidden_ready")
    y_ready, y_taken = sem("y_ready"), sem("y_taken")
    act_waited, pool_waited = sem("act_waited"), sem("pool_waited")
    if not swiglu:
        u_taken = raw_ready

    def piece_after(k):
        u, r = k // PER, k % PER
        first = LAG if U == 2 else 0
        step = 3 if PIECES > 1 else 1
        if r >= first and (r - first) % step == 0 and (r - first) // step < PIECES:
            return (u + 1) % U, (r - first) // step
        return None

    def rounds(eng, body):
        body(0, True, False)
        if ROUNDS > 2:
            with eng.Fori(1, ROUNDS - 1) as i:
                body(i, False, False)
        body(ROUNDS - 1, False, True)

    with nc.Block() as block:
        @block.sync
        def _(sp):
            def body(i, first, last):
                for u in range(U):
                    if not last:
                        sp.wait_ge(w_split, PIECES * U * i + PIECES * (u + 1))
                        load(sp, u, (i + 1) * U + u)

            rounds(sp, body)

        @block.tensor
        def _(pe):
            pe.sem_inc(y_ready, RING)

            def up_and_gate(i, k):
                u, tb, m = k // PER, k // MC % BLOCKS, k % MC
                if k % PER == 0:
                    pe.wait_ge(w_split, PIECES * U * i + PIECES * (u + 1))
                for ps, view, taken, ready in ((pg, gate_w, g_taken, g_ready), (pu, up_w, u_taken, u_ready)):
                    pe.wait_ge(taken, i * STEPS + k + 1)
                    for c in range(DC):
                        ins = split_matmul(pe, ps[:, k % 2, :],
                                           w.view(lambda t: view(t, u)[:, c, m * P:(m + 1) * P]),
                                           a.view(lambda t: t[:, c, tb * 512:(tb + 1) * 512]),
                                           start=(c == 0), stop=(c == DC - 1))
                    ins.then_inc(ready, 1)

            def down(i, k):
                u, m = k // PER % U, k % MC
                pe.wait_ge(hidden_ready, i * STEPS + k + 3)
                if m == 0:
                    pe.wait_ge(y_taken, i * U * BLOCKS + k // MC + 1)
                for q in range(4):
                    cols = hidden.view(lambda t: t[:, k % RING, :].rearrange(
                        "h (g q p) -> h g p q", q=P, p=2)[:, q // 2, q % 2, :])
                    ins = split_matmul(pe, py[:, (k // MC) % 2, q, :], cols, w.view(lambda t: down_w(t, u)[:, m, :]),
                                       start=(m == 0 and q % 2 == 0), stop=(m == MC - 1), skip_group_check=True)
                ins.then_inc(y_ready, 1)

            def body(i, first, last):
                for k in range(STEPS):
                    up_and_gate(i, k)
                    if not (first and k < LAG):
                        down(i, k - LAG)

            rounds(pe, body)
            for k in range(STEPS - LAG, STEPS):
                down(ROUNDS - 1, k)

        @block.scalar
        def _(act):
            act.preload_act_table(ACT.Silu)
            if swiglu:
                act.wait_ge(bias_in, 32)
                act.sem_inc(u_taken, 2)
            else:
                act.sem_inc(g_taken, 2)

            def split_hidden(i, k):
                act.wait_ge(raw_ready, i * STEPS + k + 3)
                act.activation(hidden.hi[:, k % RING, :], raw[:, k % 2, :], ACT.Copy).then_inc(hi_ready, 1)

            def split_weights(i, k, first):
                u, p = piece_after(k)
                cols = slice(p * PIECE, (p + 1) * PIECE)
                act.wait_ge(w_in[u], 48 * i + 48 * (2 if u == 0 else 1))
                if not (first and u):
                    act.wait_ge(y_ready, i * STEPS + (k // PER - U + 2) * PER + RING)
                act.activation(w.hi[:, u, cols], w_raw[:, u, cols], ACT.Copy).then_inc(w_hi, 1)

            def body(i, first, last):
                for k in range(STEPS):
                    n = i * STEPS + k
                    act.wait_ge(raw_ready, n + 1)
                    if swiglu:
                        wait_apart(act, u_ready, n + 1, act_waited)
                        act.activation(up[:, k % 2, :], pu[:, k % 2, :], ACT.Identity,
                                       bias=bu[:, bass.ds(i * U + k // PER, 1)]).then_inc(u_taken, 1)
                        act.wait_ge(g_taken, n + 3)
                        act.activation(silu[:, k % 2, :], gate[:, k % 2, :], ACT.Silu,
                                       scale=spec.alpha).then_inc(silu_ready, 1)
                    else:
                        act.wait_ge(g_ready, n + 1)
                        act.activation(silu[:, k % 2, :], pg[:, k % 2, :], ACT.Silu).then_inc(g_taken, 1)
                    if not (first and k == 0):
                        split_hidden(i, k - 1)
                    if piece_after(k) and not (last and k // PER == U - 1):
                        split_weights(i, k, first)

            rounds(act, body)
            split_hidden(ROUNDS - 1, STEPS - 1)

        @block.gpsimd
        def _(pool):
            def body(i, first, last):
                for k in range(STEPS):
                    if swiglu:
                        wait_apart(pool, u_taken, i * STEPS + k + 3, pool_waited)
                        pool.tensor_scalar(up[:, k % 2, :], up[:, k % 2, :], spec.limit, -spec.limit, ALU.min,
                                           ALU.max).then_inc(up_clipped, 1)
                    if piece_after(k) and not (last and k // PER == U - 1):
                        u, p = piece_after(k)
                        rest_of_weights(pool, u, p, i * U * PIECES + (k // PER + 1) * PIECES + p + 1)

            rounds(pool, body)

        @block.vector
        def _(dve):
            dve.sem_inc(y_taken, 2)
            dve.sem_inc(raw_ready, 2)
            dve.sem_inc(hidden_ready, 2)
            if swiglu:
                dve.sem_inc(g_taken, 2)
                dve.wait_ge(bias_in, 32)

            def clamp_gate(i, k):
                n = i * STEPS + k
                dve.wait_ge(g_ready, n + 1)
                dve.wait_ge(raw_ready, n + 1)
                dve.tensor_scalar(gate[:, k % 2, :], pg[:, k % 2, :], bg[:, bass.ds(i * U + k // PER, 1)],
                                  spec.limit, ALU.add, ALU.min).then_inc(g_taken, 1)

            def hide(i, k):
                n = i * STEPS + k
                dve.wait_ge(hidden_ready, n + 1)
                if swiglu:
                    dve.wait_ge(silu_ready, n + 1)
                    dve.wait_ge(up_clipped, n + 1)
                    dve.scalar_tensor_tensor(out=raw[:, k % 2, :], in0=up[:, k % 2, :], scalar=1.0,
                                             in1=silu[:, k % 2, :], op0=ALU.add, op1=ALU.mult
                                             ).then_inc(raw_ready, 1)
                else:
                    dve.wait_ge(g_taken, n + 3)
                    dve.wait_ge(u_ready, n + 1)
                    dve.tensor_tensor(raw[:, k % 2, :], pu[:, k % 2, :], silu[:, k % 2, :],
                                      ALU.mult).then_inc(raw_ready, 1)

            def rest_of_hidden(i, k):
                dve.wait_ge(y_ready, i * STEPS + k + 1)
                dve.wait_ge(hi_ready, i * STEPS + k + 1)
                dve.tensor_tensor(hidden.lo[:, k % RING, :], raw[:, k % 2, :], hidden.hi[:, k % RING, :].bitcast(F32),
                                  ALU.subtract).then_inc(hidden_ready, 1)

            def weigh(i, nb):
                u, tb = nb // BLOCKS, nb % BLOCKS
                dve.wait_ge(y_ready, i * STEPS + MC * (nb + 1) + RING)
                for q in range(4):
                    t = 4 * tb + q
                    ins = dve.scalar_tensor_tensor(out=core.x[:, t, :], in0=py[:, nb % 2, q, :],
                                                   scalar=cw[:, t, bass.ds(i * U + u, 1)], in1=core.x[:, t, :],
                                                   op0=ALU.mult, op1=ALU.add)
                ins.then_inc(y_taken, 1)

            behind = 1 if swiglu else 0

            def body(i, first, last):
                for k in range(STEPS + (LAG + 1 if last else 0)):
                    if k < STEPS and swiglu:
                        clamp_gate(i, k)
                    if not (first and k < behind) and k - behind < STEPS:
                        hide(i, k - behind)
                    if not (first and k <= behind) and k - 1 - behind < STEPS:
                        rest_of_hidden(i, k - 1 - behind)
                    done = k - LAG - 1
                    if done % MC == MC - 1 and not (first and done < 0):
                        weigh(i, done // MC)

            rounds(dve, body)


QB_ORDER = (3, 2, 1, 0)


def layer3_attention(nc, st, core, dram, aT):
    sem = st.sem
    SCALE = D ** -0.5
    w, wo = st.sb("w", [P, DC, 3 * D]), st.sb("wo", [P, DC, D])
    here = st.sb("here", [P, DC, T])
    qT, kT, v = st.sb("qT", [P, DC, T]), st.sb("kT", [P, DC, T]), st.sb("v", [P, TB, D])
    pr, prT = st.sb("pr", [P, TB, T]), st.sb("prT", [P, TB, T])
    oT = st.sb("oT", [P, DC, T])
    nmax, total, inv = (st.sb(n, [P, TB]) for n in ("nmax", "total", "inv"))
    pa = st.ps("pa", [P, 4, T])
    pv = st.ps("pv", [P, TB, D])
    pw = st.ps("pw", [P, 2, T])
    (w_in, here_ready, qk_ready, q_copied, k_copied, v_ready, v_copied, scores_ready, score_masked, max_ready,
     exp_ready, inv_ready, prob_ready, turned, turned_copied, o_ready, o_copied, y_ready, y_added, x_residual) = (
        sem(n) for n in ("w_in here_ready qk_ready q_copied k_copied v_ready v_copied scores_ready score_masked "
                         "max_ready exp_ready inv_ready prob_ready turned turned_copied o_ready o_copied y_ready "
                         "y_added x_residual").split())
    poT = pv[:].rearrange("d (c h) n -> d c (h n)", c=DC)
    py = pw[:].rearrange("q b (k n) -> q (b k) n", n=D)
    with nc.Block() as block:
        @block.sync
        def _(sp):
            sp.dma_start(w[:], in_chunks(dram["L3_attn_qkv"])).then_inc(w_in, 16)
            sp.dma_start(wo[:], in_chunks(dram["L3_attn_o_proj"])).then_inc(w_in, 16)

        @block.gpsimd
        def _(pool):
            with pool.Fori(0, B) as b:
                pool.wait_ge(v_copied, b + 1)
                pool.tensor_copy(here[:], aT[:, :, bass.ds(b * T, T)]).then_inc(here_ready, 1)
                for k, q in enumerate(QB_ORDER):
                    n = (q + 1) * P
                    pool.wait_ge(inv_ready, TB * b + k + 1)
                    pool.tensor_tensor(pr[:, q, 0:n], pr[:, q, 0:n], inv[:, q:q + 1].to_broadcast([P, n]),
                                       ALU.mult).then_inc(prob_ready, 1)

        @block.tensor
        def _(pe):
            pe.wait_ge(w_in, 32)
            with pe.Fori(0, B) as b:
                pe.wait_ge(here_ready, b + 1)
                for o in range(4):
                    for c in range(DC):
                        ins = pe.matmul(pa[:, o, :], w[:, c, o * P:(o + 1) * P], here[:, c, :],
                                        start=(c == 0), stop=(c == DC - 1))
                ins.then_inc(qk_ready, 1)
                for t in range(TB):
                    for c in range(DC):
                        ins = pe.matmul(pv[:, t, :], here[:, c, t * P:(t + 1) * P], w[:, c, 2 * D:3 * D],
                                        start=(c == 0), stop=(c == DC - 1))
                ins.then_inc(v_ready, 1)
                pe.wait_ge(q_copied, b + 1)
                pe.wait_ge(k_copied, b + 1)
                for q in QB_ORDER:
                    n = (q + 1) * P
                    for c in range(DC):
                        ins = pe.matmul(pa[:, q, 0:n], qT[:, c, q * P:(q + 1) * P], kT[:, c, 0:n],
                                        start=(c == 0), stop=(c == DC - 1))
                    ins.then_inc(scores_ready, 1)
                pe.wait_ge(prob_ready, TB * (b + 1))
                pe.wait_ge(y_added, b + 1)
                for k in range(TB):
                    if k >= 2:
                        pe.wait_ge(turned_copied, TB * b + k - 1)
                    for q in range(k, TB):
                        ins = pe.transpose(pw[:, k % 2, q * P:(q + 1) * P], pr[:, q, k * P:(k + 1) * P], core.ident)
                    ins.then_inc(turned, 1)
                pe.wait_ge(v_copied, b + 2)
                for k in range(TB):
                    pe.wait_ge(turned_copied, TB * b + k + 1)
                    for c in range(DC):
                        ins = pe.matmul(poT[:, c, k * P:T], v[:, k, c * P:(c + 1) * P], prT[:, k, k * P:T],
                                        start=(k == 0), stop=(k == TB - 1), skip_group_check=True)
                ins.then_inc(o_ready, 1)
                pe.wait_ge(o_copied, b + 1)
                for t in range(TB):
                    for c in range(DC):
                        cols = oT[:, c, :].rearrange("d (g q p) -> d g p q", q=P, p=2)[:, t // 2, t % 2, :]
                        ins = pe.matmul(py[:, t, :], cols, wo[:, c, :], start=(c == 0), stop=(c == DC - 1))
                ins.then_inc(y_ready, 1)

        @block.scalar
        def _(act):
            act.preload_act_table(ACT.Exp)
            act.sem_inc(v_copied, 1)
            with act.Fori(0, B) as b:
                act.wait_ge(qk_ready, b + 1)
                act.activation(qT[:], pa[:, 0:2, :], ACT.Copy, scale=SCALE).then_inc(q_copied, 1)
                act.wait_ge(v_ready, b + 1)
                act.activation(v[:], pv[:], ACT.Copy).then_inc(v_copied, 1)
                for k, q in enumerate(QB_ORDER):
                    n = (q + 1) * P
                    act.wait_ge(max_ready, TB * b + k + 1)
                    act.activation(pr[:, q, 0:n], pa[:, q, 0:n], ACT.Exp, bias=nmax[:, q:q + 1],
                                   accum_out=total[:, q:q + 1]).then_inc(exp_ready, 1)
                for k in range(1, TB, 2):
                    act.wait_ge(turned, TB * b + k + 1)
                    act.wait_ge(turned_copied, TB * b + k)
                    act.activation(prT[:, k, k * P:T], pw[:, k % 2, k * P:T], ACT.Copy).then_inc(turned_copied, 1)
                act.wait_ge(o_ready, b + 1)
                act.activation(oT[:], poT, ACT.Copy).then_inc(o_copied, 1)

        @block.vector
        def _(dve):
            dve.sem_inc(y_added, 1)
            with dve.Fori(0, B) as b:
                dve.wait_ge(qk_ready, b + 1)
                dve.tensor_copy(kT[:], pa[:, 2:4, :]).then_inc(k_copied, 1)
                for k, q in enumerate(QB_ORDER):
                    n = (q + 1) * P
                    dve.wait_ge(scores_ready, TB * b + k + 1)
                    dve.tensor_tensor(pa[:, q, q * P:n], pa[:, q, q * P:n], core.neg, ALU.add).then_inc(score_masked, 1)
                    dve.wait_ge(score_masked, TB * b + k + 1)
                    dve.tensor_reduce(nmax[:, q:q + 1], pa[:, q, 0:n], AX.X, ALU.max, negate=True
                                      ).then_inc(max_ready, 1)
                for k, q in enumerate(QB_ORDER):
                    dve.wait_ge(exp_ready, TB * b + k + 1)
                    dve.reciprocal(inv[:, q:q + 1], total[:, q:q + 1]).then_inc(inv_ready, 1)
                x, xn = core.x[:, bass.ds(4 * b, 4), :], core.xn[:, bass.ds(4 * b, 4), :]
                dve.tensor_tensor(x, x, xn, ALU.add).then_inc(x_residual, 1)
                for k in range(0, TB, 2):
                    dve.wait_ge(turned, TB * b + k + 1)
                    if k:
                        dve.wait_ge(turned_copied, TB * b + k)
                    dve.tensor_copy(prT[:, k, k * P:T], pw[:, k % 2, k * P:T]).then_inc(turned_copied, 1)
                dve.wait_ge(x_residual, b + 1)
                dve.wait_ge(y_ready, b + 1)
                dve.tensor_tensor(x, py, x, ALU.add).then_inc(y_added, 1)


LAYERS = (0, 1, 2, 3)


def build(nc, dram, out):
    with ExitStack() as keep:
        core, used = Core(), []

        def resident(name, shape):
            return keep.enter_context(nc.sbuf_tensor(name, shape, F32))

        core.x, core.xn = resident("x", [P, TILES, D]), resident("xn", [P, TILES, D])
        core.consts = resident("consts", [P, C_END])
        core.ab_sum, core.bcT = resident("ab_sum", [P, DC]), resident("bcT", [P, DC, B])
        core.ident = core.consts[:, C_ID:C_ID + P]
        core.tri = core.consts[:, C_TRI:C_TRI + P]
        core.neg = core.consts[:, C_NEG:C_NEG + P]
        core.blk = core.consts[:, C_BLK:C_BLK + P]

        def run(name, f, *args, **kw):
            with ExitStack() as scope:
                f(nc, Stage(nc, used, scope, name), core, *args, **kw)

        def channel_major(scope, layer):
            return scope.enter_context(nc.sbuf_tensor(f"{layer}_xnT", [P, DC, TOK], F32))

        run("s", setup, dram)
        if 0 in LAYERS:
            with ExitStack() as scope:
                st = Stage(nc, used, scope, "l0")
                core.xnT = channel_major(scope, "l0")
                run("n0", normalise, core.x, core.xn, core.xnT, 1e-5)
                gsT, gateT, last_rows = st.sb("gsT", [P, DC, TOK]), st.sb("gateT", [P, DC, TOK]), st.sb("last", [B, D])
                run("m0", layer0_mix, dram, gsT, gateT, last_rows)
                run("j0", layer0_join, dram, gsT, gateT)
        if 1 in LAYERS:
            with ExitStack() as scope:
                core.xnT = channel_major(scope, "l1")
                run("n1", normalise, core.x, core.xn, core.xnT, 1e-5)
                run("a1", layer1_attention)
                run("f1", experts, layer1_spec(dram), core.xnT)
        if 2 in LAYERS:
            release(nc, used)
            with ExitStack() as scope:
                a = Stage(nc, used, scope, "l2").sb_parts("xnT", [P, DC, TOK])
                with ExitStack() as inner:
                    xnT = channel_major(inner, "l2")
                    run("n2", normalise, core.x, core.xn, xnT, 1e-5)
                    split(nc, Stage(nc, used, inner, "s2"), xnT, a)
                run("a2", layer2_abc, dram, a)
            with ExitStack() as scope:
                st = Stage(nc, used, scope, "l2")
                aT = st.sb("aT", [P, DC, TOK])
                run("r2", normalise, core.xn, None, aT, 1e-5, rms=True, gain=dram["L2_ffn_ln1_w"])
                run("b2", layer2_attention, dram, aT)
                run("q2", normalise, core.xn, None, aT, 1e-5, rms=True, gain=dram["L2_ffn_ln2_w"])
                run("f2", experts, layer2_spec(dram), aT)
        if 3 in LAYERS:
            release(nc, used)
            with ExitStack() as scope:
                xnT = channel_major(scope, "l3")
                run("n3", normalise, core.x, core.xn, xnT, 1e-5)
                with ExitStack() as inner:
                    aT = Stage(nc, used, inner, "l3").sb("aT", [P, DC, TOK])
                    run("r3", normalise, core.xn, None, aT, 1e-5, gain=dram["L3_attn_gamma"],
                        shift=dram["L3_attn_beta"])
                    run("a3", layer3_attention, dram, aT)
                run("f3", experts, layer3_spec(dram), xnT)

        stored = nc.alloc_semaphore(name="stored")
        with nc.Block() as block:
            @block.sync
            def _(sp):
                for p in range(2):
                    sp.dma_start(token_rows(out, p), core.x[:, p::2, :]).then_inc(stored, 16)
                sp.wait_ge(stored, 32)


def constants():
    c = np.zeros((P, C_END), np.float32)
    i = np.arange(P)
    c[:, C_ID:C_ID + P] = np.eye(P)
    c[:, C_TRI:C_TRI + P] = i[None, :] >= i[:, None]
    c[:, C_NEG:C_NEG + P] = np.where(i[None, :] > i[:, None], NEG, 0.0)
    c[:, C_BLK:C_BLK + P] = i[None, :] // 32 == i[:, None] // 32
    for p in range(2):
        c[:, C_EVEN + p] = (i // 16) % 2 == p
        c[:, C_KEYS + p] = 0.25 * c[:, C_EVEN + p]
    c[:, C_HALF:C_HALF + TILES] = -0.5
    c[:, C_ONE] = 1.0
    c[:, C_COUNT:C_COUNT + 32] = np.arange(32)
    half = 4
    inv = 1.0 / 10000.0 ** (np.arange(0, 8, 2, dtype=np.float32) / np.float32(8))
    angle = np.arange(T, dtype=np.float32)[None, :] * inv.astype(np.float32)[:, None]
    cos, sin = np.ones((P, T), np.float32), np.zeros((P, T), np.float32)
    for q in range(P):
        r = q % 16 - 8
        if r >= 0:
            cos[q] = np.cos(angle[r % half])
            sin[q] = np.sin(angle[r % half]) * (-1.0 if r < half else 1.0)
    return c, np.stack([cos, sin])


def lay_out(inputs):
    a = {n: np.ascontiguousarray(v) for n, v in inputs.items() if not n.startswith("L3_ffn_decoder")}
    a["consts"], a["rope"] = constants()
    a["C_wT"] = np.ascontiguousarray(a.pop("L0_attn_C_w").T)
    a["D_wT"] = np.ascontiguousarray(a.pop("L0_attn_D_w").T)
    a["L1_gate_wT"] = np.ascontiguousarray(a.pop("L1_ffn_gate_w").T)
    for n in ("b_gate", "b_up"):
        a["L1_%sT" % n] = np.ascontiguousarray(a.pop("L1_ffn_" + n).T)
    for n in ("gate", "up", "down"):
        a["L2_" + n] = np.concatenate([a.pop("L2_ffn_r_" + n), a.pop("L2_ffn_sh_" + n)[None]])
    nh, rd = 16, 8

    def slots(w, first):
        w = w.reshape(w.shape[0], nh, rd)
        z = np.zeros_like(w)
        return np.concatenate([w, z] if first else [z, w], axis=2).reshape(w.shape[0], -1)

    def turned(w):
        w = w.reshape(w.shape[0], nh, 2, rd // 2)[:, :, ::-1]
        return np.ascontiguousarray(w).reshape(w.shape[0], -1)

    for q in "kq":
        up, rope = a.pop("L2_ffn_%s_u_w" % q), a.pop("L2_ffn_rope_%s_w" % q)
        a["L2_%s_turned" % q] = slots(turned(rope), False)
        if q == "k":
            a["L2_k_plain"], a["L2_k_rope"] = slots(up, True), slots(rope, False)
        else:
            both = [w.reshape(w.shape[0], nh, rd) for w in (up, rope)]
            a["L2_q_both"] = np.concatenate(both, axis=2).reshape(up.shape[0], -1)
    a["L2_kvq_d"] = np.concatenate([a.pop("L2_ffn_kv_d_w"), a.pop("L2_ffn_q_d_w")], axis=1)
    return a


def kernel(**inputs):
    import concourse.bacc as bacc
    from concourse.bass_utils import run_bass_kernel_spmd

    nc = bacc.Bacc("TRN2", target_bir_lowering=False, num_devices=1)
    arrays = lay_out(inputs)
    dram = {n: nc.dram_tensor(n + "_dram", a.shape, mybir.dt.from_np(a.dtype), kind="ExternalInput").ap()
            for n, a in arrays.items()}
    out = nc.dram_tensor("out_dram", (B, T, D), F32, kind="ExternalOutput").ap()
    build(nc, dram, out)
    r = run_bass_kernel_spmd(nc, [{n + "_dram": a for n, a in arrays.items()}], core_ids=[0])
    return r.results[0]["out_dram"]
```
